# Optimizing a Trainium2 kernel written in Bass

```python
import numpy as np
import jax
import jax.numpy as jnp

def _softmax(x, axis=-1):
    return jax.nn.softmax(x, axis=axis)

def _gelu(x):
    return jax.nn.gelu(x, approximate=True)

def _silu(x):
    return jax.nn.silu(x)

def _sigmoid(x):
    return jax.nn.sigmoid(x)

def _layernorm(x, axis=-1, eps=1e-05):
    m = jnp.mean(x, axis=axis, keepdims=True)
    v = jnp.var(x, axis=axis, keepdims=True)
    return (x - m) / jnp.sqrt(v + eps)

def _scatter_add(tgt, idx, src, axis=0):
    return tgt.at[idx].add(src)

def _segment_sum(src, seg, n):
    return jax.ops.segment_sum(src, seg, n)
kernel_name = 'mk_seq_preln_d4_jaxref_r8_a89838'

def setup_inputs(seed: int=0):
    np.random.seed(seed)
    _w = jnp.asarray

    def _L0_attn_setup():
        import jax, jax.numpy as jnp
        import numpy as np
        N_EMBD = 128
        N_HEAD = 16
        HORIZON = 64
        HS = N_EMBD // N_HEAD
        BD = max(HS // 4, 16)

        def _windows(t, delta):
            B, nh, T, D = t.shape
            padded = jnp.pad(t, ((0, 0), (0, 0), (delta - 1, 0), (0, 0)))
            idx = jnp.arange(T)[:, None] + jnp.arange(delta)[None, :]
            return padded[:, :, idx]
        key = jax.random.key(seed)
        ks = jax.random.split(key, 12)
        s = 0.02
        B, T = (2, 128)
        return {'x': jax.random.normal(ks[0], (B, T, N_EMBD), jnp.float32), 'W_disp': jax.random.normal(ks[1], (N_EMBD, N_HEAD * BD), jnp.float32) * s, 'W_val': jax.random.normal(ks[2], (N_EMBD, N_EMBD), jnp.float32) * s, 'rel_pos_emb': jax.random.normal(ks[3], (HORIZON, BD), jnp.float32) * s, 'W_strain': jax.random.normal(ks[4], (BD, BD), jnp.float32) * s, 'W_pos': jax.random.normal(ks[5], (BD, BD), jnp.float32) * s, 'W_bond': jax.random.normal(ks[6], (BD, 1), jnp.float32) * s, 'W_dmg': jax.random.normal(ks[7], (BD, BD), jnp.float32) * s, 'b_dmg': jnp.zeros((BD,), jnp.float32), 'W_dmg_out': jax.random.normal(ks[8], (BD, 1), jnp.float32) * s, 'b_dmg_out': jnp.full((1,), -3.0, jnp.float32), 'W_cproj': jax.random.normal(ks[9], (N_EMBD, N_EMBD), jnp.float32) * s}
    _L0_attn_in = _L0_attn_setup()

    def _L0_ffn_setup():
        import jax, jax.numpy as jnp
        import numpy as np
        D_MODEL, D_FF, D2, DL = (128, 512, 64, 64)
        D1 = D_FF // D2
        BATCH, SEQ = (2, 128)
        KERNEL_SCALE = D2 ** 0.5
        key = jax.random.key(seed)
        ks = jax.random.split(key, 7)
        xav = lambda k, shape, fan: jax.random.normal(k, shape, jnp.float32) * (2.0 / sum(fan)) ** 0.5
        x = jax.random.normal(ks[0], (BATCH, SEQ, D_MODEL), jnp.float32)
        m1 = xav(ks[1], (D_MODEL, DL), (D_MODEL, DL))
        m2 = xav(ks[2], (DL, D1, D2), (DL, D_FF))
        mb = jax.random.normal(ks[3], (D1, D2), jnp.float32)
        w1 = xav(ks[4], (D_MODEL, D1, D2), (D_MODEL, D_FF))
        w2 = xav(ks[5], (D2, D1, D_MODEL), (D_FF, D_MODEL)) * KERNEL_SCALE
        b2 = jax.random.normal(ks[6], (D_MODEL,), jnp.float32)
        return {'x': x, 'm1': m1, 'm2': m2, 'mb': mb, 'w1': w1, 'w2': w2, 'b2': b2}
    _L0_ffn_in = _L0_ffn_setup()

    def _L1_attn_setup():
        import jax, jax.numpy as jnp
        import numpy as np
        D_MODEL = 128
        D_INNER = 2 * D_MODEL
        D_STATE = 16
        D_CONV = 4
        DT_RANK = (D_MODEL + 15) // 16
        B, L = (1, 256)

        def _causal_depthwise_conv(x, w, b):
            xp = jnp.pad(x, ((0, 0), (D_CONV - 1, 0), (0, 0)))
            y = b[None, None, :]
            for k in range(D_CONV):
                y = y + xp[:, k:k + x.shape[1], :] * w[None, None, :, k]
            return y

        def _selective_scan(x, dt, Bm, Cm, A, D):
            dA = jnp.exp(dt[..., None] * A)
            dBx = (dt * x)[..., None] * Bm[:, :, None, :]

            def step(h, inputs):
                dA_t, dBx_t, C_t = inputs
                h = dA_t * h + dBx_t
                y = jnp.einsum('bdn,bn->bd', h, C_t)
                return (h, y)
            h0 = jnp.zeros((x.shape[0], x.shape[2], A.shape[1]), x.dtype)
            xs = (jnp.swapaxes(dA, 0, 1), jnp.swapaxes(dBx, 0, 1), jnp.swapaxes(Cm, 0, 1))
            _, ys = jax.lax.scan(step, h0, xs)
            return jnp.swapaxes(ys, 0, 1) + x * D[None, None, :]

        def _mamba_dir(h, in_proj_w, conv_w, conv_b, x_proj_w, dt_proj_w, dt_proj_b, A_log, D, out_proj_w):
            xz = h @ in_proj_w.T
            x, z = (xz[..., :D_INNER], xz[..., D_INNER:])
            x = jax.nn.silu(_causal_depthwise_conv(x, conv_w, conv_b))
            x_dbl = x @ x_proj_w.T
            dt = jax.nn.softplus(x_dbl[..., :DT_RANK] @ dt_proj_w.T + dt_proj_b)
            Bm = x_dbl[..., DT_RANK:DT_RANK + D_STATE]
            Cm = x_dbl[..., DT_RANK + D_STATE:]
            A = -jnp.exp(A_log)
            y = _selective_scan(x, dt, Bm, Cm, A, D)
            y = y * jax.nn.silu(z)
            return y @ out_proj_w.T
        key = jax.random.key(seed)
        ks = jax.random.split(key, 16)
        s = 0.02
        inp = {}
        inp['hidden_states'] = jax.random.normal(ks[0], (B, L, D_MODEL), jnp.float32)
        inp['in_proj_w'] = jax.random.normal(ks[1], (2 * D_INNER, D_MODEL), jnp.float32) * s
        inp['out_proj_w'] = jax.random.normal(ks[2], (D_MODEL, D_INNER), jnp.float32) * s
        for tag, off in (('f', 3), ('r', 9)):
            inp[f'conv_w_{tag}'] = jax.random.normal(ks[off + 0], (D_INNER, D_CONV), jnp.float32) * 0.3
            inp[f'conv_b_{tag}'] = jax.random.normal(ks[off + 1], (D_INNER,), jnp.float32) * 0.02
            inp[f'x_proj_w_{tag}'] = jax.random.normal(ks[off + 2], (DT_RANK + 2 * D_STATE, D_INNER), jnp.float32) * s
            inp[f'dt_proj_w_{tag}'] = jax.random.normal(ks[off + 3], (D_INNER, DT_RANK), jnp.float32) * DT_RANK ** (-0.5)
            inp[f'dt_proj_b_{tag}'] = jnp.log(jnp.expm1(jnp.full((D_INNER,), 0.01, jnp.float32)))
            inp[f'A_log_{tag}'] = jnp.log(jnp.broadcast_to(jnp.arange(1, D_STATE + 1, dtype=jnp.float32), (D_INNER, D_STATE)))
            inp[f'D_{tag}'] = jnp.ones((D_INNER,), jnp.float32)
        return inp
    _L1_attn_in = _L1_attn_setup()

    def _L1_ffn_setup():
        import jax, jax.numpy as jnp
        import numpy as np
        B, S, D, E = (4, 512, 128, 8)
        key = jax.random.key(seed)
        k1, k2, k3, k4, k5 = jax.random.split(key, 5)
        scale = 1.0 / np.sqrt(D)
        return {'x': jax.random.normal(k1, (B, S, D), dtype=jnp.float32), 'Wg': jax.random.normal(k2, (D, D), dtype=jnp.float32) * scale, 'bg': jnp.zeros((D,), dtype=jnp.float32), 'We': jax.random.normal(k3, (E, D, D), dtype=jnp.float32) * scale, 'be': jnp.zeros((E, D), dtype=jnp.float32)}
    _L1_ffn_in = _L1_ffn_setup()

    def _L2_attn_setup():
        import jax, jax.numpy as jnp
        import numpy as np
        import math
        B, S, D, H, R, DFF = (4, 128, 128, 16, 64, 512)

        def _layernorm(x, g, b, eps=1e-05):
            m = jnp.mean(x, axis=-1, keepdims=True)
            v = jnp.var(x, axis=-1, keepdims=True)
            return (x - m) / jnp.sqrt(v + eps) * g + b
        key = jax.random.key(seed)
        ks = jax.random.split(key, 12)
        sc = 0.02
        return {'src': jax.random.normal(ks[0], (B, S, D), jnp.float32), 'in_proj_w': jax.random.normal(ks[1], (3 * D, D), jnp.float32) * sc, 'in_proj_b': jnp.zeros((3 * D,), jnp.float32), 'out_proj_w': jax.random.normal(ks[2], (D, D), jnp.float32) * sc, 'out_proj_b': jnp.zeros((D,), jnp.float32), 'Qp_w': jax.random.normal(ks[3], (R, D), jnp.float32) * sc, 'Qp_b': jnp.zeros((R,), jnp.float32), 'Kp_w': jax.random.normal(ks[4], (R, D), jnp.float32) * sc, 'Kp_b': jnp.zeros((R,), jnp.float32), 'Vp_w': jax.random.normal(ks[5], (D, D), jnp.float32) * sc, 'Vp_b': jnp.zeros((D,), jnp.float32), 'lam': jnp.float32(0.5), 'ff1_w': jax.random.normal(ks[6], (DFF, D), jnp.float32) * sc, 'ff1_b': jnp.zeros((DFF,), jnp.float32), 'ff2_w': jax.random.normal(ks[7], (D, DFF), jnp.float32) * sc, 'ff2_b': jnp.zeros((D,), jnp.float32), 'ln1_g': jnp.ones((D,), jnp.float32), 'ln1_b': jnp.zeros((D,), jnp.float32), 'ln2_g': jnp.ones((D,), jnp.float32), 'ln2_b': jnp.zeros((D,), jnp.float32)}
    _L2_attn_in = _L2_attn_setup()

    def _L2_ffn_setup():
        import jax, jax.numpy as jnp
        import numpy as np
        D_IN, D_HID = (128, 512)

        def _ternary(key, shape):
            return jax.random.randint(key, shape, -1, 2).astype(jnp.float32)

        def _tlin(x, w, s):
            return jnp.einsum('bsi,oi->bso', x, w) * s
        key = jax.random.key(seed)
        ks = jax.random.split(key, 12)
        inv = lambda fan: 1.0 / np.sqrt(fan).astype(np.float32)
        return {'x': jax.random.normal(ks[0], (4, 256, D_IN), dtype=jnp.float32), 'w1_w': _ternary(ks[1], (D_HID, D_IN)), 'w1_s': jax.random.uniform(ks[2], (D_HID,), dtype=jnp.float32) * inv(D_IN), 'w2_w': _ternary(ks[3], (D_HID, D_IN)), 'w2_s': jax.random.uniform(ks[4], (D_HID,), dtype=jnp.float32) * inv(D_IN), 'h1_w': _ternary(ks[5], (D_HID, D_HID)), 'h1_s': jax.random.uniform(ks[6], (D_HID,), dtype=jnp.float32) * inv(D_HID), 'h2_w': _ternary(ks[7], (D_HID, D_HID)), 'h2_s': jax.random.uniform(ks[8], (D_HID,), dtype=jnp.float32) * inv(D_HID), 'w3_w': _ternary(ks[9], (D_IN, D_HID)), 'w3_s': jax.random.uniform(ks[10], (D_IN,), dtype=jnp.float32) * inv(D_HID)}
    _L2_ffn_in = _L2_ffn_setup()

    def _L3_attn_setup():
        import jax, jax.numpy as jnp
        import numpy as np
        HIDDEN = 128
        HEADS = 16
        BATCH = 2
        SEQ = 256
        key = jax.random.key(seed)
        k1, k2, k3 = jax.random.split(key, 3)
        x = jax.random.normal(k1, (BATCH, SEQ, HIDDEN), dtype=jnp.float32)
        w_qkv = jax.random.normal(k2, (3 * HIDDEN, HIDDEN), dtype=jnp.float32)
        w_o = jax.random.normal(k3, (HIDDEN, HIDDEN), dtype=jnp.float32)
        return {'x': x, 'w_qkv': w_qkv, 'w_o': w_o}
    _L3_attn_in = _L3_attn_setup()

    def _L3_ffn_setup():
        import jax, jax.numpy as jnp
        import numpy as np
        DIM = 128
        HIDDEN = 384
        SCALE = 1.0 / 127.0

        def _dequant(w_int, dtype):
            return w_int.astype(dtype) * jnp.asarray(SCALE, dtype)
        key = jax.random.key(seed)
        k_x, k_g, k_u, k_d = jax.random.split(key, 4)
        x = jax.random.normal(k_x, (4, 256, DIM), dtype=jnp.float32)
        w_gate = jax.random.randint(k_g, (HIDDEN, DIM), -127, 128, dtype=jnp.int32)
        w_up = jax.random.randint(k_u, (HIDDEN, DIM), -127, 128, dtype=jnp.int32)
        w_down = jax.random.randint(k_d, (DIM, HIDDEN), -127, 128, dtype=jnp.int32)
        return {'x': x, 'w_gate': w_gate, 'w_up': w_up, 'w_down': w_down}
    _L3_ffn_in = _L3_ffn_setup()
    _d = {'L0_attn_x': _L0_attn_in['x'], 'L0_attn_W_disp': _L0_attn_in['W_disp'], 'L0_attn_W_val': _L0_attn_in['W_val'], 'L0_attn_rel_pos_emb': _L0_attn_in['rel_pos_emb'], 'L0_attn_W_strain': _L0_attn_in['W_strain'], 'L0_attn_W_pos': _L0_attn_in['W_pos'], 'L0_attn_W_bond': _L0_attn_in['W_bond'], 'L0_attn_W_dmg': _L0_attn_in['W_dmg'], 'L0_attn_b_dmg': _L0_attn_in['b_dmg'], 'L0_attn_W_dmg_out': _L0_attn_in['W_dmg_out'], 'L0_attn_b_dmg_out': _L0_attn_in['b_dmg_out'], 'L0_attn_W_cproj': _L0_attn_in['W_cproj'], 'L0_ffn_m1': _L0_ffn_in['m1'], 'L0_ffn_m2': _L0_ffn_in['m2'], 'L0_ffn_mb': _L0_ffn_in['mb'], 'L0_ffn_w1': _L0_ffn_in['w1'], 'L0_ffn_w2': _L0_ffn_in['w2'], 'L0_ffn_b2': _L0_ffn_in['b2'], 'L1_attn_in_proj_w': _L1_attn_in['in_proj_w'], 'L1_attn_out_proj_w': _L1_attn_in['out_proj_w'], 'L1_attn_conv_w_f': _L1_attn_in['conv_w_f'], 'L1_attn_conv_b_f': _L1_attn_in['conv_b_f'], 'L1_attn_x_proj_w_f': _L1_attn_in['x_proj_w_f'], 'L1_attn_dt_proj_w_f': _L1_attn_in['dt_proj_w_f'], 'L1_attn_dt_proj_b_f': _L1_attn_in['dt_proj_b_f'], 'L1_attn_A_log_f': _L1_attn_in['A_log_f'], 'L1_attn_D_f': _L1_attn_in['D_f'], 'L1_attn_conv_w_r': _L1_attn_in['conv_w_r'], 'L1_attn_conv_b_r': _L1_attn_in['conv_b_r'], 'L1_attn_x_proj_w_r': _L1_attn_in['x_proj_w_r'], 'L1_attn_dt_proj_w_r': _L1_attn_in['dt_proj_w_r'], 'L1_attn_dt_proj_b_r': _L1_attn_in['dt_proj_b_r'], 'L1_attn_A_log_r': _L1_attn_in['A_log_r'], 'L1_attn_D_r': _L1_attn_in['D_r'], 'L1_ffn_Wg': _L1_ffn_in['Wg'], 'L1_ffn_bg': _L1_ffn_in['bg'], 'L1_ffn_We': _L1_ffn_in['We'], 'L1_ffn_be': _L1_ffn_in['be'], 'L2_attn_in_proj_w': _L2_attn_in['in_proj_w'], 'L2_attn_in_proj_b': _L2_attn_in['in_proj_b'], 'L2_attn_out_proj_w': _L2_attn_in['out_proj_w'], 'L2_attn_out_proj_b': _L2_attn_in['out_proj_b'], 'L2_attn_Qp_w': _L2_attn_in['Qp_w'], 'L2_attn_Qp_b': _L2_attn_in['Qp_b'], 'L2_attn_Kp_w': _L2_attn_in['Kp_w'], 'L2_attn_Kp_b': _L2_attn_in['Kp_b'], 'L2_attn_Vp_w': _L2_attn_in['Vp_w'], 'L2_attn_Vp_b': _L2_attn_in['Vp_b'], 'L2_attn_lam': _L2_attn_in['lam'], 'L2_attn_ff1_w': _L2_attn_in['ff1_w'], 'L2_attn_ff1_b': _L2_attn_in['ff1_b'], 'L2_attn_ff2_w': _L2_attn_in['ff2_w'], 'L2_attn_ff2_b': _L2_attn_in['ff2_b'], 'L2_attn_ln1_g': _L2_attn_in['ln1_g'], 'L2_attn_ln1_b': _L2_attn_in['ln1_b'], 'L2_attn_ln2_g': _L2_attn_in['ln2_g'], 'L2_attn_ln2_b': _L2_attn_in['ln2_b'], 'L2_ffn_w1_w': _L2_ffn_in['w1_w'], 'L2_ffn_w1_s': _L2_ffn_in['w1_s'], 'L2_ffn_w2_w': _L2_ffn_in['w2_w'], 'L2_ffn_w2_s': _L2_ffn_in['w2_s'], 'L2_ffn_h1_w': _L2_ffn_in['h1_w'], 'L2_ffn_h1_s': _L2_ffn_in['h1_s'], 'L2_ffn_h2_w': _L2_ffn_in['h2_w'], 'L2_ffn_h2_s': _L2_ffn_in['h2_s'], 'L2_ffn_w3_w': _L2_ffn_in['w3_w'], 'L2_ffn_w3_s': _L2_ffn_in['w3_s'], 'L3_attn_w_qkv': _L3_attn_in['w_qkv'], 'L3_attn_w_o': _L3_attn_in['w_o'], 'L3_ffn_w_gate': _L3_ffn_in['w_gate'], 'L3_ffn_w_up': _L3_ffn_in['w_up'], 'L3_ffn_w_down': _L3_ffn_in['w_down']}
    _x0 = _d['L0_attn_x']
    _d['L0_attn_x'] = jax.random.normal(jax.random.fold_in(jax.random.key(seed), 1), (1, 2048, 128), dtype=_x0.dtype)
    del _x0
    return _d

def reference(L0_attn_x, L0_attn_W_disp, L0_attn_W_val, L0_attn_rel_pos_emb, L0_attn_W_strain, L0_attn_W_pos, L0_attn_W_bond, L0_attn_W_dmg, L0_attn_b_dmg, L0_attn_W_dmg_out, L0_attn_b_dmg_out, L0_attn_W_cproj, L0_ffn_m1, L0_ffn_m2, L0_ffn_mb, L0_ffn_w1, L0_ffn_w2, L0_ffn_b2, L1_attn_in_proj_w, L1_attn_out_proj_w, L1_attn_conv_w_f, L1_attn_conv_b_f, L1_attn_x_proj_w_f, L1_attn_dt_proj_w_f, L1_attn_dt_proj_b_f, L1_attn_A_log_f, L1_attn_D_f, L1_attn_conv_w_r, L1_attn_conv_b_r, L1_attn_x_proj_w_r, L1_attn_dt_proj_w_r, L1_attn_dt_proj_b_r, L1_attn_A_log_r, L1_attn_D_r, L1_ffn_Wg, L1_ffn_bg, L1_ffn_We, L1_ffn_be, L2_attn_in_proj_w, L2_attn_in_proj_b, L2_attn_out_proj_w, L2_attn_out_proj_b, L2_attn_Qp_w, L2_attn_Qp_b, L2_attn_Kp_w, L2_attn_Kp_b, L2_attn_Vp_w, L2_attn_Vp_b, L2_attn_lam, L2_attn_ff1_w, L2_attn_ff1_b, L2_attn_ff2_w, L2_attn_ff2_b, L2_attn_ln1_g, L2_attn_ln1_b, L2_attn_ln2_g, L2_attn_ln2_b, L2_ffn_w1_w, L2_ffn_w1_s, L2_ffn_w2_w, L2_ffn_w2_s, L2_ffn_h1_w, L2_ffn_h1_s, L2_ffn_h2_w, L2_ffn_h2_s, L2_ffn_w3_w, L2_ffn_w3_s, L3_attn_w_qkv, L3_attn_w_o, L3_ffn_w_gate, L3_ffn_w_up, L3_ffn_w_down):

    def _L0_attn_ref(x, W_disp, W_val, rel_pos_emb, W_strain, W_pos, W_bond, W_dmg, b_dmg, W_dmg_out, b_dmg_out, W_cproj):
        import jax, jax.numpy as jnp
        import numpy as np
        N_EMBD = 128
        N_HEAD = 16
        HORIZON = 64
        HS = N_EMBD // N_HEAD
        BD = max(HS // 4, 16)

        def _windows(t, delta):
            B, nh, T, D = t.shape
            padded = jnp.pad(t, ((0, 0), (0, 0), (delta - 1, 0), (0, 0)))
            idx = jnp.arange(T)[:, None] + jnp.arange(delta)[None, :]
            return padded[:, :, idx]
        B, T, C = x.shape
        nh, bd, hs = (N_HEAD, BD, HS)
        delta = min(HORIZON, T)
        disp = (x @ W_disp).reshape(B, T, nh, bd).transpose(0, 2, 1, 3)
        val = (x @ W_val).reshape(B, T, nh, hs).transpose(0, 2, 1, 3)
        disp_win = _windows(disp, delta)
        val_win = _windows(val, delta)
        cmask = jnp.arange(T)[:, None] - delta + 1 + jnp.arange(delta)[None, :] >= 0
        strain = disp_win - disp[:, :, :, None, :]
        rel_emb = rel_pos_emb[:delta]
        bond_act = jax.nn.gelu(strain @ W_strain + rel_emb @ W_pos, approximate=False)
        bond_logits = (bond_act @ W_bond)[..., 0]
        damage_act = jax.nn.gelu(strain @ W_dmg + b_dmg, approximate=False)
        damage = jax.nn.sigmoid((damage_act @ W_dmg_out)[..., 0] + b_dmg_out[0])
        logits = bond_logits - 10.0 * damage
        logits = jnp.where(cmask[None, None], logits, -jnp.inf)
        weights = jax.nn.softmax(logits, axis=-1)
        out = jnp.einsum('bntd,bntde->bnte', weights, val_win)
        out = out.transpose(0, 2, 1, 3).reshape(B, T, C)
        return out @ W_cproj

    def _L0_ffn_ref(x, m1, m2, mb, w1, w2, b2):
        import jax, jax.numpy as jnp
        import numpy as np
        D_MODEL, D_FF, D2, DL = (128, 512, 64, 64)
        D1 = D_FF // D2
        BATCH, SEQ = (2, 128)
        KERNEL_SCALE = D2 ** 0.5
        x_shape = x.shape
        xf = x.reshape(-1, x_shape[-1])
        d1 = w1.shape[1]
        lr = xf @ m1
        mask_logits = jnp.einsum('bl,lxy->bxy', lr, m2) + mb
        quant_mask = jnp.argmax(mask_logits, axis=-1)
        w1p = jnp.transpose(w1, (1, 2, 0))
        w2p = jnp.transpose(w2, (1, 0, 2))
        j = jnp.arange(d1)[None, :]
        w = w1p[j, quant_mask]
        mid = jnp.einsum('ai,aji->aj', xf, w)
        relu = jax.nn.relu(mid)
        v = w2p[j, quant_mask]
        res = jnp.einsum('ai,aij->aj', relu, v) + b2
        return res.reshape(x_shape)

    def _L1_attn_ref(hidden_states, in_proj_w, out_proj_w, conv_w_f, conv_b_f, x_proj_w_f, dt_proj_w_f, dt_proj_b_f, A_log_f, D_f, conv_w_r, conv_b_r, x_proj_w_r, dt_proj_w_r, dt_proj_b_r, A_log_r, D_r):
        import jax, jax.numpy as jnp
        import numpy as np
        D_MODEL = 128
        D_INNER = 2 * D_MODEL
        D_STATE = 16
        D_CONV = 4
        DT_RANK = (D_MODEL + 15) // 16
        B, L = (1, 256)

        def _causal_depthwise_conv(x, w, b):
            xp = jnp.pad(x, ((0, 0), (D_CONV - 1, 0), (0, 0)))
            y = b[None, None, :]
            for k in range(D_CONV):
                y = y + xp[:, k:k + x.shape[1], :] * w[None, None, :, k]
            return y

        def _selective_scan(x, dt, Bm, Cm, A, D):
            dA = jnp.exp(dt[..., None] * A)
            dBx = (dt * x)[..., None] * Bm[:, :, None, :]

            def step(h, inputs):
                dA_t, dBx_t, C_t = inputs
                h = dA_t * h + dBx_t
                y = jnp.einsum('bdn,bn->bd', h, C_t)
                return (h, y)
            h0 = jnp.zeros((x.shape[0], x.shape[2], A.shape[1]), x.dtype)
            xs = (jnp.swapaxes(dA, 0, 1), jnp.swapaxes(dBx, 0, 1), jnp.swapaxes(Cm, 0, 1))
            _, ys = jax.lax.scan(step, h0, xs)
            return jnp.swapaxes(ys, 0, 1) + x * D[None, None, :]

        def _mamba_dir(h, in_proj_w, conv_w, conv_b, x_proj_w, dt_proj_w, dt_proj_b, A_log, D, out_proj_w):
            xz = h @ in_proj_w.T
            x, z = (xz[..., :D_INNER], xz[..., D_INNER:])
            x = jax.nn.silu(_causal_depthwise_conv(x, conv_w, conv_b))
            x_dbl = x @ x_proj_w.T
            dt = jax.nn.softplus(x_dbl[..., :DT_RANK] @ dt_proj_w.T + dt_proj_b)
            Bm = x_dbl[..., DT_RANK:DT_RANK + D_STATE]
            Cm = x_dbl[..., DT_RANK + D_STATE:]
            A = -jnp.exp(A_log)
            y = _selective_scan(x, dt, Bm, Cm, A, D)
            y = y * jax.nn.silu(z)
            return y @ out_proj_w.T
        out_fwd = _mamba_dir(hidden_states, in_proj_w, conv_w_f, conv_b_f, x_proj_w_f, dt_proj_w_f, dt_proj_b_f, A_log_f, D_f, out_proj_w)
        h_rev = jnp.flip(hidden_states, axis=1)
        out_rev = _mamba_dir(h_rev, in_proj_w, conv_w_r, conv_b_r, x_proj_w_r, dt_proj_w_r, dt_proj_b_r, A_log_r, D_r, out_proj_w)
        return out_fwd + jnp.flip(out_rev, axis=1)

    def _L1_ffn_ref(x, Wg, bg, We, be):
        import jax, jax.numpy as jnp
        import numpy as np
        B, S, D, E = (4, 512, 128, 8)
        probs = jax.nn.softmax(x @ Wg + bg, axis=-1)
        idx = jnp.argmax(probs, axis=-1)
        p = jnp.take_along_axis(probs, idx[..., None], axis=-1)[..., 0]
        e_idx = idx % We.shape[0]
        h = jax.nn.relu(jnp.einsum('bsd,edf->besf', x, We) + be[None, :, None, :])
        onehot = jax.nn.one_hot(e_idx, We.shape[0], dtype=x.dtype)
        out = jnp.einsum('besf,bse->bsf', h, onehot) * p[..., None]
        return out

    def _L2_attn_ref(src, in_proj_w, in_proj_b, out_proj_w, out_proj_b, Qp_w, Qp_b, Kp_w, Kp_b, Vp_w, Vp_b, lam, ff1_w, ff1_b, ff2_w, ff2_b, ln1_g, ln1_b, ln2_g, ln2_b):
        import jax, jax.numpy as jnp
        import numpy as np
        import math
        B, S, D, H, R, DFF = (4, 128, 128, 16, 64, 512)

        def _layernorm(x, g, b, eps=1e-05):
            m = jnp.mean(x, axis=-1, keepdims=True)
            v = jnp.var(x, axis=-1, keepdims=True)
            return (x - m) / jnp.sqrt(v + eps) * g + b
        b, s, d = src.shape
        dh = d // H
        qkv = src @ in_proj_w.T + in_proj_b
        q, k, v = jnp.split(qkv, 3, axis=-1)
        q = q.reshape(b, s, H, dh).transpose(0, 2, 1, 3)
        k = k.reshape(b, s, H, dh).transpose(0, 2, 1, 3)
        v = v.reshape(b, s, H, dh).transpose(0, 2, 1, 3)
        scores = jnp.einsum('bhqd,bhkd->bhqk', q, k) / math.sqrt(dh)
        attn = jax.nn.softmax(scores, axis=-1)
        ctx = jnp.einsum('bhqk,bhkd->bhqd', attn, v)
        ctx = ctx.transpose(0, 2, 1, 3).reshape(b, s, d)
        dense_output = ctx @ out_proj_w.T + out_proj_b
        Q = src @ Qp_w.T + Qp_b
        K = src @ Kp_w.T + Kp_b
        V = src @ Vp_w.T + Vp_b
        QK = jnp.einsum('bqr,bkr->bqk', Q, K) / math.sqrt(R)
        aw = jax.nn.softmax(QK, axis=-1)
        kk = max(1, int(s * 0.2))
        topv, topi = jax.lax.top_k(aw, kk)
        bi = jnp.arange(b)[:, None, None]
        si = jnp.arange(s)[None, :, None]
        sparse_attn = jnp.zeros_like(aw).at[bi, si, topi].set(topv)
        sparse_attn = sparse_attn / (jnp.sum(sparse_attn, axis=-1, keepdims=True) + 1e-09)
        sparse_output = jnp.einsum('bqk,bkd->bqd', sparse_attn, V)
        sig = jax.nn.sigmoid(lam)
        fused = sig * dense_output + (1.0 - sig) * sparse_output
        x = _layernorm(src + fused, ln1_g, ln1_b)
        ff = jax.nn.relu(x @ ff1_w.T + ff1_b) @ ff2_w.T + ff2_b
        return _layernorm(x + ff, ln2_g, ln2_b)

    def _L2_ffn_ref(x, w1_w, w1_s, w2_w, w2_s, h1_w, h1_s, h2_w, h2_s, w3_w, w3_s):
        import jax, jax.numpy as jnp
        import numpy as np
        D_IN, D_HID = (128, 512)

        def _ternary(key, shape):
            return jax.random.randint(key, shape, -1, 2).astype(jnp.float32)

        def _tlin(x, w, s):
            return jnp.einsum('bsi,oi->bso', x, w) * s
        h = jax.nn.silu(_tlin(x, w1_w, w1_s)) * _tlin(x, w2_w, w2_s)
        h = jax.nn.gelu(_tlin(h, h1_w, h1_s), approximate=False)
        h = jax.nn.gelu(_tlin(h, h2_w, h2_s), approximate=False)
        return _tlin(h, w3_w, w3_s)

    def _L3_attn_ref(x, w_qkv, w_o):
        import jax, jax.numpy as jnp
        import numpy as np
        HIDDEN = 128
        HEADS = 16
        BATCH = 2
        SEQ = 256
        b, s, hid = x.shape
        heads = HEADS
        d = hid // heads
        qkv = x @ w_qkv.T * hid ** (-0.5)
        qkv = qkv.reshape(b, s, 3, heads, d)
        q = jnp.transpose(qkv[:, :, 0], (0, 2, 1, 3))
        k = jnp.transpose(qkv[:, :, 1], (0, 2, 1, 3))
        v = jnp.transpose(qkv[:, :, 2], (0, 2, 1, 3))
        scores = jnp.einsum('bhqd,bhkd->bhqk', q, k) * d ** (-0.5)
        attn = jax.nn.softmax(scores, axis=-1) * (s / np.sqrt(s - 1.0))
        out = jnp.einsum('bhqk,bhkd->bhqd', attn, v) * s ** (-0.5)
        out = jnp.transpose(out, (0, 2, 1, 3)).reshape(b, s, hid)
        return out @ w_o.T * hid ** (-0.5)

    def _L3_ffn_ref(x, w_gate, w_up, w_down):
        import jax, jax.numpy as jnp
        import numpy as np
        DIM = 128
        HIDDEN = 384
        SCALE = 1.0 / 127.0

        def _dequant(w_int, dtype):
            return w_int.astype(dtype) * jnp.asarray(SCALE, dtype)
        wg = _dequant(w_gate, x.dtype)
        wu = _dequant(w_up, x.dtype)
        wd = _dequant(w_down, x.dtype)
        gate = jnp.einsum('bsd,hd->bsh', x, wg)
        up = jnp.einsum('bsd,hd->bsh', x, wu)
        h = jax.nn.silu(gate) * up
        return jnp.einsum('bsh,dh->bsd', h, wd)
    x = L0_attn_x
    x = x + _L0_attn_ref(_layernorm(x, axis=-1), L0_attn_W_disp, L0_attn_W_val, L0_attn_rel_pos_emb, L0_attn_W_strain, L0_attn_W_pos, L0_attn_W_bond, L0_attn_W_dmg, L0_attn_b_dmg, L0_attn_W_dmg_out, L0_attn_b_dmg_out, L0_attn_W_cproj)
    x = x + _L0_ffn_ref(_layernorm(x, axis=-1), L0_ffn_m1, L0_ffn_m2, L0_ffn_mb, L0_ffn_w1, L0_ffn_w2, L0_ffn_b2)
    x = x + _L1_attn_ref(_layernorm(x, axis=-1), L1_attn_in_proj_w, L1_attn_out_proj_w, L1_attn_conv_w_f, L1_attn_conv_b_f, L1_attn_x_proj_w_f, L1_attn_dt_proj_w_f, L1_attn_dt_proj_b_f, L1_attn_A_log_f, L1_attn_D_f, L1_attn_conv_w_r, L1_attn_conv_b_r, L1_attn_x_proj_w_r, L1_attn_dt_proj_w_r, L1_attn_dt_proj_b_r, L1_attn_A_log_r, L1_attn_D_r)
    x = x + _L1_ffn_ref(_layernorm(x, axis=-1), L1_ffn_Wg, L1_ffn_bg, L1_ffn_We, L1_ffn_be)
    x = x + _L2_attn_ref(_layernorm(x, axis=-1), L2_attn_in_proj_w, L2_attn_in_proj_b, L2_attn_out_proj_w, L2_attn_out_proj_b, L2_attn_Qp_w, L2_attn_Qp_b, L2_attn_Kp_w, L2_attn_Kp_b, L2_attn_Vp_w, L2_attn_Vp_b, L2_attn_lam, L2_attn_ff1_w, L2_attn_ff1_b, L2_attn_ff2_w, L2_attn_ff2_b, L2_attn_ln1_g, L2_attn_ln1_b, L2_attn_ln2_g, L2_attn_ln2_b)
    x = x + _L2_ffn_ref(_layernorm(x, axis=-1), L2_ffn_w1_w, L2_ffn_w1_s, L2_ffn_w2_w, L2_ffn_w2_s, L2_ffn_h1_w, L2_ffn_h1_s, L2_ffn_h2_w, L2_ffn_h2_s, L2_ffn_w3_w, L2_ffn_w3_s)
    x = x + _L3_attn_ref(_layernorm(x, axis=-1), L3_attn_w_qkv, L3_attn_w_o)
    x = x + _L3_ffn_ref(_layernorm(x, axis=-1), L3_ffn_w_gate, L3_ffn_w_up, L3_ffn_w_down)
    return x

_drawn_inputs = setup_inputs


def setup_inputs(seed=0):
    import zlib

    import numpy as np

    out = dict(_drawn_inputs(seed))
    spreads = {'L0_attn_b_dmg': (0.0, 0.1),
     'L1_attn_dt_proj_b_f': (-4.600166320800781, 0.2),
     'L1_attn_D_f': (1.0, 0.2),
     'L1_attn_dt_proj_b_r': (-4.600166320800781, 0.2),
     'L1_attn_D_r': (1.0, 0.2),
     'L1_ffn_bg': (0.0, 0.1),
     'L1_ffn_be': (0.0, 0.1),
     'L2_attn_in_proj_b': (0.0, 0.1),
     'L2_attn_out_proj_b': (0.0, 0.1),
     'L2_attn_Qp_b': (0.0, 0.1),
     'L2_attn_Kp_b': (0.0, 0.1),
     'L2_attn_Vp_b': (0.0, 0.1),
     'L2_attn_ff1_b': (0.0, 0.1),
     'L2_attn_ff2_b': (0.0, 0.1),
     'L2_attn_ln1_g': (1.0, 0.2),
     'L2_attn_ln1_b': (0.0, 0.1),
     'L2_attn_ln2_g': (1.0, 0.2),
     'L2_attn_ln2_b': (0.0, 0.1)}
    factors = {}
    for name, (base, spread) in spreads.items():
        noise = np.random.default_rng([zlib.crc32(name.encode()), seed]).standard_normal(out[name].shape)
        drawn = base * np.exp(spread * noise) if base else spread * noise
        out[name] = jnp.asarray(drawn.astype(out[name].dtype))
    for name, factor in factors.items():
        out[name] = (out[name] * factor).astype(out[name].dtype)
    return out
```

```python
from contextlib import ExitStack

import concourse.bass as bass
from concourse import mybir

P = 128
T = 2048
TB = T // P
C = 128
CH = 512
NCH = T // CH

F32 = mybir.dt.float32
BF16 = mybir.dt.bfloat16
I32 = mybir.dt.int32
ALU = mybir.AluOpType
ACT = mybir.ActivationFunctionType
AX = mybir.AxisListType.X
NEG = -1.0e30


class Steps:

    def __init__(self, eng, sem):
        self.eng, self.sem, self.n, self.base = eng, sem, 0, 0

    def __call__(self, ins):
        self.n += 1
        ins.then_inc(self.sem, 1)
        self.eng.wait_ge(self.sem, self.base + self.n)

    def enter(self, i, per, first=0):
        self.outer, self.base, self.per = self.n, (i - first) * per + self.n, per
        self.n = 0

    def leave(self, turns):
        assert self.n == self.per, (self.n, self.per)
        self.n, self.base = self.outer + turns * self.per, 0


class Room:

    def __init__(self, nc, ctx, tag):
        self.nc, self.ctx, self.tag = nc, ctx, tag

    def sb(self, name, shape, dt=F32):
        return self.ctx.enter_context(self.nc.sbuf_tensor(f"{self.tag}_{name}", shape, dt))

    def sem(self, name):
        return self.ctx.enter_context(self.nc.semaphore(f"{self.tag}_{name}"))


class Shared:
    pass


def setup_shared(nc, ctx, g, x_dram):
    r = Room(nc, ctx, "all")
    g.X = r.sb("x", [P, TB, C])
    g.hT = r.sb("hT", [C, T])
    g.ident = r.sb("ident", [P, P])
    g.ones = r.sb("ones", [P, P])
    g.eps = r.sb("eps", [P, 1])
    g.ps = ctx.enter_context(nc.psum_tensor("ps", [P, 8 * CH], F32))
    x_loaded, zeroed, ready = r.sem("x_loaded"), r.sem("ident_zeroed"), r.sem("consts_ready")
    with nc.Block() as block:

        @block.sync
        def _(sp):
            sp.dma_start(g.X[:, :, :], x_dram.rearrange("a (b p) c -> p (a b) c", p=P)).then_inc(x_loaded, 16)
            sp.wait_ge(x_loaded, 16)

        @block.gpsimd
        def _(pool):
            pool.memset(g.ident[:, :], 0.0).then_inc(zeroed, 1)
            pool.wait_ge(zeroed, 1)
            pool.affine_select(out=g.ident[:, :], in_=g.ident[:, :], compare_op=ALU.not_equal, fill=1.0,
                               base=0, pattern=[[-1, P]], channel_multiplier=1).then_inc(ready, 1)

        @block.vector
        def _(dve):
            dve.memset(g.ones[:, :], 1.0).then_inc(ready, 1)
            dve.memset(g.eps[:, :], 1.0e-5).then_inc(ready, 1)


def layernorm_transpose(nc, g, tag, load=None, src=None, affine=None, natural=None, transposed=True):
    src = g.X if src is None else src
    with ExitStack() as ctx:
        r = Room(nc, ctx, tag)
        st = r.sb("bn", [P, TB, 6])
        mv = r.sb("meanvar", [P, TB, 2])
        ve = r.sb("vareps", [P, TB])
        sd = r.sb("std", [P, TB])
        rs = r.sb("rstd", [P, TB])
        tmp = r.sb("newton", [P, TB])
        xn = r.sb("xn", [P, TB, C]) if natural is None else natural
        steps, var_ready, std_ready = r.sem("steps"), r.sem("var_ready"), r.sem("std_ready")
        norm_ready, tr_ready, ht_ready = r.sem("norm_ready"), r.sem("tr_ready"), r.sem("ht_ready")
        loads = r.sem("weights_loaded")
        with nc.Block() as block:

            @block.sync
            def _(sp):
                if load is not None:
                    n = load(sp, loads)
                    sp.wait_ge(loads, 16 * n)

            @block.vector
            def _(dve):
                step = Steps(dve, steps)
                for b in range(TB):
                    last = dve.bn_stats(st[:, b, :], src[:, b, :])
                step(last)
                for b in range(TB):
                    last = dve.bn_aggr(mv[:, b, :], st[:, b, :])
                step(last)
                step(dve.tensor_scalar(ve[:, :], mv[:, :, 1], 1.0e-5, None, ALU.add))
                dve.nop().then_inc(var_ready, 1)
                dve.wait_ge(std_ready, 1)
                step(dve.reciprocal(rs[:, :], sd[:, :]))
                step(dve.tensor_tensor(tmp[:, :], rs[:, :], rs[:, :], ALU.mult))
                step(dve.tensor_tensor(tmp[:, :], tmp[:, :], ve[:, :], ALU.mult))
                step(dve.tensor_scalar(tmp[:, :], tmp[:, :], -0.5, 1.5, ALU.mult, ALU.add))
                step(dve.tensor_tensor(rs[:, :], rs[:, :], tmp[:, :], ALU.mult))
                plain = affine is None
                for b in range(TB):
                    ins = dve.tensor_scalar(xn[:, b, :], src[:, b, :], mv[:, b, 0:1], rs[:, b:b + 1], ALU.subtract, ALU.mult)
                    if plain:
                        ins.then_inc(norm_ready, 1)
                if not plain:
                    step(ins)
                    step(dve.tensor_tensor(xn[:, :, :], xn[:, :, :], affine[0].unsqueeze(1).broadcast_to([P, TB, C]), ALU.mult))
                    dve.tensor_tensor(xn[:, :, :], xn[:, :, :], affine[1].unsqueeze(1).broadcast_to([P, TB, C]), ALU.add).then_inc(norm_ready, TB)
                for q in range(1, NCH if transposed else 1, 2):
                    dve.wait_ge(tr_ready, q + 1)
                    dve.tensor_copy(g.hT[:, q * CH:(q + 1) * CH], g.ps[:, q * CH:(q + 1) * CH]).then_inc(ht_ready, 1)

            @block.scalar
            def _(act):
                act.wait_ge(var_ready, 1)
                act.activation(sd[:, :], ve[:, :], ACT.Sqrt).then_inc(std_ready, 1)
                for q in range(0, NCH if transposed else 0, 2):
                    act.wait_ge(tr_ready, q + 1)
                    act.copy(g.hT[:, q * CH:(q + 1) * CH], g.ps[:, q * CH:(q + 1) * CH]).then_inc(ht_ready, 1)

            @block.tensor
            def _(pe):
                for b in range(TB if transposed else 0):
                    pe.wait_ge(norm_ready, b + 1)
                    last = pe.transpose(g.ps[:, b * P:(b + 1) * P], xn[:, b, :], g.ident[:, :])
                    if b % 4 == 3:
                        last.then_inc(tr_ready, 1)


def bond_attention(nc, g, I):
    NH, HS, BD, W = 16, 8, 16, 64
    HH = P // BD
    PAD = W
    NG = 8
    GD = W // NG
    UW = W + P
    with ExitStack() as ctx:
        r = Room(nc, ctx, "l0a")
        val = r.sb("val", [P, TB, NH, HS])
        valp = r.sb("valp", [W, TB, NH, HS])
        wc = r.sb("wc", [P, 4, C])
        zero = r.sb("zero", [P, 2 * UW])
        band = nc.dram_tensor("l0a_band", [TB, P, NH * UW], F32, kind="Internal").ap()
        band_zeroed = r.sem("band_zeroed")
        lgt = ExitStack()
        rl = Room(nc, lgt, "l0a")
        L = rl.sb("logits", [P, NG, T])
        with ExitStack() as ctx1:
            r1 = Room(nc, ctx1, "l0m")
            A = r1.sb("A", [P, 2, 2, PAD + T])
            Dj = r1.sb("Dj", [P, 2, PAD + T])
            pos = r1.sb("pos", [P, W])
            wb = r1.sb("wb", [P, 2, 2, 2, 32])
            bdo = r1.sb("bdo", [P, 1])
            with ExitStack() as ctx2:
                r2 = Room(nc, ctx2, "l0w")
                wd = r2.sb("wd", [C, 2 * P])
                wv = r2.sb("wv", [C, C])
                wrep = r2.sb("wrep", [P, 2, BD])
                wblk = r2.sb("wblk", [P, 2, P])
                wpos = r2.sb("wpos", [BD, BD])
                wposr = r2.sb("wposr", [BD, HH, BD])
                relT = r2.sb("relT", [BD, W])
                wo = r2.sb("wo", [P, 2])
                bm = r2.sb("bm", [P, HH])
                bd = r2.sb("bd", [P, 1])
                disp = L[:, 0:2, :]

                zr = r2.sem("zeroed")

                def load(sp, s):
                    n = 0

                    def ld(dst, src):
                        nonlocal n
                        n += 1
                        sp.dma_start(dst, src).then_inc(s, 16)
                    ld(wd[:, :], I["L0_attn_W_disp"])
                    ld(wv[:, :], I["L0_attn_W_val"])
                    ld(wpos[:, :], I["L0_attn_W_pos"])
                    ld(relT[:, :], I["L0_attn_rel_pos_embT"])
                    for h in range(HH):
                        rows = slice(h * BD, (h + 1) * BD)
                        ld(wrep[rows, 0, :], I["L0_attn_W_dmg"])
                        ld(wrep[rows, 1, :], I["L0_attn_W_strain"])
                        ld(wo[rows, 0:1], I["L0_attn_W_dmg_out"])
                        ld(wo[rows, 1:2], I["L0_attn_W_bond"])
                        ld(bd[rows, :], I["L0_attn_b_dmg"].rearrange("(a b) -> a b", b=1))
                    ld(bdo[:, :], I["L0_attn_b_dmg_out"].rearrange("(a b) -> a b", b=1).broadcast_to([P, 1]))
                    sp.wait_ge(zr, 3)
                    for h in range(NH):
                        ld(wc[32 * (h % 4):32 * (h % 4) + HS, h // 4, :], I["L0_attn_W_cproj"][h * HS:(h + 1) * HS, :])
                    return n

                made, sel = r2.sem("mask_made"), r2.sem("mask_steps")
                with nc.Block() as block:

                    @block.vector
                    def _(dve):
                        dve.memset(wc[:, :, :], 0.0).then_inc(zr, 1)
                        dve.memset(zero[:, :], 0.0).then_inc(zr, 1)
                        dve.memset(wb[:, :, :, :, :], 0.0).then_inc(zr, 1)
                        dve.memset(A[:, :, :, 0:PAD], 0.0)
                        dve.memset(Dj[:, :, 0:PAD], 0.0)

                    @block.gpsimd
                    def _(pool):
                        pool.memset(bm[:, :], 1.0).then_inc(sel, 1)
                        pool.wait_ge(sel, 1)
                        pool.affine_select(out=bm[:, :], in_=bm[:, :], compare_op=ALU.is_ge, fill=0.0, base=0,
                                           pattern=[[-BD, HH]], channel_multiplier=1).then_inc(sel, 1)
                        pool.wait_ge(sel, 2)
                        pool.affine_select(out=bm[:, :], in_=bm[:, :], compare_op=ALU.is_ge, fill=0.0, base=BD - 1,
                                           pattern=[[BD, HH]], channel_multiplier=-1).then_inc(made, 1)

                layernorm_transpose(nc, g, "ln0", load)

                built, disp_ps, disp_sb = r2.sem("weights_built"), r2.sem("disp_in_psum"), r2.sem("disp_copied")
                a_ps, a_sb = r2.sem("a_in_psum"), r2.sem("a_copied")
                v_ps, v_sb = r2.sem("val_in_psum"), r2.sem("val_copied")
                with nc.Block() as block:

                    @block.sync
                    def _(sp):
                        for b in range(TB):
                            sp.dma_start(band[b].rearrange("p (r u) -> p r u", u=2 * UW),
                                         zero[:, :].unsqueeze(1).broadcast_to([P, NH // 2, 2 * UW])).then_inc(band_zeroed, 16)

                    @block.vector
                    def _(dve):
                        for k in range(2):
                            dve.tensor_tensor(wblk[:, k, :].rearrange("p (h c) -> p h c", c=BD),
                                              wrep[:, k, :].unsqueeze(1).broadcast_to([P, HH, BD]),
                                              bm[:, :].unsqueeze(2).broadcast_to([P, HH, BD]), ALU.mult)
                            for hf in range(2):
                                for par in range(2):
                                    c0 = par * 16 + hf * HH
                                    dve.tensor_scalar(wb[:, k, hf, par, c0:c0 + HH], bm[:, :], wo[:, k:k + 1], None, ALU.mult)
                        dve.tensor_copy(wposr[:, :, :], wpos[:, :].unsqueeze(1).broadcast_to([BD, HH, BD])).then_inc(built, 1)
                        for hf in range(2):
                            for q in range(2):
                                dve.wait_ge(disp_ps, 2 * hf + q + 1)
                                dve.tensor_copy(disp[:, hf, q * 1024:(q + 1) * 1024],
                                                g.ps[:, hf * T + q * 1024:hf * T + (q + 1) * 1024]).then_inc(disp_sb, 1)
                        for n in range(4):
                            dve.wait_ge(a_ps, n + 1)
                            dve.tensor_copy(A[:, n // 2, n % 2, PAD:], g.ps[:, (n % 2) * T:(n % 2 + 1) * T]).then_inc(a_sb, 1)
                            if n % 2 == 0:
                                dve.wait_ge(a_sb, n + 1)
                                dve.tensor_scalar(Dj[:, n // 2, PAD:], A[:, n // 2, 0, PAD:], bd[:, :], None, ALU.add)
                        for n in range(TB // 4):
                            dve.wait_ge(v_ps, 2 * n + 1)
                            dve.tensor_copy(val[:, 4 * n:4 * n + 4, :, 0:HS],
                                            g.ps[:, 0:CH].rearrange("p (b h e) -> p b h e", b=4, e=HS)).then_inc(v_sb, 1)
                            dve.wait_ge(v_ps, 2 * n + 2)
                            dve.tensor_copy(valp[:, 4 * n:4 * n + 4, :, 0:HS],
                                            g.ps[0:W, CH:2 * CH].rearrange("p (b h e) -> p b h e", b=4, e=HS)).then_inc(v_sb, 1)
                        dve.wait_ge(v_ps, 2 * TB // 4 + 1)
                        dve.tensor_copy(pos[:, :], g.ps[:, 2 * CH:2 * CH + W])

                    @block.tensor
                    def _(pe):
                        for hf in range(2):
                            for q in range(NCH):
                                mm = pe.matmul(g.ps[:, hf * T + q * CH:hf * T + (q + 1) * CH], wd[:, hf * P:(hf + 1) * P],
                                               g.hT[:, q * CH:(q + 1) * CH], start=True, stop=True)
                                if q % 2:
                                    mm.then_inc(disp_ps, 1)
                        pe.wait_ge(built, 1)
                        for n in range(4):
                            pe.wait_ge(disp_sb, 4)
                            if n >= 2:
                                pe.wait_ge(a_sb, n - 1)
                            for q in range(NCH):
                                mm = pe.matmul(g.ps[:, (n % 2) * T + q * CH:(n % 2) * T + (q + 1) * CH], wblk[:, n % 2, :],
                                               disp[:, n // 2, q * CH:(q + 1) * CH], start=True, stop=True)
                            mm.then_inc(a_ps, 1)
                        pe.wait_ge(a_sb, 4)
                        for n in range(TB // 4):
                            if n:
                                pe.wait_ge(v_sb, 2 * n - 1)
                            for b in range(4 * n, 4 * n + 4):
                                mm = pe.matmul(g.ps[:, (b % 4) * P:(b % 4 + 1) * P], g.hT[:, b * P:(b + 1) * P], wv[:, :],
                                               start=True, stop=True)
                            mm.then_inc(v_ps, 1)
                            if n:
                                pe.wait_ge(v_sb, 2 * n)
                            for b in range(4 * n, 4 * n + 4):
                                t0 = max(b * P - W, 0)
                                mm = pe.matmul(g.ps[0:W, CH + (b % 4) * P:CH + (b % 4 + 1) * P], g.hT[:, t0:t0 + W], wv[:, :],
                                               start=True, stop=True)
                            mm.then_inc(v_ps, 1)
                        pe.matmul(g.ps[:, 2 * CH:2 * CH + W], wposr[:, :, :].rearrange("k h c -> k (h c)"), relT[:, :],
                                  start=True, stop=True).then_inc(v_ps, 1)

            ND, NP_, NGB = 3, 1, 2
            dd = r1.sb("diff_dve", [P, ND, T])
            dp = r1.sb("diff_pool", [P, NP_, T])
            ge = r1.sb("gelu", [P, NGB, T])
            th = r1.sb("tanh", [P, T])
            hb = r1.sb("half_bdo", [P, 1])
            pcur = r1.sb("pos_of_group", [P, GD])
            SPG = 2 * GD * 2
            diff_dve, diff_pool = r1.sem("diff_dve"), r1.sem("diff_pool")
            free_dve, free_pool = r1.sem("free_dve"), r1.sem("free_pool")
            gelu_done, gelu_used = r1.sem("gelu_done"), r1.sem("gelu_used")
            dmg_done, bond_done, tanh_done, logit_done = r1.sem("dmg_done"), r1.sem("bond_done"), r1.sem("tanh_done"), r1.sem("logit_done")
            hb_ready, pos_ready = r1.sem("hb_ready"), r1.sem("pos_ready")
            pool_steps = [s for s in range(SPG) if s % 3 == 2]
            dve_steps = [s for s in range(SPG) if s % 3 != 2]
            NDV, NPO = len(dve_steps), len(pool_steps)

            def where(s):
                k, rest = divmod(s, 2 * GD)
                d, hf = divmod(rest, 2)
                return k, d, hf

            with nc.Block() as block:

                def subtract(eng, out, gi, s):
                    k, d, hf = where(s)
                    aj = (Dj[:, hf, :] if k == 0 else A[:, hf, 1, :])
                    at = A[:, hf, k, PAD:PAD + T]
                    return eng.tensor_tensor(out, aj[:, bass.ds(gi * GD + (d + 1), T)], at, ALU.subtract)

                @block.vector
                def _(dve):
                    dve.tensor_scalar(hb[:, :], bdo[:, :], 0.5, None, ALU.mult).then_inc(hb_ready, 1)

                    def group(gi, first):
                        for n, s in enumerate(dve_steps):
                            if not (first and n < ND):
                                dve.wait_ge(free_dve, gi * NDV + (n + 1 - ND))
                            b = (n + (0 if True else 0))
                            subtract(dve, dd[:, b % ND, :], gi, s).then_inc(diff_dve, 1)
                        dve.wait_ge(tanh_done, gi + 1)
                        dve.wait_ge(bond_done, gi + 1)
                        dve.scalar_tensor_tensor(L[:, bass.ds(gi, 1), :].rearrange("p a t -> p (a t)"), th[:, :], -5.0,
                                                 g.ps[:, T:2 * T], ALU.mult, ALU.add).then_inc(logit_done, 1)
                    group(0, True)
                    with dve.Fori(1, NG) as gi:
                        group(gi, False)

                @block.gpsimd
                def _(pool):
                    def group(gi, first):
                        for n, s in enumerate(pool_steps):
                            if not (first and n < NP_):
                                pool.wait_ge(free_pool, gi * NPO + (n + 1 - NP_))
                            subtract(pool, dp[:, n % NP_, :], gi, s).then_inc(diff_pool, 1)
                    group(0, True)
                    with pool.Fori(1, NG) as gi:
                        group(gi, False)

                @block.scalar
                def _(act):
                    act.wait_ge(hb_ready, 1)

                    def group(gi, first):
                        nd = npo = 0
                        act.copy(pcur[:, :], pos[:, bass.ds(gi * GD, GD)]).then_inc(pos_ready, 1)
                        act.wait_ge(pos_ready, gi + 1)
                        for s in range(SPG):
                            k, d, hf = where(s)
                            if s == SPG // 2 + 2:
                                act.wait_ge(dmg_done, gi + 1)
                                if not first:
                                    act.wait_ge(logit_done, gi)
                                act.activation(th[:, :], g.ps[:, 0:T], ACT.Tanh, bias=hb[:, :], scale=0.5).then_inc(tanh_done, 1)
                            if s in pool_steps:
                                act.wait_ge(diff_pool, gi * NPO + npo + 1)
                                src, fr = dp[:, npo % NP_, :], free_pool
                                npo += 1
                            else:
                                act.wait_ge(diff_dve, gi * NDV + nd + 1)
                                src, fr = dd[:, nd % ND, :], free_dve
                                nd += 1
                            if not (first and s < NGB):
                                act.wait_ge(gelu_used, gi * SPG + (s + 1 - NGB))
                            bias = 0.0 if k == 0 else pcur[:, d:d + 1]
                            act.activation(ge[:, s % NGB, :], src, ACT.Gelu, bias=bias).then_inc(gelu_done, 1)
                            act.wait_ge(gelu_done, gi * SPG + s + 1)
                            act.sem_inc(fr, 1)
                    group(0, True)
                    with act.Fori(1, NG) as gi:
                        group(gi, False)

                @block.tensor
                def _(pe):
                    def group(gi, first):
                        for s in range(SPG):
                            k, d, hf = where(s)
                            pe.wait_ge(gelu_done, gi * SPG + s + 1)
                            if not first and s == 0:
                                pe.wait_ge(tanh_done, gi)
                            if not first and s == SPG // 2:
                                pe.wait_ge(logit_done, gi)
                            j, par = d // 2, d % 2
                            for q in range(NCH):
                                col = k * T + q * CH
                                mm = pe.matmul(g.ps[32 * j:32 * j + 32, col:col + CH], wb[:, k, hf, par, :],
                                               ge[:, s % NGB, q * CH:(q + 1) * CH],
                                               start=(par == 0 and hf == 0), stop=(par == 1 and hf == 1))
                            mm.then_inc(gelu_used, 1)
                            if s == SPG // 2 - 1:
                                pe.wait_ge(gelu_used, gi * SPG + s + 1)
                                pe.sem_inc(dmg_done, 1)
                            if s == SPG - 1:
                                pe.wait_ge(gelu_used, gi * SPG + s + 1)
                                pe.sem_inc(bond_done, 1)
                    group(0, True)
                    with pe.Fori(1, NG) as gi:
                        group(gi, False)

                @block.sync
                def _(sp):
                    sp.wait_ge(band_zeroed, 16 * TB)
        with ExitStack() as ctx3:
            r3 = Room(nc, ctx3, "l0s")
            LT = r3.sb("LT", [P, TB, NH, W])
            mx = r3.sb("mx", [P, TB, NH])
            sm = r3.sb("sm", [P, TB, NH])
            tr, ev, masked = r3.sem("transposed"), r3.sem("copied"), r3.sem("masked")
            steps, subd, expd, normed = r3.sem("steps"), r3.sem("max_subtracted"), r3.sem("exp_done"), r3.sem("normalised")
            band_written = r3.sem("band_written")
            with nc.Block() as block:

                @block.tensor
                def _(pe):
                    for b in range(TB):
                        if b >= 4:
                            pe.wait_ge(ev, 2 * (b - 3))
                        for gi in range(NG):
                            mm = pe.transpose(g.ps[:, (b % 4) * 1024 + gi * P:(b % 4) * 1024 + (gi + 1) * P],
                                              L[:, gi, b * P:(b + 1) * P], g.ident[:, :])
                            if gi % 4 == 3:
                                mm.then_inc(tr, 1)

                @block.scalar
                def _(act):
                    def evac(b):
                        for hf in range(2):
                            act.wait_ge(tr, 2 * b + hf + 1)
                            act.copy(LT[:, b, :, hf * 32:(hf + 1) * 32],
                                     g.ps[:, (b % 4) * 1024 + hf * CH:(b % 4) * 1024 + (hf + 1) * CH].rearrange(
                                         "p (d h) -> p h d", h=NH)).then_inc(ev, 1)
                    for b in range(TB):
                        evac(b)
                    for q in range(4):
                        act.wait_ge(subd, q + 1)
                        act.activation(LT[:, 4 * q:4 * q + 4, :, :], LT[:, 4 * q:4 * q + 4, :, :], ACT.Exp).then_inc(expd, 1)

                @block.gpsimd
                def _(pool):
                    pool.wait_ge(ev, 2)
                    pool.affine_select(out=LT[:, 0, :, :], in_=LT[:, 0, :, :], compare_op=ALU.is_ge, fill=NEG,
                                       base=1 - W, pattern=[[0, NH], [1, W]], channel_multiplier=1).then_inc(masked, 1)

                @block.vector
                def _(dve):
                    step = Steps(dve, steps)

                    def exps(q):
                        b = slice(4 * q, 4 * q + 4)
                        dve.wait_ge(expd, q + 1)
                        step(dve.tensor_reduce(sm[:, b, :], LT[:, b, :, :], AX, ALU.add))
                        step(dve.reciprocal(sm[:, b, :], sm[:, b, :]))
                        dve.tensor_tensor(LT[:, b, :, :].rearrange("p b h d -> p (b h) d"), LT[:, b, :, :].rearrange("p b h d -> p (b h) d"),
                                          sm[:, b, :].rearrange("p b h -> p (b h)").unsqueeze(2).broadcast_to([P, 4 * NH, W]),
                                          ALU.mult).then_inc(normed, 1)
                    for q in range(4):
                        b = slice(4 * q, 4 * q + 4)
                        dve.wait_ge(ev, 8 * (q + 1))
                        if q == 0:
                            dve.wait_ge(masked, 1)
                        step(dve.tensor_reduce(mx[:, b, :], LT[:, b, :, :], AX, ALU.max))
                        dve.tensor_tensor(LT[:, b, :, :].rearrange("p b h d -> p (b h) d"), LT[:, b, :, :].rearrange("p b h d -> p (b h) d"),
                                          mx[:, b, :].rearrange("p b h -> p (b h)").unsqueeze(2).broadcast_to([P, 4 * NH, W]),
                                          ALU.subtract).then_inc(subd, 1)
                        if q:
                            exps(q - 1)
                    exps(3)

                @block.sync
                def _(sp):
                    for b in range(TB):
                        sp.wait_ge(normed, b // 4 + 1)
                        dst = bass.AP(band.tensor, b * P * NH * UW + 1, [[NH * UW + 1, P], [UW, NH], [1, W]])
                        sp.dma_start(dst, LT[:, b, :, :]).then_inc(band_written, 16)
                    sp.wait_ge(band_written, 16 * TB)
        lgt.close()
        with ExitStack() as ctx4:
            r4 = Room(nc, ctx4, "l0v")
            vc = r4.sb("vc", [P, TB, NH, 32])
            vp = r4.sb("vp", [W, TB, NH, 32])
            padded, filled = r4.sem("pad_zeroed"), r4.sem("pad_filled")
            bn = r4.sb("band", [P, 2, NH, UW])
            bt = r4.sb("bandT", [P, 2, NH // 4, 4, P])
            bp = r4.sb("bandTp", [W, 2, NH // 4, 4, P])
            ot = r4.sb("oT", [P, 2, 4, P])
            loaded = [r4.sem("band_loaded0"), r4.sem("band_loaded1")]
            tc_, tp, evc, evp = r4.sem("cur_transposed"), r4.sem("prev_transposed"), r4.sem("cur_copied"), r4.sem("prev_copied")
            ops, ocp, yps, xad = r4.sem("values_weighted"), r4.sem("o_copied"), r4.sem("y_in_psum"), r4.sem("x_added")
            QH = NH // 4
            with nc.Block() as block:

                @block.sync
                def _(sp):
                    for b in range(TB):
                        if b >= 2:
                            sp.wait_ge(tp, QH * (b - 1))
                        sp.dma_start(bn[:, b % 2, :, :].rearrange("p h u -> p (h u)"), band[b]).then_inc(loaded[b % 2], 16)
                    sp.wait_ge(loaded[0], 16 * TB // 2)
                    sp.wait_ge(loaded[1], 16 * TB // 2)

                @block.gpsimd
                def _(pool):
                    pool.memset(vc[:, :, :, :], 0.0).then_inc(padded, 1)
                    pool.memset(vp[:, :, :, :], 0.0).then_inc(padded, 1)
                    pool.wait_ge(padded, 2)
                    pool.tensor_copy(vc[:, :, :, 0:HS], val[:, :, :, :]).then_inc(filled, 1)
                    pool.tensor_copy(vp[:, :, :, 0:HS], valp[:, :, :, :]).then_inc(filled, 1)

                @block.tensor
                def _(pe):
                    def transposes(b):
                        pe.wait_ge(loaded[b % 2], 16 * (b // 2 + 1))
                        for hq in range(QH):
                            n = b * QH + hq
                            if n >= 2:
                                pe.wait_ge(evc, n - 1)
                            for k in range(4):
                                mm = pe.transpose(g.ps[:, (n % 2) * CH + k * P:(n % 2) * CH + (k + 1) * P],
                                                  bn[:, b % 2, 4 * hq + k, W:UW], g.ident[:, :])
                            mm.then_inc(tc_, 1)
                            if n >= 2:
                                pe.wait_ge(evp, n - 1)
                            for k in range(4):
                                mm = pe.transpose(g.ps[0:W, (2 + n % 2) * CH + k * P:(2 + n % 2) * CH + (k + 1) * P],
                                                  bn[:, b % 2, 4 * hq + k, 0:W], g.ident[:, :])
                            mm.then_inc(tp, 1)

                    def values(b):
                        pe.wait_ge(filled, 2)
                        pe.wait_ge(evc, QH * (b + 1))
                        pe.wait_ge(evp, QH * (b + 1))
                        if b >= 2:
                            pe.wait_ge(ocp, b - 1)
                        for hq in range(QH):
                            for k in range(4):
                                o = g.ps[32 * k:32 * k + 32, (4 + b % 2) * CH + hq * P:(4 + b % 2) * CH + (hq + 1) * P]
                                pe.matmul(o, vc[:, b, 4 * hq + k, :], bt[:, b % 2, hq, k, :], start=True, stop=False)
                                mm = pe.matmul(o, vp[:, b, 4 * hq + k, :], bp[:, b % 2, hq, k, :], start=False, stop=True)
                        mm.then_inc(ops, 1)

                    def project(b):
                        pe.wait_ge(ocp, b + 1)
                        if b >= 2:
                            pe.wait_ge(xad, b - 1)
                        for hq in range(QH):
                            mm = pe.matmul(g.ps[:, (6 + b % 2) * CH:(6 + b % 2) * CH + C], ot[:, b % 2, hq, :], wc[:, hq, :],
                                           start=(hq == 0), stop=(hq == QH - 1))
                        mm.then_inc(yps, 1)
                    for b in range(TB + 2):
                        if b < TB:
                            transposes(b)
                        if 1 <= b <= TB:
                            values(b - 1)
                        if b >= 2:
                            project(b - 2)

                @block.scalar
                def _(act):
                    for b in range(TB):
                        for hq in range(QH):
                            n = b * QH + hq
                            act.wait_ge(tc_, n + 1)
                            if b >= 2 and hq == 0:
                                act.wait_ge(ops, b - 1)
                            act.copy(bt[:, b % 2, hq, :, :].rearrange("p k t -> p (k t)"),
                                     g.ps[:, (n % 2) * CH:(n % 2 + 1) * CH]).then_inc(evc, 1)

                @block.vector
                def _(dve):
                    def finish(b):
                        dve.wait_ge(yps, b + 1)
                        dve.tensor_tensor(g.X[:, b, :], g.X[:, b, :], g.ps[:, (6 + b % 2) * CH:(6 + b % 2) * CH + C],
                                          ALU.add).then_inc(xad, 1)
                    for b in range(TB + 2):
                        if b < TB:
                            for hq in range(QH):
                                n = b * QH + hq
                                dve.wait_ge(tp, n + 1)
                                if b >= 2 and hq == 0:
                                    dve.wait_ge(ops, b - 1)
                                dve.tensor_copy(bp[:, b % 2, hq, :, :].rearrange("p k t -> p (k t)"),
                                                g.ps[0:W, (2 + n % 2) * CH:(2 + n % 2 + 1) * CH]).then_inc(evp, 1)
                        if 1 <= b <= TB:
                            dve.wait_ge(ops, b)
                            if b >= 3:
                                dve.wait_ge(yps, b - 2)
                            dve.tensor_copy(ot[:, (b - 1) % 2, :, :].rearrange("p k t -> p (k t)"),
                                            g.ps[:, (4 + (b - 1) % 2) * CH:(5 + (b - 1) % 2) * CH]).then_inc(ocp, 1)
                        if b >= 2:
                            finish(b - 2)


def masked_ffn(nc, g, I):
    D1, D2, DL = 8, 64, 64
    DF = D1 * D2
    KC = DF // P
    with ExitStack() as ctx:
        r = Room(nc, ctx, "l0f")
        m1 = r.sb("m1", [C, DL])
        m2 = r.sb("m2", [DL + 1, DF])
        w1 = r.sb("w1", [C, DF])
        w2 = r.sb("w2", [P, KC, C])
        b2 = r.sb("b2", [P, C])
        pri = r.sb("pri", [P, D2])
        lr = r.sb("lr", [DL + 1, T])

        def load(sp, s):
            sp.dma_start(m1[:, :], I["L0_ffn_m1"]).then_inc(s, 16)
            sp.dma_start(m2[0:DL, :], I["L0_ffn_m2"].rearrange("l x y -> l (x y)")).then_inc(s, 16)
            sp.dma_start(m2[DL:DL + 1, :], I["L0_ffn_mb"].rearrange("(a x) y -> a (x y)", a=1)).then_inc(s, 16)
            sp.dma_start(w1[:, :], I["L0_ffn_w1"].rearrange("d x y -> d (x y)")).then_inc(s, 16)
            sp.dma_start(w2[:, :, :], I["L0_ffn_w2T"].rearrange("x y c -> (x y) c").rearrange("(k p) c -> p k c", p=P)).then_inc(s, 16)
            sp.dma_start(b2[:, :], I["L0_ffn_b2"].rearrange("(a c) -> a c", a=1).broadcast_to([P, C])).then_inc(s, 16)
            return 6
        layernorm_transpose(nc, g, "ln1", load)
        mx = r.sb("mx", [P, 2, D1])
        px = r.sb("px", [P, 2, D1])
        eq = r.sb("eq", [P, 2, DF])
        pr = r.sb("pr", [P, 2, DF])
        mid = r.sb("mid", [P, 2, DF])
        midT = r.sb("midT", [P, 2, DF])
        lr_ps, lr_sb, const, steps = r.sem("lr_in_psum"), r.sem("lr_copied"), r.sem("const_ready"), r.sem("steps")
        lgt, up, hot, tied, act_ready = r.sem("logits_in_psum"), r.sem("mid_in_psum"), r.sem("equal_found"), r.sem("priority_ready"), r.sem("mid_masked")
        tr, mt, yps, xad, eqd = r.sem("mid_transposed"), r.sem("midT_copied"), r.sem("y_in_psum"), r.sem("x_added"), r.sem("logits_read")
        xb = r.sem("x_biased")
        with nc.Block() as block:

            @block.gpsimd
            def _(pool):
                pool.iota(pri[:, :], [[-1, D2]], base=D2, channel_multiplier=0, allow_small_or_imprecise_dtypes=True).then_inc(const, 1)
                pool.tensor_tensor(g.X[:, :, :], g.X[:, :, :], b2[:, :].unsqueeze(1).broadcast_to([P, TB, C]), ALU.add).then_inc(xb, 1)
                pool.wait_ge(const, 2)
                for b in range(TB):
                    pool.wait_ge(hot, b + 1)
                    if b >= 2:
                        pool.wait_ge(act_ready, b - 1)
                    pool.tensor_tensor(pr[:, b % 2, :].rearrange("p (x y) -> p x y", x=D1), eq[:, b % 2, :].rearrange("p (x y) -> p x y", x=D1),
                                       pri[:, :].unsqueeze(1).broadcast_to([P, D1, D2]), ALU.mult).then_inc(tied, 1)

            @block.tensor
            def _(pe):
                for q in range(NCH):
                    mm = pe.matmul(g.ps[0:DL, q * CH:(q + 1) * CH], m1[:, :], g.hT[:, q * CH:(q + 1) * CH], start=True, stop=True)
                mm.then_inc(lr_ps, 1)
                pe.wait_ge(lr_sb, 1)
                pe.wait_ge(const, 2)

                def front(b):
                    if b >= 2:
                        pe.wait_ge(eqd, b - 1)
                    pe.matmul(g.ps[:, (b % 2) * CH:(b % 2 + 1) * CH], lr[:, b * P:(b + 1) * P], m2[:, :], start=True, stop=True).then_inc(lgt, 1)
                    if b >= 2:
                        pe.wait_ge(act_ready, b - 1)
                    pe.matmul(g.ps[:, (2 + b % 2) * CH:(3 + b % 2) * CH], g.hT[:, b * P:(b + 1) * P], w1[:, :], start=True, stop=True).then_inc(up, 1)

                def back(b):
                    pe.wait_ge(act_ready, b + 1)
                    if b >= 2:
                        pe.wait_ge(mt, b - 1)
                    for k in range(KC):
                        mm = pe.transpose(g.ps[:, (4 + b % 2) * CH + k * P:(4 + b % 2) * CH + (k + 1) * P], mid[:, b % 2, k * P:(k + 1) * P], g.ident[:, :])
                    mm.then_inc(tr, 1)

                def last(b):
                    pe.wait_ge(mt, b + 1)
                    if b >= 2:
                        pe.wait_ge(xad, b - 1)
                    for k in range(KC):
                        mm = pe.matmul(g.ps[:, (6 + b % 2) * CH:(6 + b % 2) * CH + C], midT[:, b % 2, k * P:(k + 1) * P], w2[:, k, :],
                                       start=(k == 0), stop=(k == KC - 1))
                    mm.then_inc(yps, 1)
                for b in range(TB + 2):
                    if b < TB:
                        front(b)
                    if 1 <= b <= TB:
                        back(b - 1)
                    if b >= 2:
                        last(b - 2)

            @block.scalar
            def _(act):
                act.wait_ge(lr_ps, 1)
                act.copy(lr[0:DL, :], g.ps[0:DL, 0:T]).then_inc(lr_sb, 1)
                for b in range(TB):
                    act.wait_ge(tr, b + 1)
                    if b >= 2:
                        act.wait_ge(yps, b - 1)
                    act.copy(midT[:, b % 2, :], g.ps[:, (4 + b % 2) * CH:(5 + b % 2) * CH]).then_inc(mt, 1)

            @block.vector
            def _(dve):
                step = Steps(dve, steps)
                dve.memset(lr[DL:DL + 1, :], 1.0).then_inc(const, 1)
                grp = lambda ap: ap.rearrange("p (x y) -> p x y", x=D1)

                def mask(b):
                    lg = grp(g.ps[:, (b % 2) * CH:(b % 2 + 1) * CH])
                    dve.wait_ge(lgt, b + 1)
                    step(dve.tensor_reduce(mx[:, b % 2, :], lg, AX, ALU.max))
                    if b >= 2:
                        dve.wait_ge(tied, b - 1)
                    ins = dve.tensor_tensor(grp(eq[:, b % 2, :]), lg, mx[:, b % 2, :].unsqueeze(2).broadcast_to([P, D1, D2]), ALU.is_equal)
                    step(ins)
                    dve.nop().then_inc(hot, 1)
                    dve.nop().then_inc(eqd, 1)

                def pick(b):
                    dve.wait_ge(tied, b + 1)
                    p3 = grp(pr[:, b % 2, :])
                    step(dve.tensor_reduce(px[:, b % 2, :], p3, AX, ALU.max))
                    step(dve.tensor_tensor(grp(eq[:, b % 2, :]), p3, px[:, b % 2, :].unsqueeze(2).broadcast_to([P, D1, D2]), ALU.is_equal))
                    dve.wait_ge(up, b + 1)
                    if b >= 2:
                        dve.wait_ge(tr, b - 1)
                    dve.scalar_tensor_tensor(mid[:, b % 2, :], g.ps[:, (2 + b % 2) * CH:(3 + b % 2) * CH], 0.0, eq[:, b % 2, :],
                                             ALU.max, ALU.mult).then_inc(act_ready, 1)

                def finish(b):
                    dve.wait_ge(yps, b + 1)
                    dve.tensor_tensor(g.X[:, b, :], g.X[:, b, :], g.ps[:, (6 + b % 2) * CH:(6 + b % 2) * CH + C], ALU.add).then_inc(xad, 1)
                for b in range(TB + 3):
                    if b < TB:
                        mask(b)
                    if 1 <= b <= TB:
                        pick(b - 1)
                    if b == 3:
                        dve.wait_ge(xb, 1)
                    if b >= 3:
                        finish(b - 3)


def mamba(nc, g, I):
    DI, NS, KW, R = 256, 16, 4, 8
    HV = DI // P
    DIRS = ("f", "r")
    PADT = KW - 1
    NB = 2 * NS
    with ExitStack() as ctx:
        r = Room(nc, ctx, "l1a")
        win = r.sb("win", [C, 2 * DI])
        wout = r.sb("wout", [P, HV, C])
        cw = r.sb("cw", [P, 2, HV, KW])
        cb = r.sb("cb", [P, 2, HV])
        wx = r.sb("wx", [P, 2, HV, R + NB])
        wdt = r.sb("wdt", [R, 2, DI])
        bdt = r.sb("bdt", [P, 2, HV])
        Al = r.sb("A", [P, 2, HV, NS])
        Dp = r.sb("D", [P, 2, HV])
        xc = r.sb("xc", [P, 2, HV, T])
        dt = r.sb("dt", [P, 2, HV, T])
        dtx = r.sb("dtx", [P, 2, HV, T])
        bc = r.sb("bc", [3 * NB, 2, T], BF16)
        sel = r.sb("sel", [3 * NB, NB], BF16)

        def load(sp, s):
            n = 0

            def ld(dst, src):
                nonlocal n
                n += 1
                sp.dma_start(dst, src, allow_slow_non_contiguous=True).then_inc(s, 16)
            ld(win[:, :], I["L1_attn_in_proj_wT"])
            ld(wout[:, :, :], I["L1_attn_out_proj_wT"].rearrange("(h p) c -> p h c", p=P))
            for i, d in enumerate(DIRS):
                ld(cw[:, i, :, :], I[f"L1_attn_conv_w_{d}"].rearrange("(h p) k -> p h k", p=P))
                ld(cb[:, i, :], I[f"L1_attn_conv_b_{d}"].rearrange("(h p) -> p h", p=P))
                ld(wx[:, i, :, :], I[f"L1_attn_x_proj_w_{d}T"].rearrange("(h p) k -> p h k", p=P))
                ld(wdt[:, i, :], I[f"L1_attn_dt_proj_w_{d}T"])
                ld(bdt[:, i, :], I[f"L1_attn_dt_proj_b_{d}"].rearrange("(h p) -> p h", p=P))
                ld(Al[:, i, :, :], I[f"L1_attn_A_log_{d}"].rearrange("(h p) n -> p h n", p=P))
                ld(Dp[:, i, :], I[f"L1_attn_D_{d}"].rearrange("(h p) -> p h", p=P))
            return n
        layernorm_transpose(nc, g, "ln2", load)

        with ExitStack() as ctx1:
            r1 = Room(nc, ctx1, "l1p")
            xi = r1.sb("xi", [P, HV, PADT + T + PADT])
            v = r1.sb("v", [P, T])
            e = r1.sb("e", [P, T])
            u = r1.sb("u", [P, T])
            x3 = r1.sb("x3", [3 * NB, T])
            hi = r1.sb("hi", [3 * NB, T], BF16)
            mid = r1.sb("mid", [3 * NB, T], BF16)
            wx3 = r1.sb("wx3", [P, 2, HV, 3 * NB])
            xdt = r1.sb("xdt", [R, T])
            sidx = r1.sb("sidx", [3 * NB, NB])
            xps, xcp, ready, convd, sil = r1.sem("x_in_psum"), r1.sem("x_copied"), r1.sem("pads_ready"), r1.sem("conv_done"), r1.sem("silu_done")
            bcps, bccp, dtps, dtcp, vps, vcp = r1.sem("bc_in_psum"), r1.sem("bc_copied"), r1.sem("dt_in_psum"), r1.sem("dt_copied"), r1.sem("v_in_psum"), r1.sem("v_copied")
            ed, ud, ld_, steps, asteps, dtd, w3, sels = r1.sem("exp_done"), r1.sem("u_done"), r1.sem("ln_done"), r1.sem("steps"), r1.sem("act_steps"), r1.sem("dt_done"), r1.sem("wx3_ready"), r1.sem("sel_steps")
            tails, aready, splitd = r1.sem("v_read"), r1.sem("a_exp"), r1.sem("split_done")
            with nc.Block() as block:

                @block.gpsimd
                def _(pool):
                    pool.memset(sidx[:, :], 0.0).then_inc(sels, 1)
                    for k in range(3):
                        pool.wait_ge(sels, k + 1)
                        pool.affine_select(out=sidx[:, :], in_=sidx[:, :], compare_op=ALU.not_equal, fill=1.0, base=-k * NB,
                                           pattern=[[-1, NB]], channel_multiplier=1).then_inc(sels, 1)
                    pool.wait_ge(sels, 4)
                    pool.tensor_copy(sel[:, :], sidx[:, :]).then_inc(sels, 1)

                @block.tensor
                def _(pe):
                    for h in range(HV):
                        for q in range(NCH):
                            mm = pe.matmul(g.ps[:, h * T + q * CH:h * T + (q + 1) * CH], win[:, h * P:(h + 1) * P],
                                           g.hT[:, q * CH:(q + 1) * CH], start=True, stop=True)
                        mm.then_inc(xps, 1)
                    pe.wait_ge(w3, 1)
                    pe.wait_ge(xcp, 2)
                    for i in range(2):
                        pe.wait_ge(sil, 2 * (i + 1))
                        if i:
                            pe.wait_ge(vcp, 2)
                        for q in range(NCH):
                            for h in range(HV):
                                mm = pe.matmul(g.ps[0:3 * NB, q * CH:(q + 1) * CH], wx3[:, i, h, :], xc[:, i, h, q * CH:(q + 1) * CH],
                                               start=(h == 0), stop=(h == HV - 1))
                        mm.then_inc(bcps, 1)
                        for q in range(NCH):
                            for h in range(HV):
                                mm = pe.matmul(g.ps[0:R, T + q * CH:T + (q + 1) * CH], wx[:, i, h, 0:R], xc[:, i, h, q * CH:(q + 1) * CH],
                                               start=(h == 0), stop=(h == HV - 1))
                        mm.then_inc(dtps, 1)
                        pe.wait_ge(dtcp, i + 1)
                        pe.wait_ge(bccp, i + 1)
                        for h in range(HV):
                            for q in range(NCH):
                                mm = pe.matmul(g.ps[:, h * T + q * CH:h * T + (q + 1) * CH], wdt[:, i, h * P:(h + 1) * P],
                                               xdt[:, q * CH:(q + 1) * CH], start=True, stop=True)
                            mm.then_inc(vps, 1)

                @block.scalar
                def _(act):
                    act.activation(Al[:, :, :, :], Al[:, :, :, :], ACT.Exp).then_inc(aready, 1)
                    for h in range(HV):
                        act.wait_ge(xps, h + 1)
                        act.copy(xi[:, h, PADT:PADT + T], g.ps[:, h * T:(h + 1) * T]).then_inc(xcp, 1)
                    for n in range(2 * HV):
                        act.wait_ge(convd, n + 1)
                        act.activation(xc[:, n // HV, n % HV, :], xc[:, n // HV, n % HV, :], ACT.Silu).then_inc(sil, 1)
                    for i in range(2):
                        act.wait_ge(bcps, i + 1)
                        act.copy(x3[:, :], g.ps[0:3 * NB, 0:T]).then_inc(bccp, 1)
                        act.wait_ge(dtps, i + 1)
                        act.copy(xdt[:, :], g.ps[0:R, T:2 * T]).then_inc(dtcp, 1)
                        for h in range(HV):
                            n = HV * i + h
                            act.wait_ge(vps, n + 1)
                            if n:
                                act.wait_ge(dtd, n)
                            act.activation(v[:, :], g.ps[:, h * T:(h + 1) * T], ACT.Identity, bias=bdt[:, i, h:h + 1]).then_inc(asteps, 1)
                            act.activation(e[:, :], g.ps[:, h * T:(h + 1) * T], ACT.Abs, bias=bdt[:, i, h:h + 1]).then_inc(vcp, 1)
                            act.wait_ge(vcp, n + 1)
                            act.activation(e[:, :], e[:, :], ACT.Exp, scale=-1.0).then_inc(ed, 1)
                            act.wait_ge(ud, n + 1)
                            act.activation(dt[:, i, h, :], u[:, :], ACT.Ln).then_inc(ld_, 1)

                @block.vector
                def _(dve):
                    step = Steps(dve, steps)
                    dve.memset(xi[:, :, 0:PADT], 0.0)
                    step(dve.memset(xi[:, :, PADT + T:], 0.0))
                    dve.wait_ge(aready, 1)
                    step(dve.tensor_scalar(Al[:, :, :, :], Al[:, :, :, :], -1.0, None, ALU.mult))
                    for k in range(3):
                        last = dve.tensor_copy(wx3[:, :, :, k * NB:(k + 1) * NB], wx[:, :, :, R:R + NB])
                    last.then_inc(w3, 1)
                    for n in range(2 * HV):
                        i, h = divmod(n, HV)
                        dve.wait_ge(xcp, h + 1)
                        at = [(k if i == 0 else 2 * PADT - k) for k in range(KW)]
                        step(dve.tensor_scalar(xc[:, i, h, :], xi[:, h, at[0]:at[0] + T], cw[:, i, h, 0:1], cb[:, i, h:h + 1], ALU.mult, ALU.add))
                        for k in range(1, KW):
                            ins = dve.scalar_tensor_tensor(xc[:, i, h, :], xi[:, h, at[k]:at[k] + T], cw[:, i, h, k:k + 1], xc[:, i, h, :],
                                                           ALU.mult, ALU.add)
                            if k < KW - 1:
                                step(ins)
                        ins.then_inc(convd, 1)
                    for i in range(2):
                        dve.wait_ge(bccp, i + 1)
                        step(dve.tensor_copy(hi[:, :], x3[:, :]))
                        step(dve.tensor_tensor(x3[:, :], x3[:, :], hi[:, :], ALU.subtract))
                        step(dve.tensor_copy(mid[:, :], x3[:, :]))
                        dve.tensor_copy(bc[0:NB, i, :], hi[0:NB, :])
                        dve.tensor_copy(bc[NB:2 * NB, i, :], mid[NB:2 * NB, :])
                        step(dve.tensor_tensor(x3[:, :], x3[:, :], mid[:, :], ALU.subtract))
                        dve.tensor_copy(bc[2 * NB:3 * NB, i, :], x3[2 * NB:3 * NB, :]).then_inc(splitd, 1)
                        dve.wait_ge(splitd, i + 1)
                        for h in range(HV):
                            n = HV * i + h
                            dve.wait_ge(ed, n + 1)
                            dve.tensor_scalar(u[:, :], e[:, :], 1.0, None, ALU.add).then_inc(ud, 1)
                            dve.wait_ge(ud, n + 1)
                            dve.wait_ge(ld_, n + 1)
                            step(dve.scalar_tensor_tensor(u[:, :], u[:, :], 1.0, e[:, :], ALU.subtract, ALU.subtract))
                            step(dve.tensor_tensor(dt[:, i, h, :], dt[:, i, h, :], u[:, :], ALU.subtract))
                            dve.wait_ge(asteps, n + 1)
                            step(dve.scalar_tensor_tensor(dt[:, i, h, :], v[:, :], 0.0, dt[:, i, h, :], ALU.max, ALU.add))
                            dve.tensor_tensor(dtx[:, i, h, :], dt[:, i, h, :], xc[:, i, h, :], ALU.mult).then_inc(dtd, 1)

        steps_ = [(h, i, n) for h in range(HV) for i in range(2) for n in range(NS)]
        M = len(steps_)
        U = r.sb("U", [P, HV, T])
        with ExitStack() as ctx2:
            r2 = Room(nc, ctx2, "l1s")
            dA = r2.sb("dA", [P, 2, T])
            Bs = r2.sb("Bs", [P, 2, T])
            hb = r2.sb("h", [P, 2, T])
            hc = r2.sb("hc", [P, 2, T])
            dad, bps, bcp, dbx, scd = r2.sem("dA_done"), r2.sem("b_in_psum"), r2.sem("b_copied"), r2.sem("dbx_done"), r2.sem("scan_done")
            cps, hcd, accd, ud, s1 = r2.sem("c_in_psum"), r2.sem("hc_done"), r2.sem("accumulated"), r2.sem("u_read"), r2.sem("steps")
            with nc.Block() as block:

                @block.tensor
                def _(pe):
                    def spread(bank, sem, row, i, q):
                        pe.matmul(g.ps[:, bank * CH:(bank + 1) * CH], sel[:, row:row + 1].broadcast_to([3 * NB, P]),
                                  bc[:, i, q * CH:(q + 1) * CH], start=True, stop=True).then_inc(sem, 1)

                    def put_b(m):
                        h, i, n = steps_[m]
                        for q in range(NCH):
                            k = m * NCH + q
                            if k >= 2:
                                pe.wait_ge(bcp, k - 1)
                            spread(4 + k % 2, bps, n, i, q)

                    def put_c(m, q):
                        h, i, n = steps_[m]
                        k = m * NCH + q
                        if k >= 2:
                            pe.wait_ge(hcd, k - 1)
                        spread(6 + k % 2, cps, NS + n, i, q)

                    def add(m):
                        h, i, n = steps_[m]
                        for q in range(NCH):
                            pe.wait_ge(hcd, m * NCH + q + 1)
                            first, last = (i, n) == (0, 0), (i, n) == (1, NS - 1)
                            if first and h:
                                pe.wait_ge(ud, h)
                            mm = pe.matmul(g.ps[:, q * CH:(q + 1) * CH], g.ident[:, :], hc[:, m % 2, q * CH:(q + 1) * CH],
                                           start=first, stop=last)
                        mm.then_inc(accd, 1)
                    put_b(0)
                    for m in range(M):
                        put_c(m, 0)
                        put_c(m, 1)
                        if m + 1 < M:
                            put_b(m + 1)
                        if m:
                            add(m - 1)
                        put_c(m, 2)
                        put_c(m, 3)
                    add(M - 1)

                @block.scalar
                def _(act):
                    for m, (h, i, n) in enumerate(steps_):
                        if m >= 2:
                            act.wait_ge(dbx, m - 1)
                        for q in range(NCH):
                            act.wait_ge(bps, m * NCH + q + 1)
                            act.copy(Bs[:, m % 2, q * CH:(q + 1) * CH], g.ps[:, (4 + q % 2) * CH:(5 + q % 2) * CH]).then_inc(bcp, 1)
                        if m >= 2:
                            act.wait_ge(scd, m - 1)
                        act.activation(dA[:, m % 2, :], dt[:, i, h, :], ACT.Exp, scale=Al[:, i, h, n:n + 1]).then_inc(dad, 1)

                @block.gpsimd
                def _(pool):
                    for m, (h, i, n) in enumerate(steps_):
                        pool.wait_ge(bcp, NCH * (m + 1))
                        if m >= 2:
                            pool.wait_ge(hcd, NCH * (m - 1))
                        pool.tensor_tensor(hb[:, m % 2, :], dtx[:, i, h, :], Bs[:, m % 2, :], ALU.mult).then_inc(dbx, 1)

                @block.vector
                def _(dve):
                    step = Steps(dve, s1)

                    def half_sum(h):
                        dve.wait_ge(accd, 2 * NS * (h + 1))
                        step(dve.scalar_tensor_tensor(U[:, h, :], xc[:, 0, h, :], Dp[:, 0, h:h + 1], g.ps[:, 0:T], ALU.mult, ALU.add))
                        dve.nop().then_inc(ud, 1)
                        step(dve.scalar_tensor_tensor(U[:, h, :], xc[:, 1, h, :], Dp[:, 1, h:h + 1], U[:, h, :], ALU.mult, ALU.add))
                    for m, (h, i, n) in enumerate(steps_):
                        dve.wait_ge(dbx, m + 1)
                        dve.wait_ge(dad, m + 1)
                        view = slice(None, None, -1) if i else slice(None)
                        dve.tensor_tensor_scan(hb[:, m % 2, view], dA[:, m % 2, view], hb[:, m % 2, view], 0.0, ALU.mult, ALU.add).then_inc(scd, 1)
                        dve.wait_ge(scd, m + 1)
                        if m >= 2:
                            dve.wait_ge(accd, m - 1)
                        for q in range(NCH):
                            k = m * NCH + q
                            dve.wait_ge(cps, k + 1)
                            dve.tensor_tensor(hc[:, m % 2, q * CH:(q + 1) * CH], hb[:, m % 2, q * CH:(q + 1) * CH],
                                              g.ps[:, (6 + k % 2) * CH:(7 + k % 2) * CH], ALU.mult).then_inc(hcd, 1)
                        if m == 2 * NS + 1 - 1:
                            half_sum(0)
                    half_sum(1)
        with ExitStack() as ctx3:
            r3 = Room(nc, ctx3, "l1o")
            sz = r3.sb("sz", [P, HV, T])
            zps, szd, gd, yps, xad = r3.sem("z_in_psum"), r3.sem("silu_done"), r3.sem("gated"), r3.sem("y_in_psum"), r3.sem("x_added")
            with nc.Block() as block:

                @block.tensor
                def _(pe):
                    for h in range(HV):
                        for q in range(NCH):
                            pe.matmul(g.ps[:, h * T + q * CH:h * T + (q + 1) * CH], win[:, DI + h * P:DI + (h + 1) * P],
                                      g.hT[:, q * CH:(q + 1) * CH], start=True, stop=True).then_inc(zps, 1)
                    for b in range(TB):
                        pe.wait_ge(gd, HV * NCH)
                        pe.wait_ge(szd, HV * NCH)
                        if b >= 2:
                            pe.wait_ge(xad, b - 1)
                        for h in range(HV):
                            mm = pe.matmul(g.ps[:, (b % 2) * CH:(b % 2) * CH + C], U[:, h, b * P:(b + 1) * P], wout[:, h, :],
                                           start=(h == 0), stop=(h == HV - 1))
                        mm.then_inc(yps, 1)

                @block.scalar
                def _(act):
                    for n in range(HV * NCH):
                        act.wait_ge(zps, n + 1)
                        h, q = divmod(n, NCH)
                        act.activation(sz[:, h, q * CH:(q + 1) * CH], g.ps[:, n * CH:(n + 1) * CH], ACT.Silu).then_inc(szd, 1)

                @block.vector
                def _(dve):
                    for n in range(HV * NCH):
                        h, q = divmod(n, NCH)
                        dve.wait_ge(szd, n + 1)
                        dve.tensor_tensor(U[:, h, q * CH:(q + 1) * CH], U[:, h, q * CH:(q + 1) * CH], sz[:, h, q * CH:(q + 1) * CH],
                                          ALU.mult).then_inc(gd, 1)
                    for b in range(TB):
                        dve.wait_ge(yps, b + 1)
                        dve.tensor_tensor(g.X[:, b, :], g.X[:, b, :], g.ps[:, (b % 2) * CH:(b % 2) * CH + C], ALU.add).then_inc(xad, 1)


def gated_experts(nc, g, I):
    E = 8
    with ExitStack() as ctx:
        r = Room(nc, ctx, "l1f")
        wg = r.sb("wg", [C, C])
        bg = r.sb("bg", [P, C])
        we = r.sb("we", [C, E, C])
        be = r.sb("be", [E, C])
        pri = r.sb("pri", [P, C])

        def load(sp, s):
            sp.dma_start(wg[:, :], I["L1_ffn_Wg"]).then_inc(s, 16)
            sp.dma_start(bg[:, :], I["L1_ffn_bg"].rearrange("(a c) -> a c", a=1).broadcast_to([P, C])).then_inc(s, 16)
            sp.dma_start(we[:, :, :], I["L1_ffn_We"].rearrange("e d f -> d e f")).then_inc(s, 16)
            sp.dma_start(be[:, :], I["L1_ffn_be"]).then_inc(s, 16)
            return 4
        layernorm_transpose(nc, g, "ln3", load)
        lg = r.sb("lg", [P, TB, C])
        ex = r.sb("ex", [P, TB, C])
        eq = r.sb("eq", [P, TB, C])
        mx = r.sb("mx", [P, TB])
        pr = r.sb("prob", [P, TB])
        px = r.sb("px", [P, TB])
        oh = r.sb("oh", [P, TB, E])
        ohT = r.sb("ohT", [E, TB, P])
        acc = r.sb("acc", [P, 2, C])
        const, steps, lps, sub, expd, hot = r.sem("const_ready"), r.sem("steps"), r.sem("logits_in_psum"), r.sem("max_subtracted"), r.sem("exp_done"), r.sem("expert_known")
        otr, ocp, zps, zrd, bps, bcp = r.sem("onehot_transposed"), r.sem("onehot_copied"), r.sem("z_in_psum"), r.sem("z_read"), r.sem("bias_in_psum"), r.sem("bias_copied")
        xad = r.sem("x_added")
        with nc.Block() as block:

            @block.gpsimd
            def _(pool):
                pool.iota(pri[:, :], [[-1, C]], base=C, channel_multiplier=0, allow_small_or_imprecise_dtypes=True).then_inc(const, 1)

            @block.tensor
            def _(pe):
                for b in range(TB):
                    mm = pe.matmul(g.ps[:, b * P:(b + 1) * P], g.hT[:, b * P:(b + 1) * P], wg[:, :], start=True, stop=True)
                    if b % 4 == 3:
                        mm.then_inc(lps, 1)
                pe.wait_ge(hot, 1)
                for b in range(TB):
                    mm = pe.transpose(g.ps[0:E, T + b * P:T + (b + 1) * P], oh[:, b, :], g.ident[:, :])
                mm.then_inc(otr, 1)
                pe.wait_ge(ocp, 1)
                for b in range(TB):
                    o = (b % 2) * 2 * CH
                    if b >= 2:
                        pe.wait_ge(zrd, b - 1)
                        pe.wait_ge(bcp, b - 1)
                    pe.matmul(g.ps[:, (4 + b % 2) * CH:(4 + b % 2) * CH + C], ohT[:, b, :], be[:, :], start=True, stop=True).then_inc(bps, 1)
                    for k in range(2):
                        mm = pe.matmul(g.ps[:, o + k * CH:o + (k + 1) * CH], g.hT[:, b * P:(b + 1) * P],
                                       we[:, 4 * k:4 * k + 4, :].rearrange("d e f -> d (e f)"), start=True, stop=True)
                    mm.then_inc(zps, 1)

            @block.scalar
            def _(act):
                act.wait_ge(sub, 1)
                act.activation(ex[:, :, :], lg[:, :, :], ACT.Exp).then_inc(expd, 1)
                act.wait_ge(otr, 1)
                act.copy(ohT[:, :, :].rearrange("e b t -> e (b t)"), g.ps[0:E, T:2 * T]).then_inc(ocp, 1)
                for b in range(TB):
                    act.wait_ge(bps, b + 1)
                    if b >= 2:
                        act.wait_ge(xad, b - 1)
                    act.copy(acc[:, b % 2, :], g.ps[:, (4 + b % 2) * CH:(4 + b % 2) * CH + C]).then_inc(bcp, 1)

            @block.vector
            def _(dve):
                step = Steps(dve, steps)
                for q in range(NCH):
                    dve.wait_ge(lps, q + 1)
                    last = dve.tensor_tensor(lg[:, 4 * q:4 * q + 4, :], g.ps[:, q * CH:(q + 1) * CH].rearrange("p (b c) -> p b c", c=C),
                                             bg[:, :].unsqueeze(1).broadcast_to([P, 4, C]), ALU.add)
                step(last)
                bc = lambda v: v.unsqueeze(2).broadcast_to([P, TB, C])
                step(dve.tensor_reduce(mx[:, :], lg[:, :, :], AX, ALU.max))
                step(dve.tensor_tensor(eq[:, :, :], lg[:, :, :], bc(mx[:, :]), ALU.is_equal))
                dve.tensor_tensor(lg[:, :, :], lg[:, :, :], bc(mx[:, :]), ALU.subtract).then_inc(sub, 1)
                dve.wait_ge(const, 1)
                step(dve.tensor_tensor(eq[:, :, :], eq[:, :, :], pri[:, :].unsqueeze(1).broadcast_to([P, TB, C]), ALU.mult))
                step(dve.tensor_reduce(px[:, :], eq[:, :, :], AX, ALU.max))
                step(dve.tensor_tensor(eq[:, :, :], eq[:, :, :], bc(px[:, :]), ALU.is_equal))
                dve.tensor_reduce(oh[:, :, :], eq[:, :, :].rearrange("p b (a e) -> p b e a", e=E), AX, ALU.add).then_inc(hot, 1)
                dve.wait_ge(expd, 1)
                step(dve.tensor_reduce(pr[:, :], ex[:, :, :], AX, ALU.add))
                step(dve.reciprocal(pr[:, :], pr[:, :]))
                for b in range(TB):
                    o = (b % 2) * 2 * CH
                    dve.wait_ge(zps, b + 1)
                    dve.wait_ge(bcp, b + 1)
                    for e in range(E):
                        ins = dve.scalar_tensor_tensor(acc[:, b % 2, :], g.ps[:, o + e * C:o + (e + 1) * C], oh[:, b, e:e + 1],
                                                       acc[:, b % 2, :], ALU.mult, ALU.add)
                        step(ins)
                    dve.nop().then_inc(zrd, 1)
                    step(dve.tensor_scalar(acc[:, b % 2, :], acc[:, b % 2, :], 0.0, pr[:, b:b + 1], ALU.max, ALU.mult))
                    dve.tensor_tensor(g.X[:, b, :], g.X[:, b, :], acc[:, b % 2, :], ALU.add).then_inc(xad, 1)


def head_attention(nc, g, tag, wqkv, bias, q_scale, k_scale, out_scale, O):
    BOUND = 40.0
    NH, HS = 16, 8
    PR = 9 * HS
    KR = PR + 3
    G4 = NH // 4
    QC = 1024
    with ExitStack() as ctx:
        r = Room(nc, ctx, tag)
        Qs = r.sb("Qs", [KR, NH, T], BF16)
        Ks = r.sb("Ks", [KR, NH, T], BF16)
        Va = r.sb("Va", [P, TB, NH, HS + 1])
        parts = nc.dram_tensor(f"{tag}_parts", [2, 3, P, T], BF16, kind="Internal").ap()
        ctxg = ctx.enter_context(ExitStack())
        rg = Room(nc, ctxg, tag + "g")
        mT = rg.sb("guard", [NH, T])
        over = rg.sb("over", [1, 1], I32)
        mparts = nc.dram_tensor(f"{tag}_mparts", [3, NH, T], BF16, kind="Internal").ap()
        with ExitStack() as ctx1:
            r1 = Room(nc, ctx1, tag + "p")
            f32 = r1.sb("f32", [P, 2, T])
            pt = r1.sb("pt", [P, 2, 3, CH], BF16)
            onesb = r1.sb("onesb", [3, T], BF16)
            sq = r1.sb("squares", [P, T])
            sel = r1.sb("head_of_row", [P, NH])
            kmax = r1.sb("kmax", [NH, 2])
            umax = r1.sb("umax", [1, NH + 1])
            qps, qcp, steps, split, stored = r1.sem("qk_in_psum"), r1.sem("qk_copied"), r1.sem("steps"), r1.sem("split"), [r1.sem("parts_stored0"), r1.sem("parts_stored1")]
            vps, vcp, onesd, stacked = r1.sem("v_in_psum"), r1.sem("v_copied"), r1.sem("ones_ready"), r1.sem("stacked")
            squared, selr, nps, kmd, und, ups = r1.sem("squared"), r1.sem("head_rows"), r1.sem("norms_in_psum"), r1.sem("kmax_done"), r1.sem("guard_done"), r1.sem("guards_in_row")
            with nc.Block() as block:

                @block.gpsimd
                def _(pool):
                    pool.memset(sel[:, :], 1.0).then_inc(selr, 1)
                    pool.wait_ge(selr, 1)
                    pool.affine_select(out=sel[:, :], in_=sel[:, :], compare_op=ALU.is_ge, fill=0.0, base=0, pattern=[[-HS, NH]],
                                       channel_multiplier=1).then_inc(selr, 1)
                    pool.wait_ge(selr, 2)
                    pool.affine_select(out=sel[:, :], in_=sel[:, :], compare_op=ALU.is_ge, fill=0.0, base=HS - 1, pattern=[[HS, NH]],
                                       channel_multiplier=-1).then_inc(selr, 1)

                @block.tensor
                def _(pe):
                    for i in range(2):
                        for q in range(NCH):
                            mm = pe.matmul(g.ps[:, i * T + q * CH:i * T + (q + 1) * CH], wqkv[:, i, :], g.hT[:, q * CH:(q + 1) * CH],
                                           start=True, stop=True)
                        mm.then_inc(qps, 1)
                    pe.wait_ge(selr, 3)
                    for i in (1, 2):
                        pe.wait_ge(squared, i)
                        if i == 2:
                            pe.wait_ge(kmd, 1)
                        for q in range(NCH):
                            mm = pe.matmul(g.ps[0:NH, T + q * CH:T + (q + 1) * CH], sel[:, :], sq[:, q * CH:(q + 1) * CH], start=True, stop=True)
                        mm.then_inc(nps, 1)
                    for b in range(TB):
                        mm = pe.matmul(g.ps[:, b * P:(b + 1) * P], g.hT[:, b * P:(b + 1) * P], wqkv[:, 2, :], start=True, stop=True)
                    mm.then_inc(vps, 1)
                    pe.wait_ge(und, 2)
                    pe.matmul(g.ps[0:1, T:T + NH], kmax[:, 1:2], g.ident[0:NH, 0:NH], start=True, stop=True).then_inc(ups, 1)

                @block.scalar
                def _(act):
                    for i, s in enumerate((q_scale, k_scale)):
                        act.wait_ge(qps, i + 1)
                        b = 0.0 if bias is None else bias[i]
                        act.activation(f32[:, i, :], g.ps[:, i * T:(i + 1) * T], ACT.Identity, bias=b, scale=s).then_inc(qcp, 1)
                    for n, (i, s) in enumerate(((1, k_scale), (0, q_scale))):
                        if n:
                            act.wait_ge(nps, 1)
                        b = 0.0 if bias is None else bias[i]
                        act.activation(sq[:, :], g.ps[:, i * T:(i + 1) * T], ACT.Square, bias=b, scale=s).then_inc(squared, 1)
                    act.wait_ge(nps, 2)
                    act.activation(mT[:, :], g.ps[0:NH, T:2 * T], ACT.Sqrt, scale=kmax[:, 0:1]).then_inc(und, 1)

                @block.vector
                def _(dve):
                    step = Steps(dve, steps)
                    dve.memset(onesb[:, :], 1.0).then_inc(onesd, 1)
                    step(dve.memset(Va[:, :, :, :], 1.0))
                    for i in range(2):
                        dve.wait_ge(qcp, i + 1)
                        for q in range(NCH):
                            cols = slice(q * CH, (q + 1) * CH)
                            m = i * NCH + q
                            if m >= 2:
                                dve.wait_ge(stored[m % 2], 16 * 3 * (m // 2))
                            for p_ in range(3):
                                step(dve.tensor_copy(pt[:, m % 2, p_, :], f32[:, i, cols]))
                                if p_ < 2:
                                    step(dve.tensor_tensor(f32[:, i, cols], f32[:, i, cols], pt[:, m % 2, p_, :], ALU.subtract))
                            dve.nop().then_inc(split, 1)
                        if i == 0:
                            dve.wait_ge(nps, 1)
                            dve.tensor_reduce(kmax[:, 0:1], g.ps[0:NH, T:2 * T], AX, ALU.max).then_inc(kmd, 1)
                    dve.wait_ge(und, 1)
                    step(dve.tensor_reduce(kmax[:, 1:2], mT[:, :], AX, ALU.max))
                    dve.tensor_scalar(mT[:, :], mT[:, :], -1.0, None, ALU.mult).then_inc(und, 1)
                    dve.wait_ge(ups, 1)
                    step(dve.tensor_reduce(umax[:, NH:NH + 1], g.ps[0:1, T:T + NH], AX, ALU.max))
                    dve.tensor_scalar(over[:, :], umax[:, NH:NH + 1], BOUND, None, ALU.is_gt)
                    dve.wait_ge(vps, 1)
                    vsrc = g.ps[:, 0:T].rearrange("p (b h e) -> p (b h) e", b=TB, e=HS)
                    vdst = Va[:, :, :, 0:HS].rearrange("p b h e -> p (b h) e")
                    if bias is None:
                        dve.tensor_copy(vdst, vsrc).then_inc(vcp, 1)
                    else:
                        for b in range(TB):
                            ins = dve.tensor_tensor(Va[:, b, :, 0:HS], g.ps[:, b * P:(b + 1) * P].rearrange("p (h e) -> p h e", e=HS),
                                                    bias[2].rearrange("p (h e) -> p h e", e=HS), ALU.add)
                        ins.then_inc(vcp, 1)

                @block.sync
                def _(sp):
                    for i in range(2):
                        for q in range(NCH):
                            m = i * NCH + q
                            sp.wait_ge(split, m + 1)
                            for p_ in range(3):
                                sp.dma_start(parts[i, p_, :, q * CH:(q + 1) * CH], pt[:, m % 2, p_, :]).then_inc(stored[m % 2], 16)
                    sp.wait_ge(stored[0], 16 * 3 * NCH)
                    sp.wait_ge(stored[1], 16 * 3 * NCH)
                    for a in range(3):
                        for b in range(3):
                            rows = slice((3 * a + b) * HS, (3 * a + b + 1) * HS)
                            sp.dma_start(Qs[rows, :, :], parts[0, a].rearrange("(h e) t -> e h t", e=HS)).then_inc(stacked, 16)
                            sp.dma_start(Ks[rows, :, :], parts[1, b].rearrange("(h e) t -> e h t", e=HS)).then_inc(stacked, 16)
                    sp.wait_ge(onesd, 1)
                    sp.dma_start(Ks[PR:KR, :, :], onesb[:, :].unsqueeze(1).broadcast_to([3, NH, T])).then_inc(stacked, 16)
                    sp.wait_ge(stacked, 16 * 19)
        with ExitStack() as ctx2:
            r2 = Room(nc, ctx2, tag + "m")
            mx = r2.sb("mx", [P, NH, TB])
            mp = r2.sb("mp", [NH, 3, T], BF16)
            sps, mxd, tr, steps, split, mst = r2.sem("scores_in_psum"), r2.sem("max_done"), r2.sem("max_transposed"), r2.sem("steps"), r2.sem("split"), r2.sem("max_stored")
            mstk = r2.sem("max_stacked")
            with nc.Block() as block:

                @block.tensor
                def _(pe):
                    flag = pe.value_load(over[0:1, 0:1], min_val=0, max_val=1)
                    with pe.If(flag > 0):
                        for h in range(NH):
                            with pe.Fori(0, TB // 2) as j:
                                for k in range(2):
                                    pe.wait_ge(mxd, j * 2 + (h * TB + k + 1))
                                    for q in range(NCH):
                                        mm = pe.matmul(g.ps[:, k * T + q * CH:k * T + (q + 1) * CH], Qs[0:PR, h, bass.ds(j * 2 * P + k * P, P)],
                                                       Ks[0:PR, h, q * CH:(q + 1) * CH], start=True, stop=True)
                                    mm.then_inc(sps, 1)
                        pe.wait_ge(mxd, NH * TB + 2)
                        for b in range(TB):
                            mm = pe.transpose(g.ps[0:NH, b * P:(b + 1) * P], mx[:, :, b], g.ident[:, :])
                        mm.then_inc(tr, 1)

                @block.vector
                def _(dve):
                    flag = dve.value_load(over[0:1, 0:1], min_val=0, max_val=1)
                    with dve.If(flag > 0):
                        dve.sem_inc(mxd, 2)
                        for h in range(NH):
                            with dve.Fori(0, TB // 2) as j:
                                for k in range(2):
                                    dve.wait_ge(sps, j * 2 + (h * TB + k + 1))
                                    dve.tensor_reduce(mx[:, h, bass.ds(j * 2 + k, 1)], g.ps[:, k * T:(k + 1) * T], AX, ALU.max, negate=True).then_inc(mxd, 1)
                        dve.wait_ge(tr, 1)
                        dve.tensor_copy(mT[:, :], g.ps[0:NH, 0:T])
            with nc.Block() as block:

                @block.vector
                def _(dve):
                    step = Steps(dve, steps)
                    for p_ in range(3):
                        step(dve.tensor_copy(mp[:, p_, :], mT[:, :]))
                        if p_ < 2:
                            step(dve.tensor_tensor(mT[:, :], mT[:, :], mp[:, p_, :], ALU.subtract))
                    dve.nop().then_inc(split, 1)

                @block.sync
                def _(sp):
                    sp.wait_ge(split, 1)
                    for p_ in range(3):
                        sp.dma_start(mparts[p_], mp[:, p_, :]).then_inc(mst, 16)
                    sp.wait_ge(mst, 48)
                    sp.dma_start(Qs[PR:KR, :, :], mparts).then_inc(mstk, 16)
                    sp.wait_ge(mstk, 16)
        ctxg.close()
        with ExitStack() as ctx3:
            r3 = Room(nc, ctx3, tag + "e")
            NPT, NST = 8, 3
            pT = r3.sb("pT", [P, NPT, QC])
            oT = r3.sb("oT", [P, T])
            rc = r3.sb("rc", [P, TB, 4])
            sps, expd, pvd, accr = r3.sem("scores_in_psum"), r3.sem("exp_done"), r3.sem("pv_done"), r3.sem("acc_read")
            otr, ord_, steps, azero = r3.sem("o_transposed"), r3.sem("o_read"), r3.sem("steps"), r3.sem("acc_zeroed")
            ACC = NST * QC
            SEG = TB * 4
            NQ = T // QC
            with nc.Block() as block:

                @block.tensor
                def _(pe):
                    pe.wait_ge(azero, 1)
                    for hg in range(G4):
                        def segment(qc):
                            base = hg * NQ * SEG

                            def scores(kt):
                                for j in range(4):
                                    n = kt * 4 + j
                                    slot = n % NST if SEG % NST == 0 else None
                                    slot = (n + 0) % NST
                                    pe.wait_ge(expd, qc * SEG + (base + n + 1))
                                    for c in range(QC // CH):
                                        mm = pe.matmul(g.ps[:, slot * QC + c * CH:slot * QC + (c + 1) * CH],
                                                       Ks[:, hg * 4 + j, kt * P:(kt + 1) * P],
                                                       Qs[:, hg * 4 + j, bass.ds(qc * QC + c * CH, CH)], start=True, stop=True)
                                    mm.then_inc(sps, 1)

                            def values(kt):
                                pe.wait_ge(expd, qc * SEG + (base + 4 * kt + 4 + NST))
                                if kt == 0:
                                    pe.wait_ge(accr, qc + (hg * NQ + 1))
                                for c in range(QC // CH):
                                    for j in range(4):
                                        mm = pe.matmul(g.ps[32 * j:32 * j + HS + 1, ACC + c * CH:ACC + (c + 1) * CH],
                                                       Va[:, kt, hg * 4 + j, :], pT[:, (4 * kt + j) % NPT, c * CH:(c + 1) * CH],
                                                       start=(kt == 0), stop=(kt == TB - 1))
                                mm.then_inc(pvd, 1)
                            scores(0)
                            for kt in range(TB):
                                if kt + 1 < TB:
                                    scores(kt + 1)
                                values(kt)
                        with pe.Fori(0, NQ) as qc:
                            segment(qc)
                        pe.wait_ge(expd, (hg + 1) * NQ * SEG + NST)
                        pe.wait_ge(accr, (hg + 1) * NQ + 1)
                        for b in range(TB):
                            mm = pe.transpose(g.ps[:, b * P:(b + 1) * P], oT[:, b * P:(b + 1) * P], g.ident[:, :])
                        mm.then_inc(otr, 1)
                        pe.wait_ge(ord_, hg + 1)

                @block.scalar
                def _(act):
                    act.sem_inc(expd, NST)
                    for hg in range(G4):
                        with act.Fori(0, NQ) as qc:
                            base = hg * NQ * SEG
                            for n in range(SEG):
                                act.wait_ge(sps, qc * SEG + (base + n + 1))
                                act.wait_ge(pvd, qc * TB + (hg * NQ * TB + n // 4 + 1))
                                act.activation(pT[:, n % NPT, :], g.ps[:, (n % NST) * QC:(n % NST + 1) * QC], ACT.Exp).then_inc(expd, 1)

                @block.vector
                def _(dve):
                    step = Steps(dve, steps)
                    dve.memset(g.ps[:, ACC:ACC + QC], 0.0).then_inc(azero, 1)
                    dve.sem_inc(accr, 1)
                    dve.sem_inc(pvd, NPT // 4)
                    for hg in range(G4):
                        for qc in range(NQ):
                            dve.wait_ge(pvd, (hg * NQ + qc + 1) * TB + NPT // 4)
                            if hg and qc == 0:
                                dve.wait_ge(otr, hg)
                            dve.tensor_copy(oT[:, qc * QC:(qc + 1) * QC], g.ps[:, ACC:ACC + QC]).then_inc(accr, 1)
                        dve.wait_ge(otr, hg + 1)
                        o = g.ps[:, 0:T].rearrange("p (b j e) -> p b j e", b=TB, e=32)
                        step(dve.reciprocal(rc[:, :, :], o[:, :, :, HS]))
                        for j in range(4):
                            h = hg * 4 + j
                            ins = dve.scalar_tensor_tensor(O[:, :, h * HS:(h + 1) * HS], o[:, :, j, 0:HS], out_scale,
                                                           rc[:, :, j].unsqueeze(2).broadcast_to([P, TB, HS]), ALU.mult, ALU.mult)
                        step(ins)
                        dve.nop().then_inc(ord_, 1)


def transpose_blocks(pe, g, src, first, sem):
    for b in range(TB):
        mm = pe.transpose(g.ps[:, first + b * P:first + (b + 1) * P], src[:, b, :], g.ident[:, :])
    mm.then_inc(sem, 1)


def find_cut(nc, g, E, kk, Z, var, cut, need, general):
    ITERS, A = 6, TB // 2
    AIM = kk - 4.4
    SPREAD = 90.0
    with ExitStack() as ctx:
        r = Room(nc, ctx, "cut")
        at = r.sb("at", [P, 2, TB])
        lo = r.sb("lo", [P, 2, TB])
        hi = r.sb("hi", [P, 2, TB])
        w = r.sb("width", [P, 2, TB])
        d = r.sb("move", [P, 2, TB])
        sd = r.sb("std", [P, TB])
        nt = r.sb("minus_at", [P, TB])
        u = r.sb("up", [P, TB])
        v = r.sb("down", [P, TB])
        ok = r.sb("ok", [P, TB])
        okr = r.sb("row_ok", [P, 1])
        junk = r.sb("junk", [P, 2, T], BF16)
        junka = r.sb("junk_act", [P, 2, T], BF16)
        steps, sdr, probe, counted, okd, okps = r.sem("steps"), r.sem("std_ready"), r.sem("probe_ready"), r.sem("act_counted"), r.sem("rows_ok"), r.sem("ok_in_psum")
        with nc.Block() as block:

            @block.scalar
            def _(act):
                act.activation(sd[:, :], var, ACT.Sqrt).then_inc(sdr, 1)
                with act.Fori(0, ITERS) as i:
                    for b in range(A, TB):
                        if b == A:
                            act.wait_ge(probe, i + 1)
                        if b >= A + 2:
                            act.wait_ge(counted, i * A + (b - A - 1))
                        act.activation(junka[:, b % 2, :], E[:, b, :], ACT.Sign, bias=nt[:, b:b + 1], accum_out=at[:, 1, b:b + 1]).then_inc(counted, 1)
                    act.wait_ge(counted, i * A + A)

            @block.vector
            def _(dve):
                step = Steps(dve, steps)
                dve.wait_ge(sdr, 1)
                step(dve.tensor_scalar(at[:, 0, :], Z[:, :], 1.0 / T, None, ALU.mult))
                step(dve.scalar_tensor_tensor(at[:, 0, :], sd[:, :], 0.8416, at[:, 0, :], ALU.mult, ALU.add))
                delta = SPREAD / (T * 0.28)
                dve.scalar_tensor_tensor(lo[:, 0, :], sd[:, :], -delta, at[:, 0, :], ALU.mult, ALU.add)
                dve.scalar_tensor_tensor(hi[:, 0, :], sd[:, :], delta, at[:, 0, :], ALU.mult, ALU.add)
                dve.memset(cut[:, :], 0.0)
                dve.memset(need[:, :], 0.0)
                dve.memset(lo[:, 1, :], AIM + SPREAD)
                step(dve.memset(hi[:, 1, :], AIM - SPREAD))
                PER = 7 + A + 1 + 7 + 1 + 3 + 1 + 3
                with dve.Fori(0, ITERS) as i:
                    step.enter(i, PER)
                    step(dve.tensor_tensor(w[:, :, :], hi[:, :, :], lo[:, :, :], ALU.subtract))
                    step(dve.reciprocal(w[:, 1, :], w[:, 1, :]))
                    step(dve.scalar_tensor_tensor(w[:, 1, :], lo[:, 1, :], AIM, w[:, 1, :], ALU.subtract, ALU.mult))
                    step(dve.tensor_scalar(w[:, 1, :], w[:, 1, :], -0.2, -0.8, ALU.min, ALU.max))
                    step(dve.tensor_tensor(w[:, 0, :], w[:, 0, :], w[:, 1, :], ALU.mult))
                    step(dve.tensor_tensor(at[:, 0, :], lo[:, 0, :], w[:, 0, :], ALU.subtract))
                    step(dve.tensor_scalar(nt[:, :], at[:, 0, :], -1.0, None, ALU.mult))
                    dve.sem_inc(probe, 1)
                    for b in range(A):
                        step(dve.tensor_scalar(junk[:, b % 2, :], E[:, b, :], at[:, 0, b:b + 1], 0.0, ALU.is_ge, ALU.add, accum_out=at[:, 1, b:b + 1]))
                    dve.wait_ge(counted, i * A + A)
                    step(dve.tensor_scalar(at[:, 1, A:TB], at[:, 1, A:TB], 0.5, T * 0.5, ALU.mult, ALU.add))
                    step(dve.tensor_scalar(ok[:, :], at[:, 1, :], kk - 8.5, None, ALU.is_ge))
                    step(dve.scalar_tensor_tensor(ok[:, :], at[:, 1, :], kk - 0.5, ok[:, :], ALU.is_le, ALU.mult))
                    step(dve.tensor_scalar(v[:, :], at[:, 1, :], -1.0, float(kk), ALU.mult, ALU.add))
                    step(dve.tensor_tensor(v[:, :], v[:, :], ok[:, :], ALU.mult))
                    step(dve.tensor_tensor(need[:, :], need[:, :], v[:, :], ALU.max))
                    step(dve.tensor_tensor(ok[:, :], ok[:, :], at[:, 0, :], ALU.mult))
                    step(dve.tensor_tensor(cut[:, :], cut[:, :], ok[:, :], ALU.max))
                    step(dve.tensor_scalar(u[:, :], at[:, 1, :], AIM, None, ALU.is_ge))
                    for end, sign in ((lo, 1.0), (hi, -1.0)):
                        if sign < 0:
                            step(dve.tensor_scalar(u[:, :], u[:, :], -1.0, 1.0, ALU.mult, ALU.add))
                        step(dve.tensor_tensor(d[:, :, :], at[:, :, :], end[:, :, :], ALU.subtract))
                        step(dve.tensor_tensor(d[:, :, :], d[:, :, :], u[:, :].unsqueeze(1).broadcast_to([P, 2, TB]), ALU.mult))
                        step(dve.tensor_tensor(end[:, :, :], end[:, :, :], d[:, :, :], ALU.add))
                step.leave(ITERS)
                for b in range(A, TB):
                    step(dve.tensor_scalar(junk[:, b % 2, :], E[:, b, :], cut[:, b:b + 1], 0.0, ALU.is_ge, ALU.add, accum_out=at[:, 1, b:b + 1]))
                step(dve.tensor_scalar(need[:, A:TB], at[:, 1, A:TB], -1.0, float(kk), ALU.mult, ALU.add))
                step(dve.tensor_scalar(ok[:, :], need[:, :], 1.0, None, ALU.is_ge))
                step(dve.scalar_tensor_tensor(ok[:, :], need[:, :], 8.0, ok[:, :], ALU.is_le, ALU.mult))
                dve.tensor_reduce(okr[:, :], ok[:, :], AX, ALU.min).then_inc(okd, 1)
                dve.wait_ge(okps, 1)
                dve.tensor_scalar(general[:, :], g.ps[0:1, 0:1], P - 0.5, None, ALU.is_lt)

            @block.tensor
            def _(pe):
                pe.wait_ge(okd, 1)
                pe.matmul(g.ps[0:1, 0:1], okr[:, :], g.ones[:, 0:1], start=True, stop=True).then_inc(okps, 1)


def keep_below_cut(dve, steps, E, cut, need, ssum, room, kept):
    below, rest, top, place, drop = room
    step = Steps(dve, steps)
    for i in range(8):
        dve.memset(place[:, i:i + 1], float(i))
    step(dve.memset(drop[:, :], 0.0))
    for b in range(TB):
        e = E[:, b, :]
        step(dve.scalar_tensor_tensor(below[:, :], e, cut[:, b:b + 1], e, ALU.is_lt, ALU.mult))
        step(dve.max(top[:, :], below[:, :]))
        step(dve.scalar_tensor_tensor(drop[:, :], place[:, :], need[:, b:b + 1], top[:, :], ALU.is_lt, ALU.mult))
        step(dve.match_replace(rest[:, :], drop[:, :], below[:, :], 0.0))
        step(dve.scalar_tensor_tensor(e, e, 1.0, rest[:, :], ALU.mult, ALU.subtract, accum_out=ssum[:, b:b + 1]))
        dve.sem_inc(kept, 1)


def keep_by_bisection(dve, steps, E, kk, ssum, room, kept):
    ITERS = 31
    lo, hi, mid, cnt, need, up, dn, tie, rank = room
    junk = rank
    step = Steps(dve, steps)

    def count(at):
        for b in range(TB):
            step(dve.tensor_scalar(junk[:, :], E[:, b, :], at[:, b:b + 1], 0.0, ALU.is_ge, ALU.add, accum_out=cnt[:, b:b + 1]))
    dve.memset(lo[:, :], 0.0)
    step(dve.memset(hi[:, :], 2.0))
    PER = TB + 7
    with dve.Fori(0, ITERS) as i:
        step.enter(i, PER)
        step(dve.tensor_tensor(mid[:, :], lo[:, :], hi[:, :], ALU.add))
        step(dve.tensor_scalar(mid[:, :], mid[:, :], 0.5, None, ALU.mult))
        count(mid)
        step(dve.tensor_scalar(up[:, :], cnt[:, :], float(kk), None, ALU.is_ge))
        step(dve.tensor_tensor(dn[:, :], up[:, :], mid[:, :], ALU.mult))
        step(dve.tensor_tensor(lo[:, :], lo[:, :], dn[:, :], ALU.max))
        step(dve.scalar_tensor_tensor(dn[:, :], up[:, :], 1.0e30, mid[:, :], ALU.mult, ALU.add))
        step(dve.tensor_tensor(hi[:, :], hi[:, :], dn[:, :], ALU.min))
    step.leave(ITERS)
    count(hi)
    step(dve.tensor_scalar(need[:, :], cnt[:, :], -1.0, float(kk), ALU.mult, ALU.add))
    for b in range(TB):
        e = E[:, b, :]
        step(dve.tensor_scalar(rank[:, :], e, hi[:, b:b + 1], None, ALU.is_ge))
        step(dve.scalar_tensor_tensor(tie[:, :], e, lo[:, b:b + 1], rank[:, :], ALU.is_ge, ALU.subtract))
        step(dve.tensor_tensor_scan(rank[:, :], tie[:, :], tie[:, :], 0.0, ALU.add, ALU.max))
        step(dve.scalar_tensor_tensor(tie[:, :], rank[:, :], need[:, b:b + 1], tie[:, :], ALU.is_le, ALU.mult))
        step(dve.scalar_tensor_tensor(tie[:, :], e, hi[:, b:b + 1], tie[:, :], ALU.is_ge, ALU.add))
        step(dve.scalar_tensor_tensor(e, e, 1.0, tie[:, :], ALU.mult, ALU.mult, accum_out=ssum[:, b:b + 1]))
    dve.sem_inc(kept, TB)


def dual_attention(nc, g, I):
    R, DFF = 64, 512
    K = DFF // P
    KEEP = max(1, int(T * 0.2))
    with ExitStack() as ctx:
        r = Room(nc, ctx, "l2a")
        dense = r.sb("dense", [P, TB, C])
        bp = r.sb("bp", [R, 2])
        lam = r.sb("lam", [P, 2])
        sc = r.sb("sc", [P, 2])
        with ExitStack() as ctx0:
            r0 = Room(nc, ctx0, "l2h")
            w = r0.sb("wqkv", [C, 3, C])
            bqk = r0.sb("bqk", [P, 2])
            bv = r0.sb("bv", [P, C])

            def load(sp, s):
                sp.dma_start(w[:, :, :].rearrange("c i o -> c (i o)"), I["L2_attn_in_proj_wT"]).then_inc(s, 16)
                sp.dma_start(bqk[:, :], I["L2_attn_in_proj_b"][0:2 * C].rearrange("(i p) -> p i", p=P), allow_slow_non_contiguous=True).then_inc(s, 16)
                sp.dma_start(bv[:, :], I["L2_attn_in_proj_b"][2 * C:3 * C].rearrange("(a c) -> a c", a=1).broadcast_to([P, C])).then_inc(s, 16)
                sp.dma_start(bp[:, 0:1], I["L2_attn_Qp_b"].rearrange("(p a) -> p a", a=1), allow_slow_non_contiguous=True).then_inc(s, 16)
                sp.dma_start(bp[:, 1:2], I["L2_attn_Kp_b"].rearrange("(p a) -> p a", a=1), allow_slow_non_contiguous=True).then_inc(s, 16)
                sp.dma_start(lam[:, 0:1], I["L2_attn_lam"].rearrange("(p a) -> p a", a=1).broadcast_to([P, 1]), allow_slow_non_contiguous=True).then_inc(s, 16)
                return 6
            layernorm_transpose(nc, g, "ln4", load)
            prep = r0.sem("bias_scaled")
            QS = 8 ** -0.5
            with nc.Block() as block:

                @block.vector
                def _(dve):
                    dve.tensor_scalar(bqk[:, 0:1], bqk[:, 0:1], QS, None, ALU.mult).then_inc(prep, 1)
                    dve.tensor_scalar(bp[:, 0:1], bp[:, 0:1], R ** -0.5, None, ALU.mult)
                    dve.tensor_scalar(lam[:, 1:2], lam[:, 0:1], -1.0, None, ALU.mult).then_inc(prep, 1)

                @block.scalar
                def _(act):
                    act.wait_ge(prep, 2)
                    act.activation(sc[:, :], lam[:, :], ACT.Sigmoid)
            head_attention(nc, g, "l2m", w, (bqk[:, 0:1], bqk[:, 1:2], bv[:, :]), QS, 1.0, 1.0, dense)
        wo = r.sb("wo", [C, C])
        wp = r.sb("wp", [C, 2, R])
        wv = r.sb("wv", [C, C])
        rows = r.sb("rows", [P, 7, C])
        f1 = r.sb("f1", [C, DFF])
        f2 = r.sb("f2", [P, K, C])
        b1 = r.sb("b1", [P, K])
        with ExitStack() as ctx0:
            r0 = Room(nc, ctx0, "l2o")
            OT = r0.sb("OT", [C, T])
            tr, cp, yps, dd = r0.sem("o_transposed"), r0.sem("o_copied"), r0.sem("y_in_psum"), r0.sem("dense_done")
            first, rest = r0.sem("projection_loaded"), r0.sem("rest_loaded")
            with nc.Block() as block:

                @block.sync
                def _(sp):
                    rest_loads = 0

                    def ld(dst, src, slow=False):
                        nonlocal rest_loads
                        rest_loads += 1
                        sp.dma_start(dst, src, allow_slow_non_contiguous=slow).then_inc(rest, 16)
                    sp.dma_start(wo[:, :], I["L2_attn_out_proj_wT"]).then_inc(first, 16)
                    for i, nm in enumerate(("out_proj_b", "Vp_b", "ff2_b", "ln1_g", "ln1_b", "ln2_g", "ln2_b")):
                        v = I["L2_attn_" + nm].rearrange("(a c) -> a c", a=1).broadcast_to([P, C])
                        if i == 0:
                            sp.dma_start(rows[:, i, :], v).then_inc(first, 16)
                        else:
                            ld(rows[:, i, :], v)
                    ld(wp[:, 0, :], I["L2_attn_Qp_wT"])
                    ld(wp[:, 1, :], I["L2_attn_Kp_wT"])
                    ld(wv[:, :], I["L2_attn_Vp_wT"])
                    ld(f1[:, :], I["L2_attn_ff1_wT"])
                    ld(f2[:, :, :], I["L2_attn_ff2_wT"].rearrange("(k p) c -> p k c", p=P))
                    ld(b1[:, :], I["L2_attn_ff1_b"].rearrange("(k p) -> p k", p=P), slow=True)
                    sp.wait_ge(rest, 16 * rest_loads)

                @block.tensor
                def _(pe):
                    transpose_blocks(pe, g, dense, 0, tr)
                    pe.wait_ge(first, 32)
                    pe.wait_ge(cp, 1)
                    for b in range(TB):
                        pe.matmul(g.ps[:, T + b * P:T + (b + 1) * P], OT[:, b * P:(b + 1) * P], wo[:, :], start=True, stop=True).then_inc(yps, 1)

                @block.vector
                def _(dve):
                    dve.wait_ge(tr, 1)
                    dve.tensor_copy(OT[:, :], g.ps[:, 0:T]).then_inc(cp, 1)
                    dve.wait_ge(first, 32)
                    for q in range(NCH):
                        dve.wait_ge(yps, 4 * q + 4)
                        dve.tensor_tensor(dense[:, 4 * q:4 * q + 4, :], g.ps[:, T + q * CH:T + (q + 1) * CH].rearrange("p (b c) -> p b c", c=C),
                                          rows[:, 0, :].unsqueeze(1).broadcast_to([P, 4, C]), ALU.add).then_inc(dd, 1)
        with ExitStack() as ctx1:
            r1 = Room(nc, ctx1, "l2s")
            E = r1.sb("E", [P, TB, T])
            V = r1.sb("V", [P, TB, C])
            mx = r1.sb("mx", [P, TB])
            Z = r1.sb("Z", [P, TB])
            ssum = r1.sb("ssum", [P, TB])
            st = r1.sb("bn", [P, TB, 2, 6])
            mv = r1.sb("meanvar", [P, TB, 2])
            cut = r1.sb("cut", [P, TB])
            need = r1.sb("need", [P, TB])
            general = r1.sb("general", [1, 1], I32)
            with ExitStack() as ctx2:
                r2 = Room(nc, ctx2, "l2q")
                qk = r2.sb("qk", [P, 2, T])
                zero, qps, qcp, vps, vcp = r2.sem("zeroed"), r2.sem("qk_in_psum"), r2.sem("qk_copied"), r2.sem("v_in_psum"), r2.sem("v_copied")
                sps, mxd, exd = r2.sem("scores_in_psum"), r2.sem("max_done"), r2.sem("exp_done")
                smp = r2.sem("sampled")
                with nc.Block() as block:

                    @block.gpsimd
                    def _(pool):
                        pool.memset(qk[R:P, :, :], 0.0).then_inc(zero, 1)

                    @block.tensor
                    def _(pe):
                        for i in range(2):
                            for q in range(NCH):
                                mm = pe.matmul(g.ps[0:R, i * T + q * CH:i * T + (q + 1) * CH], wp[:, i, :], g.hT[:, q * CH:(q + 1) * CH],
                                               start=True, stop=True)
                            mm.then_inc(qps, 1)
                        pe.wait_ge(qcp, 1)
                        for b in range(TB):
                            mm = pe.matmul(g.ps[:, b * P:(b + 1) * P], g.hT[:, b * P:(b + 1) * P], wv[:, :], start=True, stop=True)
                        mm.then_inc(vps, 1)
                        pe.wait_ge(zero, 1)
                        pe.wait_ge(qcp, 2)
                        for b in range(TB):
                            if b == 1:
                                pe.wait_ge(vcp, 1)
                            if b >= 2:
                                pe.wait_ge(exd, b - 1)
                            half = (b + 1) % 2
                            for q in range(NCH):
                                mm = pe.matmul(g.ps[:, half * T + q * CH:half * T + (q + 1) * CH], qk[:, 0, b * P:(b + 1) * P],
                                               qk[:, 1, q * CH:(q + 1) * CH], start=True, stop=True)
                            mm.then_inc(sps, 1)

                    @block.scalar
                    def _(act):
                        for i, s in enumerate((R ** -0.5, 1.0)):
                            act.wait_ge(qps, i + 1)
                            act.activation(qk[0:R, i, :], g.ps[0:R, i * T:(i + 1) * T], ACT.Identity, bias=bp[:, i:i + 1], scale=s).then_inc(qcp, 1)
                        for b in range(TB):
                            act.wait_ge(mxd, b + 1)
                            half = (b + 1) % 2
                            act.activation(E[:, b, :], g.ps[:, half * T:(half + 1) * T], ACT.Exp, bias=mx[:, b:b + 1],
                                           accum_out=Z[:, b:b + 1]).then_inc(exd, 1)

                    @block.vector
                    def _(dve):
                        dve.wait_ge(vps, 1)
                        dve.tensor_tensor(V[:, :, :], g.ps[:, 0:T].rearrange("p (b c) -> p b c", c=C),
                                          rows[:, 1, :].unsqueeze(1).broadcast_to([P, TB, C]), ALU.add).then_inc(vcp, 1)

                        def sample(b):
                            dve.wait_ge(exd, b + 1)
                            for k in range(2):
                                ins = dve.bn_stats(st[:, b, k, :], E[:, b, k * (T // 2):(k + 1) * (T // 2):2])
                            ins.then_inc(smp, 1)
                        for b in range(TB):
                            dve.wait_ge(sps, b + 1)
                            half = (b + 1) % 2
                            dve.tensor_reduce(mx[:, b:b + 1], g.ps[:, half * T:(half + 1) * T], AX, ALU.max, negate=True).then_inc(mxd, 1)
                            if b:
                                sample(b - 1)
                        sample(TB - 1)
                        dve.wait_ge(smp, TB)
                        for b in range(TB):
                            dve.bn_aggr(mv[:, b, :], st[:, b, :, :].rearrange("p k s -> p (k s)"))
            find_cut(nc, g, E, KEEP, Z, mv[:, :, 1], cut, need, general)
            with ExitStack() as ctx3:
                r3 = Room(nc, ctx3, "l2v")
                NPT = 4
                pT = r3.sb("pT", [P, NPT, CH])
                sT = r3.sb("sT", [C, 2, CH])
                below = r3.sb("below", [P, T])
                rest = r3.sb("rest", [P, T])
                small = [r3.sb("small%d" % i, [P, TB]) for i in range(7)]
                top8 = [r3.sb("top%d" % i, [P, 8]) for i in range(3)]
                kept, gsteps, fsteps = r3.sem("rows_kept"), r3.sem("general_steps"), r3.sem("fast_steps")
                tr, pcp, ops, ocp, otr, fin, steps, rsr = r3.sem("p_transposed"), r3.sem("p_copied"), r3.sem("values_done"), r3.sem("values_copied"), r3.sem("values_transposed"), r3.sem("sparse_done"), r3.sem("steps"), r3.sem("str")
                with nc.Block() as block:

                    @block.tensor
                    def _(pe):
                        def back(q):
                            pe.wait_ge(ocp, q + 1)
                            if q >= 2:
                                pe.wait_ge(fin, q - 1)
                            for j in range(4):
                                mm = pe.transpose(g.ps[:, (6 + q % 2) * CH + j * P:(6 + q % 2) * CH + (j + 1) * P], sT[:, q % 2, j * P:(j + 1) * P],
                                                  g.ident[:, :])
                            mm.then_inc(otr, 1)

                        def turn(n):
                            q, kt = divmod(n, TB)
                            if n >= 4:
                                pe.wait_ge(pcp, n - 3)
                            if kt == 0:
                                pe.wait_ge(kept, 4 * q + 4)
                            for j in range(4):
                                mm = pe.transpose(g.ps[:, (n % 4) * CH + j * P:(n % 4) * CH + (j + 1) * P], E[:, 4 * q + j, kt * P:(kt + 1) * P],
                                                  g.ident[:, :])
                            mm.then_inc(tr, 1)

                        def weigh(n):
                            q, kt = divmod(n, TB)
                            pe.wait_ge(pcp, n + 1)
                            if kt == 0 and q >= 2:
                                pe.wait_ge(ocp, q - 1)
                            mm = pe.matmul(g.ps[:, (4 + q % 2) * CH:(5 + q % 2) * CH], V[:, kt, :], pT[:, n % NPT, :], start=(kt == 0), stop=(kt == TB - 1))
                            mm.then_inc(ops, 1)
                        N = NCH * TB
                        for n in range(N + 1):
                            if n < N:
                                turn(n)
                            if n:
                                weigh(n - 1)
                            if n % TB == 4 and n > TB:
                                back(n // TB - 1)
                        back(NCH - 1)

                    @block.scalar
                    def _(act):
                        for n in range(NCH * TB):
                            act.wait_ge(tr, n + 1)
                            if n >= NPT:
                                act.wait_ge(ops, n - NPT + 1)
                            act.copy(pT[:, n % NPT, :], g.ps[:, (n % 4) * CH:(n % 4 + 1) * CH]).then_inc(pcp, 1)

                    @block.vector
                    def _(dve):
                        step = Steps(dve, steps)
                        flag = dve.value_load(general[0:1, 0:1], min_val=0, max_val=1)
                        with dve.If(flag > 0):
                            keep_by_bisection(dve, gsteps, E, KEEP, ssum, (*small, below, rest), kept)
                        with dve.Else():
                            keep_below_cut(dve, fsteps, E, cut, need, ssum, (below, rest, *top8), kept)
                        step(dve.scalar_tensor_tensor(ssum[:, :], Z[:, :], 1.0e-9, ssum[:, :], ALU.mult, ALU.add))
                        step(dve.reciprocal(ssum[:, :], ssum[:, :]))
                        step(dve.tensor_scalar(ssum[:, :], ssum[:, :], sc[:, 1:2], None, ALU.mult))
                        step(dve.tensor_scalar(dense[:, :, :], dense[:, :, :], sc[:, 0:1], None, ALU.mult))
                        for q in range(NCH):
                            dve.wait_ge(ops, TB * (q + 1))
                            if q >= 2:
                                dve.wait_ge(otr, q - 1)
                            dve.tensor_copy(sT[:, q % 2, :], g.ps[:, (4 + q % 2) * CH:(5 + q % 2) * CH]).then_inc(ocp, 1)
                            dve.wait_ge(otr, q + 1)
                            for j in range(4):
                                b = 4 * q + j
                                ins = dve.scalar_tensor_tensor(dense[:, b, :], g.ps[:, (6 + q % 2) * CH + j * P:(6 + q % 2) * CH + (j + 1) * P],
                                                               ssum[:, b:b + 1], dense[:, b, :], ALU.mult, ALU.add)
                            ins.then_inc(fin, 1)
        with ExitStack() as ctx4:
            r4 = Room(nc, ctx4, "l2p")
            x1 = r4.sb("x1", [P, TB, C])
            hb = r4.sb("hb", [P, K, T])
            tr, add, fps, rel, yps, yd = r4.sem("src_transposed"), r4.sem("src_added"), r4.sem("ff_in_psum"), r4.sem("relu_done"), r4.sem("y_in_psum"), r4.sem("y_done")
            with nc.Block() as block:

                @block.tensor
                def _(pe):
                    for b in range(TB):
                        mm = pe.transpose(g.ps[:, b * P:(b + 1) * P], g.hT[:, b * P:(b + 1) * P], g.ident[:, :])
                    mm.then_inc(tr, 1)

                @block.vector
                def _(dve):
                    dve.wait_ge(tr, 1)
                    dve.tensor_tensor(dense[:, :, :], dense[:, :, :], g.ps[:, 0:T].rearrange("p (b c) -> p b c", c=C), ALU.add).then_inc(add, 1)
            layernorm_transpose(nc, g, "lnp1", None, dense, (rows[:, 3, :], rows[:, 4, :]), x1)
            with nc.Block() as block:

                @block.tensor
                def _(pe):
                    for n in range(K * NCH):
                        m, q = n % K, n // K
                        if n >= 4:
                            pe.wait_ge(rel, n - 3)
                        pe.matmul(g.ps[:, (n % 4) * CH:(n % 4 + 1) * CH], f1[:, m * P:(m + 1) * P], g.hT[:, q * CH:(q + 1) * CH],
                                  start=True, stop=True).then_inc(fps, 1)
                    for b in range(TB):
                        pe.wait_ge(rel, K * (b // 4 + 1))
                        if b >= 4:
                            pe.wait_ge(yd, b - 3)
                        for k in range(K):
                            mm = pe.matmul(g.ps[:, (4 + b % 4) * CH:(4 + b % 4) * CH + C], hb[:, k, b * P:(b + 1) * P], f2[:, k, :],
                                           start=(k == 0), stop=(k == K - 1))
                        mm.then_inc(yps, 1)

                @block.scalar
                def _(act):
                    for n in range(K * NCH):
                        m, q = n % K, n // K
                        act.wait_ge(fps, n + 1)
                        act.activation(hb[:, m, q * CH:(q + 1) * CH], g.ps[:, (n % 4) * CH:(n % 4 + 1) * CH], ACT.Relu, bias=b1[:, m:m + 1]).then_inc(rel, 1)

                @block.gpsimd
                def _(pool):
                    pool.tensor_tensor(x1[:, :, :], x1[:, :, :], rows[:, 2, :].unsqueeze(1).broadcast_to([P, TB, C]), ALU.add).then_inc(add, 1)

                @block.vector
                def _(dve):
                    dve.wait_ge(add, 2)
                    for b in range(TB):
                        dve.wait_ge(yps, b + 1)
                        dve.tensor_tensor(x1[:, b, :], x1[:, b, :], g.ps[:, (4 + b % 4) * CH:(4 + b % 4) * CH + C], ALU.add).then_inc(yd, 1)
            layernorm_transpose(nc, g, "lnp2", None, x1, (rows[:, 5, :], rows[:, 6, :]), dense, transposed=False)
            with nc.Block() as block:

                @block.vector
                def _(dve):
                    dve.tensor_tensor(g.X[:, :, :], g.X[:, :, :], dense[:, :, :], ALU.add)


def ternary_ffn(nc, g, I):
    H = 512
    K = H // P
    with ExitStack() as ctx:
        r = Room(nc, ctx, "l2f")
        w12 = r.sb("w12", [C, 2, H])
        h12 = r.sb("h12", [P, 2, K, H])
        w3 = r.sb("w3", [P, K, C])
        sc = r.sb("scales", [P, 4, K])
        s3 = r.sb("s3", [P, C])
        a = r.sb("a", [P, K, T])
        b_ = r.sb("b", [P, K, T])

        def load(sp, s):
            n = 0
            for i, nm in enumerate(("w1", "w2")):
                sp.dma_start(w12[:, i, :], I[f"L2_ffn_{nm}_wT"]).then_inc(s, 16)
            for i, nm in enumerate(("h1", "h2")):
                sp.dma_start(h12[:, i, :, :], I[f"L2_ffn_{nm}_wT"].rearrange("(k p) o -> p k o", p=P)).then_inc(s, 16)
            for i, nm in enumerate(("w1", "w2", "h1", "h2")):
                sp.dma_start(sc[:, i, :], I[f"L2_ffn_{nm}_s"].rearrange("(k p) -> p k", p=P), allow_slow_non_contiguous=True).then_inc(s, 16)
            sp.dma_start(w3[:, :, :], I["L2_ffn_w3_wT"].rearrange("(k p) o -> p k o", p=P)).then_inc(s, 16)
            sp.dma_start(s3[:, :], I["L2_ffn_w3_s"].rearrange("(a c) -> a c", a=1).broadcast_to([P, C])).then_inc(s, 16)
            return 10
        layernorm_transpose(nc, g, "ln5", load)
        sl = r.sb("silu", [P, 2, CH])
        yb = r.sb("y", [P, 2, C])
        gps, ups, sid, had = r.sem("gate_in_psum"), r.sem("up_in_psum"), r.sem("silu_done"), r.sem("product_done")
        zps, gel = r.sem("hidden_in_psum"), r.sem("gelu_done")
        yps, ysc, xad = r.sem("y_in_psum"), r.sem("y_scaled"), r.sem("x_added")
        N1 = K * NCH
        with nc.Block() as block:

            @block.tensor
            def _(pe):
                for n in range(N1):
                    m, q = n % K, n // K
                    if n >= 2:
                        pe.wait_ge(sid, n - 1)
                    pe.matmul(g.ps[:, (n % 2) * CH:(n % 2 + 1) * CH], w12[:, 0, m * P:(m + 1) * P], g.hT[:, q * CH:(q + 1) * CH],
                              start=True, stop=True).then_inc(gps, 1)
                    if n >= 2:
                        pe.wait_ge(had, n - 1)
                    pe.matmul(g.ps[:, (2 + n % 2) * CH:(3 + n % 2) * CH], w12[:, 1, m * P:(m + 1) * P], g.hT[:, q * CH:(q + 1) * CH],
                              start=True, stop=True).then_inc(ups, 1)
                for layer in range(2):
                    src = a if layer == 0 else b_
                    for n in range(N1):
                        m, q = n % K, n // K
                        i = layer * N1 + n
                        if layer == 0:
                            pe.wait_ge(had, K * (q + 1))
                        else:
                            pe.wait_ge(gel, K * (q + 1))
                        if i >= 4:
                            pe.wait_ge(gel, i - 3)
                        for k in range(K):
                            mm = pe.matmul(g.ps[:, (4 + i % 4) * CH:(5 + i % 4) * CH], h12[:, layer, k, m * P:(m + 1) * P],
                                           src[:, k, q * CH:(q + 1) * CH], start=(k == 0), stop=(k == K - 1))
                        mm.then_inc(zps, 1)
                for t in range(TB):
                    pe.wait_ge(gel, N1 + K * (t // 4 + 1))
                    if t >= 2:
                        pe.wait_ge(ysc, t - 1)
                    for k in range(K):
                        mm = pe.matmul(g.ps[:, (t % 2) * CH:(t % 2) * CH + C], a[:, k, t * P:(t + 1) * P], w3[:, k, :],
                                       start=(k == 0), stop=(k == K - 1))
                    mm.then_inc(yps, 1)

            @block.scalar
            def _(act):
                for n in range(N1):
                    act.wait_ge(gps, n + 1)
                    if n >= 2:
                        act.wait_ge(had, n - 1)
                    act.activation(sl[:, n % 2, :], g.ps[:, (n % 2) * CH:(n % 2 + 1) * CH], ACT.Silu, scale=sc[:, 0, n % K:n % K + 1]).then_inc(sid, 1)
                for i in range(2 * N1):
                    layer, n = divmod(i, N1)
                    m, q = n % K, n // K
                    dst = b_ if layer == 0 else a
                    act.wait_ge(zps, N1 if layer == 1 and n == 0 else i + 1)
                    act.wait_ge(zps, i + 1)
                    act.activation(dst[:, m, q * CH:(q + 1) * CH], g.ps[:, (4 + i % 4) * CH:(5 + i % 4) * CH], ACT.Gelu,
                                   scale=sc[:, 2 + layer, m:m + 1]).then_inc(gel, 1)

            @block.vector
            def _(dve):
                for n in range(N1):
                    dve.wait_ge(ups, n + 1)
                    dve.wait_ge(sid, n + 1)
                    dve.scalar_tensor_tensor(a[:, n % K, (n // K) * CH:(n // K + 1) * CH], g.ps[:, (2 + n % 2) * CH:(3 + n % 2) * CH],
                                             sc[:, 1, n % K:n % K + 1], sl[:, n % 2, :], ALU.mult, ALU.mult).then_inc(had, 1)
                for t in range(TB):
                    dve.wait_ge(yps, t + 1)
                    dve.tensor_tensor(yb[:, t % 2, :], g.ps[:, (t % 2) * CH:(t % 2) * CH + C], s3[:, :], ALU.mult).then_inc(ysc, 1)
                    dve.wait_ge(ysc, t + 1)
                    dve.tensor_tensor(g.X[:, t, :], g.X[:, t, :], yb[:, t % 2, :], ALU.add).then_inc(xad, 1)
                    if t >= 1:
                        dve.wait_ge(xad, t)


def int8_ffn(nc, g, I):
    H = 384
    K = H // P
    import numpy as np
    SCALE = float(np.float32(1.0 / 127.0))
    with ExitStack() as ctx:
        r = Room(nc, ctx, "l3f")
        wi = r.sb("wi", [C, 2, H], I32)
        wdi = r.sb("wdi", [P, K, C], I32)
        w = r.sb("w", [C, 2, H])
        wd = r.sb("wd", [P, K, C])

        def load(sp, s):
            sp.dma_start(wi[:, 0, :], I["L3_ffn_w_gateT"]).then_inc(s, 16)
            sp.dma_start(wi[:, 1, :], I["L3_ffn_w_upT"]).then_inc(s, 16)
            sp.dma_start(wdi[:, :, :], I["L3_ffn_w_downT"].rearrange("(k p) o -> p k o", p=P)).then_inc(s, 16)
            return 3
        layernorm_transpose(nc, g, "ln7", load)
        a = r.sb("a", [P, K, T])
        sl = r.sb("silu", [P, 2, CH])
        deq = r.sem("dequantised")
        gps, ups, sid, had = r.sem("gate_in_psum"), r.sem("up_in_psum"), r.sem("silu_done"), r.sem("product_done")
        yps, xad = r.sem("y_in_psum"), r.sem("x_added")
        N1 = K * NCH
        with nc.Block() as block:

            @block.tensor
            def _(pe):
                def down(t):
                    pe.wait_ge(had, K * (t // 4 + 1))
                    if t >= 2:
                        pe.wait_ge(xad, t - 1)
                    for k in range(K):
                        mm = pe.matmul(g.ps[:, (4 + t % 2) * CH:(4 + t % 2) * CH + C], a[:, k, t * P:(t + 1) * P], wd[:, k, :],
                                       start=(k == 0), stop=(k == K - 1))
                    mm.then_inc(yps, 1)
                pe.wait_ge(deq, 2)
                for n in range(N1):
                    m, q = n % K, n // K
                    if n >= 2:
                        pe.wait_ge(sid, n - 1)
                    pe.matmul(g.ps[:, (n % 2) * CH:(n % 2 + 1) * CH], w[:, 0, m * P:(m + 1) * P], g.hT[:, q * CH:(q + 1) * CH],
                              start=True, stop=True).then_inc(gps, 1)
                    if n >= 2:
                        pe.wait_ge(had, n - 1)
                    pe.matmul(g.ps[:, (2 + n % 2) * CH:(3 + n % 2) * CH], w[:, 1, m * P:(m + 1) * P], g.hT[:, q * CH:(q + 1) * CH],
                              start=True, stop=True).then_inc(ups, 1)
                for t in range(TB):
                    down(t)

            @block.scalar
            def _(act):
                for n in range(N1):
                    act.wait_ge(gps, n + 1)
                    if n >= 2:
                        act.wait_ge(had, n - 1)
                    act.activation(sl[:, n % 2, :], g.ps[:, (n % 2) * CH:(n % 2 + 1) * CH], ACT.Silu).then_inc(sid, 1)

            @block.vector
            def _(dve):
                dve.tensor_scalar(w[:, :, :], wi[:, :, :], SCALE, None, ALU.mult).then_inc(deq, 1)
                dve.tensor_scalar(wd[:, :, :], wdi[:, :, :], SCALE, None, ALU.mult).then_inc(deq, 1)
                for n in range(N1):
                    dve.wait_ge(ups, n + 1)
                    dve.wait_ge(sid, n + 1)
                    dve.tensor_tensor(a[:, n % K, (n // K) * CH:(n // K + 1) * CH], g.ps[:, (2 + n % 2) * CH:(3 + n % 2) * CH],
                                      sl[:, n % 2, :], ALU.mult).then_inc(had, 1)
                for t in range(TB):
                    dve.wait_ge(yps, t + 1)
                    dve.tensor_tensor(g.X[:, t, :], g.X[:, t, :], g.ps[:, (4 + t % 2) * CH:(4 + t % 2) * CH + C], ALU.add).then_inc(xad, 1)


def plain_attention(nc, g, I):
    S = T
    with ExitStack() as ctx:
        r = Room(nc, ctx, "l3a")
        w = r.sb("wqkv", [C, 3, C])
        wo = r.sb("wo", [C, C])

        def load(sp, s):
            sp.dma_start(w[:, :, :].rearrange("c i o -> c (i o)"), I["L3_attn_w_qkvT"]).then_inc(s, 16)
            sp.dma_start(wo[:, :], I["L3_attn_w_oT"]).then_inc(s, 16)
            return 2
        layernorm_transpose(nc, g, "ln6", load)
        O = r.sb("O", [P, TB, C])
        hid = C ** -0.5
        head_attention(nc, g, "l3h", w, None, hid * 8 ** -0.5, hid, hid * (S / (S - 1.0) ** 0.5) * S ** -0.5 * hid, O)
        OT = r.sb("OT", [C, T])
        tr, cp, yps, xad = r.sem("o_transposed"), r.sem("o_copied"), r.sem("y_in_psum"), r.sem("x_added")
        with nc.Block() as block:

            @block.tensor
            def _(pe):
                transpose_blocks(pe, g, O, 0, tr)
                pe.wait_ge(cp, 1)
                for b in range(TB):
                    pe.matmul(g.ps[:, T + b * P:T + (b + 1) * P], OT[:, b * P:(b + 1) * P], wo[:, :], start=True, stop=True).then_inc(yps, 1)

            @block.vector
            def _(dve):
                dve.wait_ge(tr, 1)
                dve.tensor_copy(OT[:, :], g.ps[:, 0:T]).then_inc(cp, 1)
                for q in range(NCH):
                    dve.wait_ge(yps, 4 * q + 4)
                    dve.tensor_tensor(g.X[:, 4 * q:4 * q + 4, :], g.X[:, 4 * q:4 * q + 4, :],
                                      g.ps[:, T + q * CH:T + (q + 1) * CH].rearrange("p (b c) -> p b c", c=C), ALU.add).then_inc(xad, 1)


def store_output(nc, g, out):
    with ExitStack() as ctx:
        r = Room(nc, ctx, "out")
        stored = r.sem("stored")
        with nc.Block() as block:

            @block.sync
            def _(sp):
                sp.dma_start(out.rearrange("a (b p) c -> p (a b) c", p=P), g.X[:, :, :]).then_inc(stored, 16)
                sp.wait_ge(stored, 16)


LAYERS = (bond_attention, masked_ffn, mamba, gated_experts, dual_attention, ternary_ffn, plain_attention, int8_ffn)


def clear_semaphores(nc):
    used = list(nc.released_uncleared_semaphores)
    with nc.Block() as block:

        @block.gpsimd
        def _(pool):
            pool.sem_clear(range(min(used), max(used) + 1))


def build_program(nc, I, out, layers=LAYERS):
    g = Shared()
    with ExitStack() as ctx:
        setup_shared(nc, ctx, g, I["L0_attn_x"])
        for i, layer in enumerate(layers):
            if i:
                clear_semaphores(nc)
            layer(nc, g, I)
        store_output(nc, g, out)


TRANSPOSED = {
    "L0_attn_rel_pos_emb": (1, 0), "L0_ffn_w2": (1, 0, 2),
    "L1_attn_in_proj_w": (1, 0), "L1_attn_out_proj_w": (1, 0),
    "L1_attn_x_proj_w_f": (1, 0), "L1_attn_x_proj_w_r": (1, 0), "L1_attn_dt_proj_w_f": (1, 0), "L1_attn_dt_proj_w_r": (1, 0),
    "L2_attn_in_proj_w": (1, 0), "L2_attn_out_proj_w": (1, 0), "L2_attn_Qp_w": (1, 0), "L2_attn_Kp_w": (1, 0),
    "L2_attn_Vp_w": (1, 0), "L2_attn_ff1_w": (1, 0), "L2_attn_ff2_w": (1, 0),
    "L2_ffn_w1_w": (1, 0), "L2_ffn_w2_w": (1, 0), "L2_ffn_h1_w": (1, 0), "L2_ffn_h2_w": (1, 0), "L2_ffn_w3_w": (1, 0),
    "L3_attn_w_qkv": (1, 0), "L3_attn_w_o": (1, 0), "L3_ffn_w_gate": (1, 0), "L3_ffn_w_up": (1, 0), "L3_ffn_w_down": (1, 0),
}


def lay_out(inputs):
    import numpy as np
    arrays = {}
    for name, a in inputs.items():
        a = np.asarray(a)
        if name in TRANSPOSED:
            name, a = name + "T", a.transpose(TRANSPOSED[name])
        arrays[name] = np.ascontiguousarray(a).reshape(a.shape or (1,))
    return arrays


def kernel(**inputs):
    import numpy as np
    import concourse.bacc as bacc
    from concourse.bass_utils import run_bass_kernel_spmd

    nc = bacc.Bacc("TRN2", target_bir_lowering=False, num_devices=1)
    arrays = {"in_" + k: a for k, a in lay_out(inputs).items()}
    I = {k[3:]: nc.dram_tensor(k, a.shape, mybir.dt.from_np(a.dtype), kind="ExternalInput").ap() for k, a in arrays.items()}
    out = nc.dram_tensor("out_0", (1, T, C), F32, kind="ExternalOutput").ap()
    build_program(nc, I, out)
    r = run_bass_kernel_spmd(nc, [arrays], core_ids=[0])
    return r.results[0]["out_0"]
```

```python
from contextlib import ExitStack

import concourse.bass as bass
from concourse import mybir

P = 128
T = 2048
TB = T // P
C = 128
CH = 512
NCH = T // CH

F32 = mybir.dt.float32
BF16 = mybir.dt.bfloat16
I32 = mybir.dt.int32
ALU = mybir.AluOpType
ACT = mybir.ActivationFunctionType
AX = mybir.AxisListType.X
NEG = -1.0e30


class Steps:

    def __init__(self, eng, sem):
        self.eng, self.sem, self.n, self.base = eng, sem, 0, 0

    def __call__(self, ins):
        self.n += 1
        ins.then_inc(self.sem, 1)
        self.eng.wait_ge(self.sem, self.base + self.n)

    def enter(self, i, per, first=0):
        self.outer, self.base, self.per = self.n, (i - first) * per + self.n, per
        self.n = 0

    def leave(self, turns):
        assert self.n == self.per, (self.n, self.per)
        self.n, self.base = self.outer + turns * self.per, 0


class Room:

    def __init__(self, nc, ctx, tag):
        self.nc, self.ctx, self.tag = nc, ctx, tag

    def sb(self, name, shape, dt=F32):
        return self.ctx.enter_context(self.nc.sbuf_tensor(f"{self.tag}_{name}", shape, dt))

    def sem(self, name):
        return self.ctx.enter_context(self.nc.semaphore(f"{self.tag}_{name}"))


class Shared:
    pass


def setup_shared(nc, ctx, g, x_dram):
    r = Room(nc, ctx, "all")
    g.X = r.sb("x", [P, TB, C])
    g.hT = r.sb("hT", [C, T])
    g.ident = r.sb("ident", [P, P])
    g.ones = r.sb("ones", [P, P])
    g.eps = r.sb("eps", [P, 1])
    g.ps = ctx.enter_context(nc.psum_tensor("ps", [P, 8 * CH], F32))
    x_loaded, zeroed, ready = r.sem("x_loaded"), r.sem("ident_zeroed"), r.sem("consts_ready")
    with nc.Block() as block:

        @block.sync
        def _(sp):
            sp.dma_start(g.X[:, :, :], x_dram.rearrange("a (b p) c -> p (a b) c", p=P)).then_inc(x_loaded, 16)
            sp.wait_ge(x_loaded, 16)

        @block.gpsimd
        def _(pool):
            pool.memset(g.ident[:, :], 0.0).then_inc(zeroed, 1)
            pool.wait_ge(zeroed, 1)
            pool.affine_select(out=g.ident[:, :], in_=g.ident[:, :], compare_op=ALU.not_equal, fill=1.0,
                               base=0, pattern=[[-1, P]], channel_multiplier=1).then_inc(ready, 1)

        @block.vector
        def _(dve):
            dve.memset(g.ones[:, :], 1.0).then_inc(ready, 1)
            dve.memset(g.eps[:, :], 1.0e-5).then_inc(ready, 1)


def layernorm_transpose(nc, g, tag, load=None, src=None, affine=None, natural=None, transposed=True):
    src = g.X if src is None else src
    with ExitStack() as ctx:
        r = Room(nc, ctx, tag)
        st = r.sb("bn", [P, TB, 6])
        mv = r.sb("meanvar", [P, TB, 2])
        ve = r.sb("vareps", [P, TB])
        sd = r.sb("std", [P, TB])
        rs = r.sb("rstd", [P, TB])
        tmp = r.sb("newton", [P, TB])
        xn = r.sb("xn", [P, TB, C]) if natural is None else natural
        steps, var_ready, std_ready = r.sem("steps"), r.sem("var_ready"), r.sem("std_ready")
        norm_ready, tr_ready, ht_ready = r.sem("norm_ready"), r.sem("tr_ready"), r.sem("ht_ready")
        loads = r.sem("weights_loaded")
        with nc.Block() as block:

            @block.sync
            def _(sp):
                if load is not None:
                    n = load(sp, loads)
                    sp.wait_ge(loads, 16 * n)

            @block.vector
            def _(dve):
                step = Steps(dve, steps)
                for b in range(TB):
                    last = dve.bn_stats(st[:, b, :], src[:, b, :])
                step(last)
                for b in range(TB):
                    last = dve.bn_aggr(mv[:, b, :], st[:, b, :])
                step(last)
                step(dve.tensor_scalar(ve[:, :], mv[:, :, 1], 1.0e-5, None, ALU.add))
                dve.nop().then_inc(var_ready, 1)
                dve.wait_ge(std_ready, 1)
                step(dve.reciprocal(rs[:, :], sd[:, :]))
                step(dve.tensor_tensor(tmp[:, :], rs[:, :], rs[:, :], ALU.mult))
                step(dve.tensor_tensor(tmp[:, :], tmp[:, :], ve[:, :], ALU.mult))
                step(dve.tensor_scalar(tmp[:, :], tmp[:, :], -0.5, 1.5, ALU.mult, ALU.add))
                step(dve.tensor_tensor(rs[:, :], rs[:, :], tmp[:, :], ALU.mult))
                plain = affine is None
                for b in range(TB):
                    ins = dve.tensor_scalar(xn[:, b, :], src[:, b, :], mv[:, b, 0:1], rs[:, b:b + 1], ALU.subtract, ALU.mult)
                    if plain:
                        ins.then_inc(norm_ready, 1)
                if not plain:
                    step(ins)
                    step(dve.tensor_tensor(xn[:, :, :], xn[:, :, :], affine[0].unsqueeze(1).broadcast_to([P, TB, C]), ALU.mult))
                    dve.tensor_tensor(xn[:, :, :], xn[:, :, :], affine[1].unsqueeze(1).broadcast_to([P, TB, C]), ALU.add).then_inc(norm_ready, TB)
                for q in range(1, NCH if transposed else 1, 2):
                    dve.wait_ge(tr_ready, q + 1)
                    dve.tensor_copy(g.hT[:, q * CH:(q + 1) * CH], g.ps[:, q * CH:(q + 1) * CH]).then_inc(ht_ready, 1)

            @block.scalar
            def _(act):
                act.wait_ge(var_ready, 1)
                act.activation(sd[:, :], ve[:, :], ACT.Sqrt).then_inc(std_ready, 1)
                for q in range(0, NCH if transposed else 0, 2):
                    act.wait_ge(tr_ready, q + 1)
                    act.copy(g.hT[:, q * CH:(q + 1) * CH], g.ps[:, q * CH:(q + 1) * CH]).then_inc(ht_ready, 1)

            @block.tensor
            def _(pe):
                for b in range(TB if transposed else 0):
                    pe.wait_ge(norm_ready, b + 1)
                    last = pe.transpose(g.ps[:, b * P:(b + 1) * P], xn[:, b, :], g.ident[:, :])
                    if b % 4 == 3:
                        last.then_inc(tr_ready, 1)


def bond_attention(nc, g, I):
    NH, HS, BD, W = 16, 8, 16, 64
    HH = P // BD
    PAD = W
    NG = 8
    GD = W // NG
    UW = W + P
    with ExitStack() as ctx:
        r = Room(nc, ctx, "l0a")
        val = r.sb("val", [P, TB, NH, HS])
        valp = r.sb("valp", [W, TB, NH, HS])
        wc = r.sb("wc", [P, 4, C])
        zero = r.sb("zero", [P, 2 * UW])
        band = nc.dram_tensor("l0a_band", [TB, P, NH * UW], F32, kind="Internal").ap()
        band_zeroed = r.sem("band_zeroed")
        lgt = ExitStack()
        rl = Room(nc, lgt, "l0a")
        L = rl.sb("logits", [P, NG, T])
        with ExitStack() as ctx1:
            r1 = Room(nc, ctx1, "l0m")
            A = r1.sb("A", [P, 2, 2, PAD + T])
            Dj = r1.sb("Dj", [P, 2, PAD + T])
            pos = r1.sb("pos", [P, W])
            wb = r1.sb("wb", [P, 2, 2, 2, 32])
            bdo = r1.sb("bdo", [P, 1])
            with ExitStack() as ctx2:
                r2 = Room(nc, ctx2, "l0w")
                wd = r2.sb("wd", [C, 2 * P])
                wv = r2.sb("wv", [C, C])
                wrep = r2.sb("wrep", [P, 2, BD])
                wblk = r2.sb("wblk", [P, 2, P])
                wpos = r2.sb("wpos", [BD, BD])
                wposr = r2.sb("wposr", [BD, HH, BD])
                relT = r2.sb("relT", [BD, W])
                wo = r2.sb("wo", [P, 2])
                bm = r2.sb("bm", [P, HH])
                bd = r2.sb("bd", [P, 1])
                disp = L[:, 0:2, :]

                zr = r2.sem("zeroed")

                def load(sp, s):
                    n = 0

                    def ld(dst, src):
                        nonlocal n
                        n += 1
                        sp.dma_start(dst, src, allow_slow_non_contiguous=True).then_inc(s, 16)
                    ld(wd[:, :], I["L0_attn_W_disp"])
                    ld(wv[:, :], I["L0_attn_W_val"])
                    ld(wpos[:, :], I["L0_attn_W_pos"])
                    ld(relT[:, :], I["L0_attn_rel_pos_embT"])
                    def each_head(dst, src):
                        ld(dst, src.unsqueeze(0).broadcast_to([HH, *src.shape]))
                    each_head(wrep[:, 0, :], I["L0_attn_W_dmg"])
                    each_head(wrep[:, 1, :], I["L0_attn_W_strain"])
                    each_head(wo[:, 0:1], I["L0_attn_W_dmg_out"])
                    each_head(wo[:, 1:2], I["L0_attn_W_bond"])
                    each_head(bd[:, :], I["L0_attn_b_dmg"].rearrange("(a b) -> a b", b=1))
                    ld(bdo[:, :], I["L0_attn_b_dmg_out"].rearrange("(a b) -> a b", b=1).broadcast_to([P, 1]))
                    sp.wait_ge(zr, 3)
                    for k in range(4):
                        ld(wc[32 * k:32 * k + HS, :, :], I["L0_attn_W_cproj"].rearrange("(q k e) c -> k e q c", k=4, e=HS)[k])
                    return n

                made, sel = r2.sem("mask_made"), r2.sem("mask_steps")
                with nc.Block() as block:

                    @block.vector
                    def _(dve):
                        dve.memset(wc[:, :, :], 0.0).then_inc(zr, 1)
                        dve.memset(zero[:, :], 0.0).then_inc(zr, 1)
                        dve.memset(wb[:, :, :, :, :], 0.0).then_inc(zr, 1)
                        dve.memset(A[:, :, :, 0:PAD], 0.0)
                        dve.memset(Dj[:, :, 0:PAD], 0.0)

                    @block.gpsimd
                    def _(pool):
                        pool.memset(bm[:, :], 1.0).then_inc(sel, 1)
                        pool.wait_ge(sel, 1)
                        pool.affine_select(out=bm[:, :], in_=bm[:, :], compare_op=ALU.is_ge, fill=0.0, base=0,
                                           pattern=[[-BD, HH]], channel_multiplier=1).then_inc(sel, 1)
                        pool.wait_ge(sel, 2)
                        pool.affine_select(out=bm[:, :], in_=bm[:, :], compare_op=ALU.is_ge, fill=0.0, base=BD - 1,
                                           pattern=[[BD, HH]], channel_multiplier=-1).then_inc(made, 1)

                layernorm_transpose(nc, g, "ln0", load)

                built, disp_ps, disp_sb = r2.sem("weights_built"), r2.sem("disp_in_psum"), r2.sem("disp_copied")
                a_ps, a_sb = r2.sem("a_in_psum"), r2.sem("a_copied")
                v_ps, v_sb = r2.sem("val_in_psum"), r2.sem("val_copied")
                with nc.Block() as block:

                    @block.sync
                    def _(sp):
                        for b in range(TB):
                            sp.dma_start(band[b].rearrange("p (r u) -> p r u", u=2 * UW),
                                         zero[:, :].unsqueeze(1).broadcast_to([P, NH // 2, 2 * UW])).then_inc(band_zeroed, 16)

                    @block.vector
                    def _(dve):
                        for k in range(2):
                            dve.tensor_tensor(wblk[:, k, :].rearrange("p (h c) -> p h c", c=BD),
                                              wrep[:, k, :].unsqueeze(1).broadcast_to([P, HH, BD]),
                                              bm[:, :].unsqueeze(2).broadcast_to([P, HH, BD]), ALU.mult)
                            for hf in range(2):
                                for par in range(2):
                                    cols = wb[:, k, hf, par, :].rearrange("p (h o) -> p h o", o=2)[:, hf * HH:(hf + 1) * HH, par]
                                    dve.tensor_scalar(cols, bm[:, :], wo[:, k:k + 1], None, ALU.mult)
                        dve.tensor_copy(wposr[:, :, :], wpos[:, :].unsqueeze(1).broadcast_to([BD, HH, BD])).then_inc(built, 1)
                        for hf in range(2):
                            for q in range(2):
                                dve.wait_ge(disp_ps, 2 * hf + q + 1)
                                dve.tensor_copy(disp[:, hf, q * 1024:(q + 1) * 1024],
                                                g.ps[:, hf * T + q * 1024:hf * T + (q + 1) * 1024]).then_inc(disp_sb, 1)
                        for n in range(4):
                            dve.wait_ge(a_ps, n + 1)
                            dve.tensor_copy(A[:, n // 2, n % 2, PAD:], g.ps[:, (n % 2) * T:(n % 2 + 1) * T]).then_inc(a_sb, 1)
                            if n % 2 == 0:
                                dve.wait_ge(a_sb, n + 1)
                                dve.tensor_scalar(Dj[:, n // 2, PAD:], A[:, n // 2, 0, PAD:], bd[:, :], None, ALU.add)
                        for n in range(TB // 4):
                            dve.wait_ge(v_ps, 2 * n + 1)
                            dve.tensor_copy(val[:, 4 * n:4 * n + 4, :, 0:HS],
                                            g.ps[:, 0:CH].rearrange("p (b h e) -> p b h e", b=4, e=HS)).then_inc(v_sb, 1)
                            dve.wait_ge(v_ps, 2 * n + 2)
                            dve.tensor_copy(valp[:, 4 * n:4 * n + 4, :, 0:HS],
                                            g.ps[0:W, CH:2 * CH].rearrange("p (b h e) -> p b h e", b=4, e=HS)).then_inc(v_sb, 1)
                        dve.wait_ge(v_ps, 2 * TB // 4 + 1)
                        dve.tensor_copy(pos[:, :], g.ps[:, 2 * CH:2 * CH + W])

                    @block.tensor
                    def _(pe):
                        for hf in range(2):
                            for q in range(NCH):
                                mm = pe.matmul(g.ps[:, hf * T + q * CH:hf * T + (q + 1) * CH], wd[:, hf * P:(hf + 1) * P],
                                               g.hT[:, q * CH:(q + 1) * CH], start=True, stop=True)
                                if q % 2:
                                    mm.then_inc(disp_ps, 1)
                        pe.wait_ge(built, 1)
                        for n in range(4):
                            pe.wait_ge(disp_sb, 4)
                            if n >= 2:
                                pe.wait_ge(a_sb, n - 1)
                            for q in range(NCH):
                                mm = pe.matmul(g.ps[:, (n % 2) * T + q * CH:(n % 2) * T + (q + 1) * CH], wblk[:, n % 2, :],
                                               disp[:, n // 2, q * CH:(q + 1) * CH], start=True, stop=True)
                            mm.then_inc(a_ps, 1)
                        pe.wait_ge(a_sb, 4)
                        for n in range(TB // 4):
                            if n:
                                pe.wait_ge(v_sb, 2 * n - 1)
                            for b in range(4 * n, 4 * n + 4):
                                mm = pe.matmul(g.ps[:, (b % 4) * P:(b % 4 + 1) * P], g.hT[:, b * P:(b + 1) * P], wv[:, :],
                                               start=True, stop=True)
                            mm.then_inc(v_ps, 1)
                            if n:
                                pe.wait_ge(v_sb, 2 * n)
                            for b in range(4 * n, 4 * n + 4):
                                t0 = max(b * P - W, 0)
                                mm = pe.matmul(g.ps[0:W, CH + (b % 4) * P:CH + (b % 4 + 1) * P], g.hT[:, t0:t0 + W], wv[:, :],
                                               start=True, stop=True)
                            mm.then_inc(v_ps, 1)
                        pe.matmul(g.ps[:, 2 * CH:2 * CH + W], wposr[:, :, :].rearrange("k h c -> k (h c)"), relT[:, :],
                                  start=True, stop=True).then_inc(v_ps, 1)

            ND, NP_, NGB = 3, 2, 2
            dd = r1.sb("diff_dve", [P, ND, T])
            dp = r1.sb("diff_pool", [P, NP_, T])
            ge = r1.sb("gelu", [P, NGB, T])
            th = g.hT
            hb = r1.sb("half_bdo", [P, 1])
            pcur = r1.sb("pos_of_group", [P, GD])
            SPG = 2 * GD * 2
            diff_dve, diff_pool = r1.sem("diff_dve"), r1.sem("diff_pool")
            free_dve, free_pool = r1.sem("free_dve"), r1.sem("free_pool")
            gelu_done, gelu_used = r1.sem("gelu_done"), r1.sem("gelu_used")
            dmg_done, bond_done, tanh_done, logit_done = r1.sem("dmg_done"), r1.sem("bond_done"), r1.sem("tanh_done"), r1.sem("logit_done")
            hb_ready, pos_ready = r1.sem("hb_ready"), r1.sem("pos_ready")
            pool_steps = [s for s in range(SPG) if s % 4 == 3]
            dve_steps = [s for s in range(SPG) if s % 4 != 3]
            NDV, NPO = len(dve_steps), len(pool_steps)
            assert NDV % ND == 0 and NPO % NP_ == 0

            def where(s):
                k, rest = divmod(s, 2 * GD)
                d, hf = divmod(rest, 2)
                return k, d, hf

            with nc.Block() as block:

                def subtract(eng, out, gi, s):
                    k, d, hf = where(s)
                    aj = (Dj[:, hf, :] if k == 0 else A[:, hf, 1, :])
                    at = A[:, hf, k, PAD:PAD + T]
                    return eng.tensor_tensor(out, aj[:, bass.ds(gi * GD + (d + 1), T)], at, ALU.subtract)

                @block.vector
                def _(dve):
                    dve.tensor_scalar(hb[:, :], bdo[:, :], 0.5, None, ALU.mult).then_inc(hb_ready, 1)

                    def logits(gi):
                        dve.wait_ge(tanh_done, gi + 1)
                        dve.wait_ge(bond_done, gi + 1)
                        dve.scalar_tensor_tensor(L[:, bass.ds(gi, 1), :].rearrange("p a t -> p (a t)"), th[:, :], -5.0,
                                                 g.ps[:, T:2 * T], ALU.mult, ALU.add).then_inc(logit_done, 1)

                    def group(gi, first):
                        for n, s in enumerate(dve_steps):
                            if n == ND and not first:
                                logits(gi - 1)
                            if not (first and n < ND):
                                dve.wait_ge(free_dve, gi * NDV + (n + 1 - ND))
                            b = (n + (0 if True else 0))
                            subtract(dve, dd[:, b % ND, :], gi, s).then_inc(diff_dve, 1)
                    group(0, True)
                    with dve.Fori(1, NG) as gi:
                        group(gi, False)
                    logits(NG - 1)

                @block.gpsimd
                def _(pool):
                    def group(gi, first):
                        for n, s in enumerate(pool_steps):
                            if not (first and n < NP_):
                                pool.wait_ge(free_pool, gi * NPO + (n + 1 - NP_))
                            subtract(pool, dp[:, n % NP_, :], gi, s).then_inc(diff_pool, 1)
                    group(0, True)
                    with pool.Fori(1, NG) as gi:
                        group(gi, False)

                @block.scalar
                def _(act):
                    act.wait_ge(hb_ready, 1)

                    def group(gi, first):
                        nd = npo = 0
                        act.copy(pcur[:, :], pos[:, bass.ds(gi * GD, GD)]).then_inc(pos_ready, 1)
                        act.wait_ge(pos_ready, gi + 1)
                        for s in range(SPG):
                            k, d, hf = where(s)
                            if s == SPG // 2 + 2:
                                act.wait_ge(dmg_done, gi + 1)
                                if not first:
                                    act.wait_ge(logit_done, gi)
                                act.activation(th[:, :], g.ps[:, 0:T], ACT.Tanh, bias=hb[:, :], scale=0.5).then_inc(tanh_done, 1)
                            if s in pool_steps:
                                act.wait_ge(diff_pool, gi * NPO + npo + 1)
                                src, fr = dp[:, npo % NP_, :], free_pool
                                npo += 1
                            else:
                                act.wait_ge(diff_dve, gi * NDV + nd + 1)
                                src, fr = dd[:, nd % ND, :], free_dve
                                nd += 1
                            if not (first and s < NGB):
                                act.wait_ge(gelu_used, gi * SPG + (s + 1 - NGB))
                            bias = 0.0 if k == 0 else pcur[:, d:d + 1]
                            act.activation(ge[:, s % NGB, :], src, ACT.Gelu, bias=bias).then_inc(gelu_done, 1)
                            act.wait_ge(gelu_done, gi * SPG + s + 1)
                            act.sem_inc(fr, 1)
                    group(0, True)
                    with act.Fori(1, NG) as gi:
                        group(gi, False)

                @block.tensor
                def _(pe):
                    def group(gi, first):
                        for s in range(SPG):
                            k, d, hf = where(s)
                            pe.wait_ge(gelu_done, gi * SPG + s + 1)
                            if not first and s == 0:
                                pe.wait_ge(tanh_done, gi)
                            if not first and s == SPG // 2:
                                pe.wait_ge(logit_done, gi)
                            j, par = d // 2, d % 2
                            for q in range(NCH):
                                col = k * T + j * CH
                                mm = pe.matmul(g.ps[32 * q:32 * q + 32, col:col + CH], wb[:, k, hf, par, :],
                                               ge[:, s % NGB, q * CH:(q + 1) * CH],
                                               start=(par == 0 and hf == 0), stop=(par == 1 and hf == 1))
                            mm.then_inc(gelu_used, 1)
                            if s == SPG // 2 - 1:
                                pe.wait_ge(gelu_used, gi * SPG + s + 1)
                                pe.sem_inc(dmg_done, 1)
                            if s == SPG - 1:
                                pe.wait_ge(gelu_used, gi * SPG + s + 1)
                                pe.sem_inc(bond_done, 1)
                    group(0, True)
                    with pe.Fori(1, NG) as gi:
                        group(gi, False)

                @block.sync
                def _(sp):
                    sp.wait_ge(band_zeroed, 16 * TB)
        with ExitStack() as ctx3:
            r3 = Room(nc, ctx3, "l0s")
            LT = r3.sb("LT", [P, TB, NH, W])
            mx = r3.sb("mx", [P, TB, NH])
            sm = r3.sb("sm", [P, TB, NH])
            tr, ev, masked = r3.sem("transposed"), r3.sem("copied"), r3.sem("masked")
            steps, maxd, expd, rcpd = r3.sem("steps"), r3.sem("max_done"), r3.sem("exp_done"), r3.sem("sum_inverted")
            subd = [r3.sem("max_subtracted%d" % q) for q in range(4)]
            normed = [r3.sem("normalised%d" % q) for q in range(4)]

            def scale(eng, q, by, op):
                b = slice(4 * q, 4 * q + 4)
                lt = LT[:, b, :, :].rearrange("p b h d -> p (b h) d")
                return eng.tensor_tensor(lt, lt, by[:, b, :].rearrange("p b h -> p (b h)").unsqueeze(2).broadcast_to([P, 4 * NH, W]), op)
            band_written = r3.sem("band_written")
            with nc.Block() as block:

                @block.tensor
                def _(pe):
                    for n in range(NCH * NG):
                        r_, gi = divmod(n, NG)
                        if n >= 8:
                            pe.wait_ge(ev, n - 7)
                        for j in range(4):
                            mm = pe.transpose(g.ps[:, (n % 8) * CH + j * P:(n % 8) * CH + (j + 1) * P],
                                              L[:, gi, j * CH + r_ * P:j * CH + (r_ + 1) * P], g.ident[:, :])
                        mm.then_inc(tr, 1)

                @block.scalar
                def _(act):
                    for n in range(NCH * NG):
                        r_, gi = divmod(n, NG)
                        act.wait_ge(tr, n + 1)
                        act.copy(LT[:, 4 * r_:4 * r_ + 4, :, gi * GD:(gi + 1) * GD].rearrange("p q h (j o) -> p (q h) j o", o=2),
                                 g.ps[:, (n % 8) * CH:(n % 8 + 1) * CH].rearrange("p (j m o) -> p m j o", j=4, o=2)).then_inc(ev, 1)
                    for q in range(4):
                        act.wait_ge(subd[q], 1)
                        act.activation(LT[:, 4 * q:4 * q + 4, :, :], LT[:, 4 * q:4 * q + 4, :, :], ACT.Exp).then_inc(expd, 1)

                @block.gpsimd
                def _(pool):
                    pool.wait_ge(ev, NG)
                    pool.affine_select(out=LT[:, 0, :, :], in_=LT[:, 0, :, :], compare_op=ALU.is_ge, fill=NEG,
                                       base=1 - W, pattern=[[0, NH], [1, W]], channel_multiplier=1).then_inc(masked, 1)
                    pool.wait_ge(maxd, 1)
                    scale(pool, 0, mx, ALU.subtract).then_inc(subd[0], 1)
                    pool.wait_ge(rcpd, 2)
                    scale(pool, 1, sm, ALU.mult).then_inc(normed[1], 1)

                @block.vector
                def _(dve):
                    step = Steps(dve, steps)

                    def exps(q):
                        b = slice(4 * q, 4 * q + 4)
                        dve.wait_ge(expd, q + 1)
                        step(dve.tensor_reduce(sm[:, b, :], LT[:, b, :, :], AX, ALU.add))
                        step(dve.reciprocal(sm[:, b, :], sm[:, b, :]))
                        dve.sem_inc(rcpd, 1)
                        if q != 1:
                            scale(dve, q, sm, ALU.mult).then_inc(normed[q], 1)
                    for q in range(4):
                        b = slice(4 * q, 4 * q + 4)
                        dve.wait_ge(ev, NG * (q + 1))
                        if q == 0:
                            dve.wait_ge(masked, 1)
                        step(dve.tensor_reduce(mx[:, b, :], LT[:, b, :, :], AX, ALU.max))
                        if q == 0:
                            dve.sem_inc(maxd, 1)
                        else:
                            scale(dve, q, mx, ALU.subtract).then_inc(subd[q], 1)
                        if q:
                            exps(q - 1)
                    exps(3)

                @block.sync
                def _(sp):
                    for i in range(TB):
                        sp.wait_ge(normed[i // 4], 1)
                        b = 4 * (i % 4) + i // 4
                        dst = bass.AP(band.tensor, b * P * NH * UW + 1, [[NH * UW + 1, P], [UW, NH], [1, W]])
                        sp.dma_start(dst, LT[:, i, :, :]).then_inc(band_written, 16)
                    sp.wait_ge(band_written, 16 * TB)
        lgt.close()
        with ExitStack() as ctx4:
            r4 = Room(nc, ctx4, "l0v")
            vc = r4.sb("vc", [P, TB, NH, 32])
            vp = r4.sb("vp", [W, TB, NH, 32])
            filled, placed = r4.sem("padding_zeroed"), r4.sem("values_placed")
            bn = r4.sb("band", [P, 2, NH, UW])
            bt = r4.sb("bandT", [P, 2, NH // 4, 4, P])
            bp = r4.sb("bandTp", [W, 2, NH // 4, 4, P])
            ot = r4.sb("oT", [P, 2, 4, P])
            loaded = [r4.sem("band_loaded0"), r4.sem("band_loaded1")]
            tc_, tp, evc, evp = r4.sem("cur_transposed"), r4.sem("prev_transposed"), r4.sem("cur_copied"), r4.sem("prev_copied")
            ops, ocp, yps, xad = r4.sem("values_weighted"), r4.sem("o_copied"), r4.sem("y_in_psum"), r4.sem("x_added")
            QH = NH // 4
            with nc.Block() as block:

                @block.sync
                def _(sp):
                    for b in range(TB):
                        if b >= 2:
                            sp.wait_ge(tp, QH * (b - 1))
                        sp.dma_start(bn[:, b % 2, :, :].rearrange("p h u -> p (h u)"), band[b]).then_inc(loaded[b % 2], 16)
                    sp.wait_ge(loaded[0], 16 * TB // 2)
                    sp.wait_ge(loaded[1], 16 * TB // 2)

                @block.gpsimd
                def _(pool):
                    for hf in range(2):
                        b = slice(hf * TB // 2, (hf + 1) * TB // 2)
                        pool.memset(vc[:, b, :, HS:32], 0.0).then_inc(filled, 1)
                        pool.memset(vp[:, b, :, HS:32], 0.0).then_inc(filled, 1)

                @block.tensor
                def _(pe):
                    def transposes(b):
                        pe.wait_ge(loaded[b % 2], 16 * (b // 2 + 1))
                        for hq in range(QH):
                            n = b * QH + hq
                            if n >= 2:
                                pe.wait_ge(evc, n - 1)
                            for k in range(4):
                                mm = pe.transpose(g.ps[:, (n % 2) * CH + k * P:(n % 2) * CH + (k + 1) * P],
                                                  bn[:, b % 2, 4 * hq + k, W:UW], g.ident[:, :])
                            mm.then_inc(tc_, 1)
                            if n >= 2:
                                pe.wait_ge(evp, n - 1)
                            for k in range(4):
                                mm = pe.transpose(g.ps[0:W, (2 + n % 2) * CH + k * P:(2 + n % 2) * CH + (k + 1) * P],
                                                  bn[:, b % 2, 4 * hq + k, 0:W], g.ident[:, :])
                            mm.then_inc(tp, 1)

                    def values(b):
                        pe.wait_ge(filled, 2 if b < TB // 2 else 4)
                        pe.wait_ge(placed, 2)
                        pe.wait_ge(evc, QH * (b + 1))
                        pe.wait_ge(evp, QH * (b + 1))
                        if b >= 2:
                            pe.wait_ge(ocp, b - 1)
                        for hq in range(QH):
                            for k in range(4):
                                o = g.ps[32 * k:32 * k + 32, (4 + b % 2) * CH + hq * P:(4 + b % 2) * CH + (hq + 1) * P]
                                pe.matmul(o, vc[:, b, 4 * hq + k, :], bt[:, b % 2, hq, k, :], start=True, stop=False)
                                mm = pe.matmul(o, vp[:, b, 4 * hq + k, :], bp[:, b % 2, hq, k, :], start=False, stop=True)
                        mm.then_inc(ops, 1)

                    def project(b):
                        pe.wait_ge(ocp, b + 1)
                        if b >= 2:
                            pe.wait_ge(xad, b - 1)
                        for hq in range(QH):
                            mm = pe.matmul(g.ps[:, (6 + b % 2) * CH:(6 + b % 2) * CH + C], ot[:, b % 2, hq, :], wc[:, hq, :],
                                           start=(hq == 0), stop=(hq == QH - 1))
                        mm.then_inc(yps, 1)
                    for b in range(TB + 2):
                        if b < TB:
                            transposes(b)
                        if 1 <= b <= TB:
                            values(b - 1)
                        if b >= 2:
                            project(b - 2)

                @block.scalar
                def _(act):
                    act.copy(vc[:, :, :, 0:HS], val[:, :, :, :]).then_inc(placed, 1)
                    for b in range(TB):
                        for hq in range(QH):
                            n = b * QH + hq
                            act.wait_ge(tc_, n + 1)
                            if b >= 2 and hq == 0:
                                act.wait_ge(ops, b - 1)
                            act.copy(bt[:, b % 2, hq, :, :].rearrange("p k t -> p (k t)"),
                                     g.ps[:, (n % 2) * CH:(n % 2 + 1) * CH]).then_inc(evc, 1)

                @block.vector
                def _(dve):
                    def finish(b):
                        dve.wait_ge(yps, b + 1)
                        dve.tensor_tensor(g.X[:, b, :], g.X[:, b, :], g.ps[:, (6 + b % 2) * CH:(6 + b % 2) * CH + C],
                                          ALU.add).then_inc(xad, 1)
                    dve.tensor_copy(vp[:, :, :, 0:HS], valp[:, :, :, :]).then_inc(placed, 1)
                    for b in range(TB + 2):
                        if b < TB:
                            for hq in range(QH):
                                n = b * QH + hq
                                dve.wait_ge(tp, n + 1)
                                if b >= 2 and hq == 0:
                                    dve.wait_ge(ops, b - 1)
                                dve.tensor_copy(bp[:, b % 2, hq, :, :].rearrange("p k t -> p (k t)"),
                                                g.ps[0:W, (2 + n % 2) * CH:(2 + n % 2 + 1) * CH]).then_inc(evp, 1)
                        if 1 <= b <= TB:
                            dve.wait_ge(ops, b)
                            if b >= 3:
                                dve.wait_ge(yps, b - 2)
                            dve.tensor_copy(ot[:, (b - 1) % 2, :, :].rearrange("p k t -> p (k t)"),
                                            g.ps[:, (4 + (b - 1) % 2) * CH:(5 + (b - 1) % 2) * CH]).then_inc(ocp, 1)
                        if b >= 2:
                            finish(b - 2)


def masked_ffn(nc, g, I):
    D1, D2, DL = 8, 64, 64
    DF = D1 * D2
    KC = DF // P
    with ExitStack() as ctx:
        r = Room(nc, ctx, "l0f")
        m1 = r.sb("m1", [C, DL])
        m2 = r.sb("m2", [DL + 1, DF])
        w1 = r.sb("w1", [C, DF])
        w2 = r.sb("w2", [P, KC, C])
        b2 = r.sb("b2", [P, C])
        pri = r.sb("pri", [P, D2])
        lr = r.sb("lr", [DL + 1, T])

        def load(sp, s):
            sp.dma_start(m1[:, :], I["L0_ffn_m1"]).then_inc(s, 16)
            sp.dma_start(m2[0:DL, :], I["L0_ffn_m2"].rearrange("l x y -> l (x y)")).then_inc(s, 16)
            sp.dma_start(m2[DL:DL + 1, :], I["L0_ffn_mb"].rearrange("(a x) y -> a (x y)", a=1)).then_inc(s, 16)
            sp.dma_start(w1[:, :], I["L0_ffn_w1"].rearrange("d x y -> d (x y)")).then_inc(s, 16)
            sp.dma_start(w2[:, :, :], I["L0_ffn_w2T"].rearrange("x y c -> (x y) c").rearrange("(k p) c -> p k c", p=P)).then_inc(s, 16)
            sp.dma_start(b2[:, :], I["L0_ffn_b2"].rearrange("(a c) -> a c", a=1).broadcast_to([P, C])).then_inc(s, 16)
            return 6
        layernorm_transpose(nc, g, "ln1", load)
        mx = r.sb("mx", [P, 2, D1])
        px = r.sb("px", [P, 2, D1])
        eq = r.sb("eq", [P, 2, DF])
        pr = r.sb("pr", [P, 2, DF])
        mid = r.sb("mid", [P, 2, DF])
        midT = r.sb("midT", [P, 2, DF])
        lr_ps, lr_sb, const, steps = r.sem("lr_in_psum"), r.sem("lr_copied"), r.sem("const_ready"), r.sem("steps")
        lgt, up, hot, tied, act_ready = r.sem("logits_in_psum"), r.sem("mid_in_psum"), r.sem("equal_found"), r.sem("priority_ready"), r.sem("mid_masked")
        tr, mt, yps, xad, eqd = r.sem("mid_transposed"), r.sem("midT_copied"), r.sem("y_in_psum"), r.sem("x_added"), r.sem("logits_read")
        xb = r.sem("x_biased")
        with nc.Block() as block:

            @block.gpsimd
            def _(pool):
                pool.iota(pri[:, :], [[-1, D2]], base=D2, channel_multiplier=0, allow_small_or_imprecise_dtypes=True).then_inc(const, 1)
                pool.tensor_tensor(g.X[:, :, :], g.X[:, :, :], b2[:, :].unsqueeze(1).broadcast_to([P, TB, C]), ALU.add).then_inc(xb, 1)
                pool.wait_ge(const, 2)
                for b in range(TB):
                    pool.wait_ge(hot, b + 1)
                    if b >= 2:
                        pool.wait_ge(act_ready, b - 1)
                    pool.tensor_tensor(pr[:, b % 2, :].rearrange("p (x y) -> p x y", x=D1), eq[:, b % 2, :].rearrange("p (x y) -> p x y", x=D1),
                                       pri[:, :].unsqueeze(1).broadcast_to([P, D1, D2]), ALU.mult).then_inc(tied, 1)

            @block.tensor
            def _(pe):
                for q in range(NCH):
                    mm = pe.matmul(g.ps[0:DL, q * CH:(q + 1) * CH], m1[:, :], g.hT[:, q * CH:(q + 1) * CH], start=True, stop=True)
                mm.then_inc(lr_ps, 1)
                pe.wait_ge(lr_sb, 1)
                pe.wait_ge(const, 2)

                def front(b):
                    if b >= 2:
                        pe.wait_ge(eqd, b - 1)
                    pe.matmul(g.ps[:, (b % 2) * CH:(b % 2 + 1) * CH], lr[:, b * P:(b + 1) * P], m2[:, :], start=True, stop=True).then_inc(lgt, 1)
                    if b >= 2:
                        pe.wait_ge(act_ready, b - 1)
                    pe.matmul(g.ps[:, (2 + b % 2) * CH:(3 + b % 2) * CH], g.hT[:, b * P:(b + 1) * P], w1[:, :], start=True, stop=True).then_inc(up, 1)

                def back(b):
                    pe.wait_ge(act_ready, b + 1)
                    if b >= 2:
                        pe.wait_ge(mt, b - 1)
                    for k in range(KC):
                        mm = pe.transpose(g.ps[:, (4 + b % 2) * CH + k * P:(4 + b % 2) * CH + (k + 1) * P], mid[:, b % 2, k * P:(k + 1) * P], g.ident[:, :])
                    mm.then_inc(tr, 1)

                def last(b):
                    pe.wait_ge(mt, b + 1)
                    if b >= 2:
                        pe.wait_ge(xad, b - 1)
                    for k in range(KC):
                        mm = pe.matmul(g.ps[:, (6 + b % 2) * CH:(6 + b % 2) * CH + C], midT[:, b % 2, k * P:(k + 1) * P], w2[:, k, :],
                                       start=(k == 0), stop=(k == KC - 1))
                    mm.then_inc(yps, 1)
                for b in range(TB + 2):
                    if b < TB:
                        front(b)
                    if 1 <= b <= TB:
                        back(b - 1)
                    if b >= 2:
                        last(b - 2)

            @block.scalar
            def _(act):
                act.wait_ge(lr_ps, 1)
                act.copy(lr[0:DL, :], g.ps[0:DL, 0:T]).then_inc(lr_sb, 1)
                for b in range(TB):
                    act.wait_ge(tr, b + 1)
                    if b >= 2:
                        act.wait_ge(yps, b - 1)
                    act.copy(midT[:, b % 2, :], g.ps[:, (4 + b % 2) * CH:(5 + b % 2) * CH]).then_inc(mt, 1)

            @block.vector
            def _(dve):
                step = Steps(dve, steps)
                dve.memset(lr[DL:DL + 1, :], 1.0).then_inc(const, 1)
                grp = lambda ap: ap.rearrange("p (x y) -> p x y", x=D1)

                def mask(b):
                    lg = grp(g.ps[:, (b % 2) * CH:(b % 2 + 1) * CH])
                    dve.wait_ge(lgt, b + 1)
                    step(dve.tensor_reduce(mx[:, b % 2, :], lg, AX, ALU.max))
                    if b >= 2:
                        dve.wait_ge(tied, b - 1)
                    ins = dve.tensor_tensor(grp(eq[:, b % 2, :]), lg, mx[:, b % 2, :].unsqueeze(2).broadcast_to([P, D1, D2]), ALU.is_equal)
                    step(ins)
                    dve.nop().then_inc(hot, 1)
                    dve.nop().then_inc(eqd, 1)

                def pick(b):
                    dve.wait_ge(tied, b + 1)
                    p3 = grp(pr[:, b % 2, :])
                    step(dve.tensor_reduce(px[:, b % 2, :], p3, AX, ALU.max))
                    step(dve.tensor_tensor(grp(eq[:, b % 2, :]), p3, px[:, b % 2, :].unsqueeze(2).broadcast_to([P, D1, D2]), ALU.is_equal))
                    dve.wait_ge(up, b + 1)
                    if b >= 2:
                        dve.wait_ge(tr, b - 1)
                    dve.scalar_tensor_tensor(mid[:, b % 2, :], g.ps[:, (2 + b % 2) * CH:(3 + b % 2) * CH], 0.0, eq[:, b % 2, :],
                                             ALU.max, ALU.mult).then_inc(act_ready, 1)

                def finish(b):
                    dve.wait_ge(yps, b + 1)
                    dve.tensor_tensor(g.X[:, b, :], g.X[:, b, :], g.ps[:, (6 + b % 2) * CH:(6 + b % 2) * CH + C], ALU.add).then_inc(xad, 1)
                for b in range(TB + 3):
                    if b < TB:
                        mask(b)
                    if 1 <= b <= TB:
                        pick(b - 1)
                    if b == 3:
                        dve.wait_ge(xb, 1)
                    if b >= 3:
                        finish(b - 3)


def mamba(nc, g, I):
    DI, NS, KW, R = 256, 16, 4, 8
    HV = DI // P
    DIRS = ("f", "r")
    PADT = KW - 1
    NB = 2 * NS
    with ExitStack() as ctx:
        r = Room(nc, ctx, "l1a")
        win = r.sb("win", [C, 2 * DI])
        wout = r.sb("wout", [P, HV, C])
        cw = r.sb("cw", [P, 2, HV, KW])
        cb = r.sb("cb", [P, 2, HV])
        wx = r.sb("wx", [P, 2, HV, R + NB])
        wdt = r.sb("wdt", [R, 2, DI])
        bdt = r.sb("bdt", [P, 2, HV])
        Al = r.sb("A", [P, 2, HV, NS])
        Dp = r.sb("D", [P, 2, HV])
        xc = r.sb("xc", [P, 2, HV, T])
        dt = r.sb("dt", [P, 2, HV, T])
        dtx = r.sb("dtx", [P, 2, HV, T])
        bc = r.sb("bc", [3 * NB, 2, T], BF16)
        sel = r.sb("sel", [3 * NB, NB], BF16)

        def load(sp, s):
            n = 0

            def ld(dst, src):
                nonlocal n
                n += 1
                sp.dma_start(dst, src, allow_slow_non_contiguous=True).then_inc(s, 16)
            ld(win[:, :], I["L1_attn_in_proj_wT"])
            ld(wout[:, :, :], I["L1_attn_out_proj_wT"].rearrange("(h p) c -> p h c", p=P))
            for i, d in enumerate(DIRS):
                ld(cw[:, i, :, :], I[f"L1_attn_conv_w_{d}"].rearrange("(h p) k -> p h k", p=P))
                ld(cb[:, i, :], I[f"L1_attn_conv_b_{d}"].rearrange("(h p) -> p h", p=P))
                ld(wx[:, i, :, :], I[f"L1_attn_x_proj_w_{d}T"].rearrange("(h p) k -> p h k", p=P))
                ld(wdt[:, i, :], I[f"L1_attn_dt_proj_w_{d}T"])
                ld(bdt[:, i, :], I[f"L1_attn_dt_proj_b_{d}"].rearrange("(h p) -> p h", p=P))
                ld(Al[:, i, :, :], I[f"L1_attn_A_log_{d}"].rearrange("(h p) n -> p h n", p=P))
                ld(Dp[:, i, :], I[f"L1_attn_D_{d}"].rearrange("(h p) -> p h", p=P))
            return n
        layernorm_transpose(nc, g, "ln2", load)

        with ExitStack() as ctx1:
            r1 = Room(nc, ctx1, "l1p")
            xi = r1.sb("xi", [P, HV, PADT + T + PADT])
            v = r1.sb("v", [P, T])
            e = r1.sb("e", [P, T])
            u = r1.sb("u", [P, T])
            x3 = r1.sb("x3", [3 * NB, T])
            hi = r1.sb("hi", [3 * NB, T], BF16)
            mid = r1.sb("mid", [3 * NB, T], BF16)
            wx3 = r1.sb("wx3", [P, 2, HV, 3 * NB])
            xdt = r1.sb("xdt", [R, T])
            sidx = r1.sb("sidx", [3 * NB, NB])
            xps, xcp, ready, convd, sil = r1.sem("x_in_psum"), r1.sem("x_copied"), r1.sem("pads_ready"), r1.sem("conv_done"), r1.sem("silu_done")
            bcps, bccp, dtps, dtcp, vps, vcp = r1.sem("bc_in_psum"), r1.sem("bc_copied"), r1.sem("dt_in_psum"), r1.sem("dt_copied"), r1.sem("v_in_psum"), r1.sem("v_copied")
            ed, ud, ld_, steps, asteps, dtd, w3, sels = r1.sem("exp_done"), r1.sem("u_done"), r1.sem("ln_done"), r1.sem("steps"), r1.sem("act_steps"), r1.sem("dt_done"), r1.sem("wx3_ready"), r1.sem("sel_steps")
            tails, aready, splitd = r1.sem("v_read"), r1.sem("a_exp"), r1.sem("split_done")
            with nc.Block() as block:

                @block.gpsimd
                def _(pool):
                    pool.memset(sidx[:, :], 0.0).then_inc(sels, 1)
                    for k in range(3):
                        pool.wait_ge(sels, k + 1)
                        pool.affine_select(out=sidx[:, :], in_=sidx[:, :], compare_op=ALU.not_equal, fill=1.0, base=-k * NB,
                                           pattern=[[-1, NB]], channel_multiplier=1).then_inc(sels, 1)
                    pool.wait_ge(sels, 4)
                    pool.tensor_copy(sel[:, :], sidx[:, :]).then_inc(sels, 1)

                @block.tensor
                def _(pe):
                    for h in range(HV):
                        for q in range(NCH):
                            mm = pe.matmul(g.ps[:, h * T + q * CH:h * T + (q + 1) * CH], win[:, h * P:(h + 1) * P],
                                           g.hT[:, q * CH:(q + 1) * CH], start=True, stop=True)
                        mm.then_inc(xps, 1)
                    pe.wait_ge(w3, 1)
                    pe.wait_ge(xcp, 2)
                    for i in range(2):
                        pe.wait_ge(sil, 2 * (i + 1))
                        if i:
                            pe.wait_ge(vcp, 2)
                        for q in range(NCH):
                            for h in range(HV):
                                mm = pe.matmul(g.ps[0:3 * NB, q * CH:(q + 1) * CH], wx3[:, i, h, :], xc[:, i, h, q * CH:(q + 1) * CH],
                                               start=(h == 0), stop=(h == HV - 1))
                        mm.then_inc(bcps, 1)
                        for q in range(NCH):
                            for h in range(HV):
                                mm = pe.matmul(g.ps[0:R, T + q * CH:T + (q + 1) * CH], wx[:, i, h, 0:R], xc[:, i, h, q * CH:(q + 1) * CH],
                                               start=(h == 0), stop=(h == HV - 1))
                        mm.then_inc(dtps, 1)
                        pe.wait_ge(dtcp, i + 1)
                        pe.wait_ge(bccp, i + 1)
                        for h in range(HV):
                            for q in range(NCH):
                                mm = pe.matmul(g.ps[:, h * T + q * CH:h * T + (q + 1) * CH], wdt[:, i, h * P:(h + 1) * P],
                                               xdt[:, q * CH:(q + 1) * CH], start=True, stop=True)
                            mm.then_inc(vps, 1)

                @block.scalar
                def _(act):
                    act.activation(Al[:, :, :, :], Al[:, :, :, :], ACT.Exp).then_inc(aready, 1)
                    for h in range(HV):
                        act.wait_ge(xps, h + 1)
                        act.copy(xi[:, h, PADT:PADT + T], g.ps[:, h * T:(h + 1) * T]).then_inc(xcp, 1)
                    for n in range(2 * HV):
                        act.wait_ge(convd, n + 1)
                        act.activation(xc[:, n // HV, n % HV, :], xc[:, n // HV, n % HV, :], ACT.Silu).then_inc(sil, 1)
                    for i in range(2):
                        act.wait_ge(bcps, i + 1)
                        act.copy(x3[:, :], g.ps[0:3 * NB, 0:T]).then_inc(bccp, 1)
                        act.wait_ge(dtps, i + 1)
                        act.copy(xdt[:, :], g.ps[0:R, T:2 * T]).then_inc(dtcp, 1)
                        for h in range(HV):
                            n = HV * i + h
                            act.wait_ge(vps, n + 1)
                            if n:
                                act.wait_ge(dtd, n)
                            act.activation(v[:, :], g.ps[:, h * T:(h + 1) * T], ACT.Identity, bias=bdt[:, i, h:h + 1]).then_inc(asteps, 1)
                            act.activation(e[:, :], g.ps[:, h * T:(h + 1) * T], ACT.Abs, bias=bdt[:, i, h:h + 1]).then_inc(vcp, 1)
                            act.wait_ge(vcp, n + 1)
                            act.activation(e[:, :], e[:, :], ACT.Exp, scale=-1.0).then_inc(ed, 1)
                            act.wait_ge(ud, n + 1)
                            act.activation(dt[:, i, h, :], u[:, :], ACT.Ln).then_inc(ld_, 1)

                @block.vector
                def _(dve):
                    step = Steps(dve, steps)
                    dve.memset(xi[:, :, 0:PADT], 0.0)
                    step(dve.memset(xi[:, :, PADT + T:], 0.0))
                    dve.wait_ge(aready, 1)
                    step(dve.tensor_scalar(Al[:, :, :, :], Al[:, :, :, :], -1.0, None, ALU.mult))
                    for k in range(3):
                        last = dve.tensor_copy(wx3[:, :, :, k * NB:(k + 1) * NB], wx[:, :, :, R:R + NB])
                    last.then_inc(w3, 1)
                    for n in range(2 * HV):
                        i, h = divmod(n, HV)
                        dve.wait_ge(xcp, h + 1)
                        at = [(k if i == 0 else 2 * PADT - k) for k in range(KW)]
                        step(dve.tensor_scalar(xc[:, i, h, :], xi[:, h, at[0]:at[0] + T], cw[:, i, h, 0:1], cb[:, i, h:h + 1], ALU.mult, ALU.add))
                        for k in range(1, KW):
                            ins = dve.scalar_tensor_tensor(xc[:, i, h, :], xi[:, h, at[k]:at[k] + T], cw[:, i, h, k:k + 1], xc[:, i, h, :],
                                                           ALU.mult, ALU.add)
                            if k < KW - 1:
                                step(ins)
                        ins.then_inc(convd, 1)
                    for i in range(2):
                        dve.wait_ge(bccp, i + 1)
                        step(dve.tensor_copy(hi[:, :], x3[:, :]))
                        step(dve.tensor_tensor(x3[:, :], x3[:, :], hi[:, :], ALU.subtract))
                        step(dve.tensor_copy(mid[:, :], x3[:, :]))
                        dve.tensor_copy(bc[0:NB, i, :], hi[0:NB, :])
                        dve.tensor_copy(bc[NB:2 * NB, i, :], mid[NB:2 * NB, :])
                        step(dve.tensor_tensor(x3[:, :], x3[:, :], mid[:, :], ALU.subtract))
                        dve.tensor_copy(bc[2 * NB:3 * NB, i, :], x3[2 * NB:3 * NB, :]).then_inc(splitd, 1)
                        dve.wait_ge(splitd, i + 1)
                        for h in range(HV):
                            n = HV * i + h
                            dve.wait_ge(ed, n + 1)
                            dve.tensor_scalar(u[:, :], e[:, :], 1.0, None, ALU.add).then_inc(ud, 1)
                            dve.wait_ge(ud, n + 1)
                            dve.wait_ge(ld_, n + 1)
                            step(dve.scalar_tensor_tensor(u[:, :], u[:, :], 1.0, e[:, :], ALU.subtract, ALU.subtract))
                            step(dve.tensor_tensor(dt[:, i, h, :], dt[:, i, h, :], u[:, :], ALU.subtract))
                            dve.wait_ge(asteps, n + 1)
                            step(dve.scalar_tensor_tensor(dt[:, i, h, :], v[:, :], 0.0, dt[:, i, h, :], ALU.max, ALU.add))
                            dve.tensor_tensor(dtx[:, i, h, :], dt[:, i, h, :], xc[:, i, h, :], ALU.mult).then_inc(dtd, 1)

        steps_ = [(h, i, n) for h in range(HV) for i in range(2) for n in range(NS)]
        M = len(steps_)
        U = r.sb("U", [P, HV, T])
        with ExitStack() as ctx2:
            r2 = Room(nc, ctx2, "l1s")
            dA = r2.sb("dA", [P, 2, T])
            Bs = r2.sb("Bs", [P, 2, T])
            NHB, AHEAD = 3, 3
            hb = r2.sb("h", [P, NHB, T])
            hc = (r2.sb("hc", [P, T]), U[:, 1, :])
            dad, bps, bcp, dbx, scd = r2.sem("dA_done"), r2.sem("b_in_psum"), r2.sem("b_copied"), r2.sem("dbx_done"), r2.sem("scan_done")
            cps, hcd, accd, ud, s1 = r2.sem("c_in_psum"), r2.sem("hc_done"), r2.sem("accumulated"), r2.sem("u_read"), r2.sem("steps")
            with nc.Block() as block:

                @block.tensor
                def _(pe):
                    def spread(bank, sem, row, i, q):
                        pe.matmul(g.ps[:, bank * CH:(bank + 1) * CH], sel[:, row:row + 1].broadcast_to([3 * NB, P]),
                                  bc[:, i, q * CH:(q + 1) * CH], start=True, stop=True).then_inc(sem, 1)

                    def put_b(m, q):
                        if m >= M:
                            return
                        h, i, n = steps_[m]
                        k = m * NCH + q
                        if k >= 2:
                            pe.wait_ge(bcp, k - 1)
                        spread(4 + k % 2, bps, n, i, q)

                    def put_c(m, q):
                        h, i, n = steps_[m]
                        k = m * NCH + q
                        if k >= 2:
                            pe.wait_ge(hcd, k - 1)
                        spread(6 + k % 2, cps, NS + n, i, q)

                    def add(m, q):
                        if m < 0:
                            return
                        h, i, n = steps_[m]
                        pe.wait_ge(hcd, m * NCH + q + 1)
                        first, last = (i, n) == (0, 0), (i, n) == (1, NS - 1)
                        if first and h:
                            pe.wait_ge(ud, h)
                        mm = pe.matmul(g.ps[:, q * CH:(q + 1) * CH], g.ident[:, :], hc[m % 2][:, q * CH:(q + 1) * CH],
                                       start=first, stop=last)
                        if q == NCH - 1:
                            mm.then_inc(accd, 1)
                    for m in range(AHEAD):
                        for q in range(NCH):
                            put_b(m, q)
                    for m in range(M):
                        put_c(m, 0)
                        put_c(m, 1)
                        add(m - 1, 0)
                        put_b(m + AHEAD, 0)
                        put_c(m, 2)
                        put_c(m, 3)
                        for q in range(1, NCH):
                            add(m - 1, q)
                            put_b(m + AHEAD, q)
                    for q in range(NCH):
                        add(M - 1, q)

                @block.scalar
                def _(act):
                    for m, (h, i, n) in enumerate(steps_):
                        if m >= 2:
                            act.wait_ge(dbx, m - 1)
                        for q in range(NCH):
                            act.wait_ge(bps, m * NCH + q + 1)
                            act.copy(Bs[:, m % 2, q * CH:(q + 1) * CH], g.ps[:, (4 + q % 2) * CH:(5 + q % 2) * CH]).then_inc(bcp, 1)
                        if m >= 2:
                            act.wait_ge(scd, m - 1)
                        act.activation(dA[:, m % 2, :], dt[:, i, h, :], ACT.Exp, scale=Al[:, i, h, n:n + 1]).then_inc(dad, 1)

                @block.gpsimd
                def _(pool):
                    for m, (h, i, n) in enumerate(steps_):
                        pool.wait_ge(bcp, NCH * (m + 1))
                        if m >= NHB:
                            pool.wait_ge(hcd, NCH * (m - NHB + 1))
                        pool.tensor_tensor(hb[:, m % NHB, :], dtx[:, i, h, :], Bs[:, m % 2, :], ALU.mult).then_inc(dbx, 1)

                @block.vector
                def _(dve):
                    step = Steps(dve, s1)

                    def half_sum(h):
                        dve.wait_ge(accd, 2 * NS * (h + 1))
                        step(dve.scalar_tensor_tensor(U[:, h, :], xc[:, 0, h, :], Dp[:, 0, h:h + 1], g.ps[:, 0:T], ALU.mult, ALU.add))
                        dve.nop().then_inc(ud, 1)
                        step(dve.scalar_tensor_tensor(U[:, h, :], xc[:, 1, h, :], Dp[:, 1, h:h + 1], U[:, h, :], ALU.mult, ALU.add))
                    def scan(m):
                        h, i, n = steps_[m]
                        dve.wait_ge(dbx, m + 1)
                        dve.wait_ge(dad, m + 1)
                        view = slice(None, None, -1) if i else slice(None)
                        dve.tensor_tensor_scan(hb[:, m % NHB, view], dA[:, m % 2, view], hb[:, m % NHB, view], 0.0, ALU.mult, ALU.add).then_inc(scd, 1)

                    def weigh(m, q):
                        k = m * NCH + q
                        dve.wait_ge(cps, k + 1)
                        dve.tensor_tensor(hc[m % 2][:, q * CH:(q + 1) * CH], hb[:, m % NHB, q * CH:(q + 1) * CH],
                                          g.ps[:, (6 + k % 2) * CH:(7 + k % 2) * CH], ALU.mult).then_inc(hcd, 1)
                    scan(0)
                    for m in range(M):
                        dve.wait_ge(scd, m + 1)
                        if m >= 2:
                            dve.wait_ge(accd, m - 1)
                        weigh(m, 0)
                        weigh(m, 1)
                        if m + 1 < M:
                            scan(m + 1)
                        weigh(m, 2)
                        weigh(m, 3)
                        if m == 2 * NS + 1 - 1:
                            half_sum(0)
                    half_sum(1)
        with ExitStack() as ctx3:
            r3 = Room(nc, ctx3, "l1o")
            sz = r3.sb("sz", [P, HV, T])
            zps, szd, gd, yps, xad = r3.sem("z_in_psum"), r3.sem("silu_done"), r3.sem("gated"), r3.sem("y_in_psum"), r3.sem("x_added")
            with nc.Block() as block:

                @block.tensor
                def _(pe):
                    for h in range(HV):
                        for q in range(NCH):
                            pe.matmul(g.ps[:, h * T + q * CH:h * T + (q + 1) * CH], win[:, DI + h * P:DI + (h + 1) * P],
                                      g.hT[:, q * CH:(q + 1) * CH], start=True, stop=True).then_inc(zps, 1)
                    for b in range(TB):
                        pe.wait_ge(gd, HV * NCH)
                        pe.wait_ge(szd, HV * NCH)
                        if b >= 2:
                            pe.wait_ge(xad, b - 1)
                        for h in range(HV):
                            mm = pe.matmul(g.ps[:, (b % 2) * CH:(b % 2) * CH + C], U[:, h, b * P:(b + 1) * P], wout[:, h, :],
                                           start=(h == 0), stop=(h == HV - 1))
                        mm.then_inc(yps, 1)

                @block.scalar
                def _(act):
                    for n in range(HV * NCH):
                        act.wait_ge(zps, n + 1)
                        h, q = divmod(n, NCH)
                        act.activation(sz[:, h, q * CH:(q + 1) * CH], g.ps[:, n * CH:(n + 1) * CH], ACT.Silu).then_inc(szd, 1)

                @block.vector
                def _(dve):
                    for n in range(HV * NCH):
                        h, q = divmod(n, NCH)
                        dve.wait_ge(szd, n + 1)
                        dve.tensor_tensor(U[:, h, q * CH:(q + 1) * CH], U[:, h, q * CH:(q + 1) * CH], sz[:, h, q * CH:(q + 1) * CH],
                                          ALU.mult).then_inc(gd, 1)
                    for b in range(TB):
                        dve.wait_ge(yps, b + 1)
                        dve.tensor_tensor(g.X[:, b, :], g.X[:, b, :], g.ps[:, (b % 2) * CH:(b % 2) * CH + C], ALU.add).then_inc(xad, 1)


def gated_experts(nc, g, I):
    E = 8
    with ExitStack() as ctx:
        r = Room(nc, ctx, "l1f")
        wg = r.sb("wg", [C, C])
        bg = r.sb("bg", [P, C])
        we = r.sb("we", [C, E, C])
        be = r.sb("be", [E, C])
        pri = r.sb("pri", [P, C])

        def load(sp, s):
            sp.dma_start(wg[:, :], I["L1_ffn_Wg"]).then_inc(s, 16)
            sp.dma_start(bg[:, :], I["L1_ffn_bg"].rearrange("(a c) -> a c", a=1).broadcast_to([P, C])).then_inc(s, 16)
            sp.dma_start(we[:, :, :], I["L1_ffn_We"].rearrange("e d f -> d e f")).then_inc(s, 16)
            sp.dma_start(be[:, :], I["L1_ffn_be"]).then_inc(s, 16)
            return 4
        layernorm_transpose(nc, g, "ln3", load)
        lg = r.sb("lg", [P, TB, C])
        ex = r.sb("ex", [P, TB, C])
        eq = r.sb("eq", [P, TB, C])
        mx = r.sb("mx", [P, TB])
        pr = r.sb("prob", [P, TB])
        px = r.sb("px", [P, TB])
        oh = r.sb("oh", [P, TB, E])
        ohT = r.sb("ohT", [E, TB, P])
        acc = r.sb("acc", [P, 2, C])
        const, steps, lps, sub, expd, hot = r.sem("const_ready"), r.sem("steps"), r.sem("logits_in_psum"), r.sem("max_subtracted"), r.sem("exp_done"), r.sem("expert_known")
        otr, ocp, zps, zrd, bps, bcp = r.sem("onehot_transposed"), r.sem("onehot_copied"), r.sem("z_in_psum"), r.sem("z_read"), r.sem("bias_in_psum"), r.sem("bias_copied")
        xad = r.sem("x_added")
        with nc.Block() as block:

            @block.gpsimd
            def _(pool):
                pool.iota(pri[:, :], [[-1, C]], base=C, channel_multiplier=0, allow_small_or_imprecise_dtypes=True).then_inc(const, 1)

            @block.tensor
            def _(pe):
                for b in range(TB):
                    mm = pe.matmul(g.ps[:, b * P:(b + 1) * P], g.hT[:, b * P:(b + 1) * P], wg[:, :], start=True, stop=True)
                    if b % 4 == 3:
                        mm.then_inc(lps, 1)
                pe.wait_ge(hot, 1)
                for b in range(TB):
                    mm = pe.transpose(g.ps[0:E, T + b * P:T + (b + 1) * P], oh[:, b, :], g.ident[:, :])
                mm.then_inc(otr, 1)
                pe.wait_ge(ocp, 1)
                for b in range(TB):
                    o = (b % 2) * 2 * CH
                    if b >= 2:
                        pe.wait_ge(zrd, b - 1)
                        pe.wait_ge(bcp, b - 1)
                    pe.matmul(g.ps[:, (4 + b % 2) * CH:(4 + b % 2) * CH + C], ohT[:, b, :], be[:, :], start=True, stop=True).then_inc(bps, 1)
                    for k in range(2):
                        mm = pe.matmul(g.ps[:, o + k * CH:o + (k + 1) * CH], g.hT[:, b * P:(b + 1) * P],
                                       we[:, 4 * k:4 * k + 4, :].rearrange("d e f -> d (e f)"), start=True, stop=True)
                    mm.then_inc(zps, 1)

            @block.scalar
            def _(act):
                act.wait_ge(sub, 1)
                act.activation(ex[:, :, :], lg[:, :, :], ACT.Exp).then_inc(expd, 1)
                act.wait_ge(otr, 1)
                act.copy(ohT[:, :, :].rearrange("e b t -> e (b t)"), g.ps[0:E, T:2 * T]).then_inc(ocp, 1)
                for b in range(TB):
                    act.wait_ge(bps, b + 1)
                    if b >= 2:
                        act.wait_ge(xad, b - 1)
                    act.copy(acc[:, b % 2, :], g.ps[:, (4 + b % 2) * CH:(4 + b % 2) * CH + C]).then_inc(bcp, 1)

            @block.vector
            def _(dve):
                step = Steps(dve, steps)
                for q in range(NCH):
                    dve.wait_ge(lps, q + 1)
                    last = dve.tensor_tensor(lg[:, 4 * q:4 * q + 4, :], g.ps[:, q * CH:(q + 1) * CH].rearrange("p (b c) -> p b c", c=C),
                                             bg[:, :].unsqueeze(1).broadcast_to([P, 4, C]), ALU.add)
                step(last)
                bc = lambda v: v.unsqueeze(2).broadcast_to([P, TB, C])
                step(dve.tensor_reduce(mx[:, :], lg[:, :, :], AX, ALU.max))
                step(dve.tensor_tensor(eq[:, :, :], lg[:, :, :], bc(mx[:, :]), ALU.is_equal))
                dve.tensor_tensor(lg[:, :, :], lg[:, :, :], bc(mx[:, :]), ALU.subtract).then_inc(sub, 1)
                dve.wait_ge(const, 1)
                step(dve.tensor_tensor(eq[:, :, :], eq[:, :, :], pri[:, :].unsqueeze(1).broadcast_to([P, TB, C]), ALU.mult))
                step(dve.tensor_reduce(px[:, :], eq[:, :, :], AX, ALU.max))
                step(dve.tensor_tensor(eq[:, :, :], eq[:, :, :], bc(px[:, :]), ALU.is_equal))
                dve.tensor_reduce(oh[:, :, :], eq[:, :, :].rearrange("p b (a e) -> p b e a", e=E), AX, ALU.add).then_inc(hot, 1)
                dve.wait_ge(expd, 1)
                step(dve.tensor_reduce(pr[:, :], ex[:, :, :], AX, ALU.add))
                step(dve.reciprocal(pr[:, :], pr[:, :]))
                for b in range(TB):
                    o = (b % 2) * 2 * CH
                    dve.wait_ge(zps, b + 1)
                    dve.wait_ge(bcp, b + 1)
                    for e in range(E):
                        ins = dve.scalar_tensor_tensor(acc[:, b % 2, :], g.ps[:, o + e * C:o + (e + 1) * C], oh[:, b, e:e + 1],
                                                       acc[:, b % 2, :], ALU.mult, ALU.add)
                        step(ins)
                    dve.nop().then_inc(zrd, 1)
                    step(dve.tensor_scalar(acc[:, b % 2, :], acc[:, b % 2, :], 0.0, pr[:, b:b + 1], ALU.max, ALU.mult))
                    dve.tensor_tensor(g.X[:, b, :], g.X[:, b, :], acc[:, b % 2, :], ALU.add).then_inc(xad, 1)


def head_attention(nc, g, tag, wqkv, bias, q_scale, k_scale, out_scale, O):
    BOUND = 40.0
    NH, HS = 16, 8
    PR = 9 * HS
    KR = PR + 3
    G4 = NH // 4
    QC = 1024
    with ExitStack() as ctx:
        r = Room(nc, ctx, tag)
        Qs = r.sb("Qs", [KR, NH, T], BF16)
        Ks = r.sb("Ks", [KR, NH, T], BF16)
        Va = r.sb("Va", [P, TB, NH, HS + 1])
        parts = nc.dram_tensor(f"{tag}_parts", [2, 3, P, T], BF16, kind="Internal").ap()
        ctxg = ctx.enter_context(ExitStack())
        rg = Room(nc, ctxg, tag + "g")
        mT = rg.sb("guard", [NH, T])
        over = rg.sb("over", [1, 1], I32)
        mp = rg.sb("guard_parts", [NH, 3, T], BF16)
        mparts = nc.dram_tensor(f"{tag}_mparts", [3, NH, T], BF16, kind="Internal").ap()

        def split_guard(dve, step, split):
            for p_ in range(3):
                step(dve.tensor_copy(mp[:, p_, :], mT[:, :]))
                if p_ < 2:
                    step(dve.tensor_tensor(mT[:, :], mT[:, :], mp[:, p_, :], ALU.subtract))
            dve.sem_inc(split, 1)

        def stack_guard(sp, split, stored, stacked):
            sp.wait_ge(split, 1)
            for p_ in range(3):
                sp.dma_start(mparts[p_], mp[:, p_, :]).then_inc(stored, 16)
            sp.wait_ge(stored, 48)
            sp.dma_start(Qs[PR:KR, :, :], mparts).then_inc(stacked, 16)
            sp.wait_ge(stacked, 16)
        with ExitStack() as ctx1:
            r1 = Room(nc, ctx1, tag + "p")
            f32 = r1.sb("f32", [P, 2, T])
            pt = r1.sb("pt", [P, 2, 3, CH], BF16)
            onesb = r1.sb("onesb", [3, CH], BF16)
            sq = O[:, :, :].rearrange("p b c -> p (b c)")
            sel = r1.sb("head_of_row", [P, NH])
            kmax = r1.sb("kmax", [NH, 2])
            umax = r1.sb("umax", [1, NH + 1])
            qps, qcp, steps, split, stored = r1.sem("qk_in_psum"), r1.sem("qk_copied"), r1.sem("steps"), r1.sem("split"), [r1.sem("parts_stored0"), r1.sem("parts_stored1")]
            vps, vcp, onesd, stacked = r1.sem("v_in_psum"), r1.sem("v_copied"), r1.sem("ones_ready"), r1.sem("stacked")
            squared, selr, nps, kmd, und, ups = r1.sem("squared"), r1.sem("head_rows"), r1.sem("norms_in_psum"), r1.sem("kmax_done"), r1.sem("guard_done"), r1.sem("guards_in_row")
            gsplit, gstored, gstacked = r1.sem("guard_split"), r1.sem("guard_stored"), r1.sem("guard_stacked")
            with nc.Block() as block:

                @block.gpsimd
                def _(pool):
                    pool.memset(sel[:, :], 1.0).then_inc(selr, 1)
                    pool.wait_ge(selr, 1)
                    pool.affine_select(out=sel[:, :], in_=sel[:, :], compare_op=ALU.is_ge, fill=0.0, base=0, pattern=[[-HS, NH]],
                                       channel_multiplier=1).then_inc(selr, 1)
                    pool.wait_ge(selr, 2)
                    pool.affine_select(out=sel[:, :], in_=sel[:, :], compare_op=ALU.is_ge, fill=0.0, base=HS - 1, pattern=[[HS, NH]],
                                       channel_multiplier=-1).then_inc(selr, 1)

                @block.tensor
                def _(pe):
                    for i in range(2):
                        for q in range(NCH):
                            mm = pe.matmul(g.ps[:, i * T + q * CH:i * T + (q + 1) * CH], wqkv[:, i, :], g.hT[:, q * CH:(q + 1) * CH],
                                           start=True, stop=True)
                        mm.then_inc(qps, 1)
                    pe.wait_ge(selr, 3)
                    for i in (1, 2):
                        pe.wait_ge(squared, i)
                        if i == 2:
                            pe.wait_ge(kmd, 1)
                        for q in range(NCH):
                            mm = pe.matmul(g.ps[0:NH, T + q * CH:T + (q + 1) * CH], sel[:, :], sq[:, q * CH:(q + 1) * CH], start=True, stop=True)
                        mm.then_inc(nps, 1)
                    for b in range(TB):
                        mm = pe.matmul(g.ps[:, b * P:(b + 1) * P], g.hT[:, b * P:(b + 1) * P], wqkv[:, 2, :], start=True, stop=True)
                    mm.then_inc(vps, 1)
                    pe.wait_ge(und, 2)
                    pe.matmul(g.ps[0:1, T:T + NH], kmax[:, 1:2], g.ident[0:NH, 0:NH], start=True, stop=True).then_inc(ups, 1)

                @block.scalar
                def _(act):
                    def stack(i, half):
                        cols = slice(half * T // 2, (half + 1) * T // 2)
                        for k in range(2):
                            act.wait_ge(stored[k], 16 * 3 * (2 * i + half + 1))
                        for a in range(3):
                            for b in range(3):
                                rows = slice((3 * a + b) * HS, (3 * a + b + 1) * HS)
                                dst, part = ((Qs, a), (Ks, b))[i]
                                act.dma_start(dst[rows, :, cols], parts[i, part, :, cols].rearrange("(h e) t -> e h t", e=HS)).then_inc(stacked, 16)
                    for i, s in enumerate((q_scale, k_scale)):
                        act.wait_ge(qps, i + 1)
                        b = 0.0 if bias is None else bias[i]
                        act.activation(f32[:, i, :], g.ps[:, i * T:(i + 1) * T], ACT.Identity, bias=b, scale=s).then_inc(qcp, 1)
                    for n, (i, s) in enumerate(((1, k_scale), (0, q_scale))):
                        if n:
                            act.wait_ge(nps, 1)
                        b = 0.0 if bias is None else bias[i]
                        act.activation(sq[:, :], g.ps[:, i * T:(i + 1) * T], ACT.Square, bias=b, scale=s).then_inc(squared, 1)
                    stack(0, 0)
                    act.wait_ge(nps, 2)
                    act.activation(mT[:, :], g.ps[0:NH, T:2 * T], ACT.Sqrt, scale=kmax[:, 0:1]).then_inc(und, 1)
                    stack(0, 1)
                    stack(1, 0)
                    stack(1, 1)

                @block.vector
                def _(dve):
                    step = Steps(dve, steps)
                    dve.memset(onesb[:, :], 1.0).then_inc(onesd, 1)
                    step(dve.memset(Va[:, :, :, :], 1.0))
                    for i in range(2):
                        dve.wait_ge(qcp, i + 1)
                        for q in range(NCH):
                            cols = slice(q * CH, (q + 1) * CH)
                            m = i * NCH + q
                            if m >= 2:
                                dve.wait_ge(stored[m % 2], 16 * 3 * (m // 2))
                            for p_ in range(3):
                                step(dve.tensor_copy(pt[:, m % 2, p_, :], f32[:, i, cols]))
                                if p_ < 2:
                                    step(dve.tensor_tensor(f32[:, i, cols], f32[:, i, cols], pt[:, m % 2, p_, :], ALU.subtract))
                            dve.nop().then_inc(split, 1)
                        if i == 0:
                            dve.wait_ge(nps, 1)
                            dve.tensor_reduce(kmax[:, 0:1], g.ps[0:NH, T:2 * T], AX, ALU.max).then_inc(kmd, 1)
                    dve.wait_ge(und, 1)
                    step(dve.tensor_reduce(kmax[:, 1:2], mT[:, :], AX, ALU.max))
                    step(dve.tensor_scalar(mT[:, :], mT[:, :], -1.0, None, ALU.mult))
                    dve.sem_inc(und, 1)
                    dve.wait_ge(ups, 1)
                    step(dve.tensor_reduce(umax[:, NH:NH + 1], g.ps[0:1, T:T + NH], AX, ALU.max))
                    dve.tensor_scalar(over[:, :], umax[:, NH:NH + 1], BOUND, None, ALU.is_gt)
                    split_guard(dve, step, gsplit)
                    dve.wait_ge(vps, 1)
                    vsrc = g.ps[:, 0:T].rearrange("p (b h e) -> p (b h) e", b=TB, e=HS)
                    vdst = Va[:, :, :, 0:HS].rearrange("p b h e -> p (b h) e")
                    if bias is None:
                        dve.tensor_copy(vdst, vsrc).then_inc(vcp, 1)
                    else:
                        for b in range(TB):
                            ins = dve.tensor_tensor(Va[:, b, :, 0:HS], g.ps[:, b * P:(b + 1) * P].rearrange("p (h e) -> p h e", e=HS),
                                                    bias[2].rearrange("p (h e) -> p h e", e=HS), ALU.add)
                        ins.then_inc(vcp, 1)

                @block.sync
                def _(sp):
                    sp.wait_ge(onesd, 1)
                    sp.dma_start(Ks[PR:KR, :, :], onesb[:, :].unsqueeze(1).broadcast_to([3, NH * NCH, CH])).then_inc(stacked, 16)
                    for m in range(2 * NCH):
                        i, q = divmod(m, NCH)
                        sp.wait_ge(split, m + 1)
                        for p_ in range(3):
                            sp.dma_start(parts[i, p_, :, q * CH:(q + 1) * CH], pt[:, m % 2, p_, :]).then_inc(stored[m % 2], 16)
                    stack_guard(sp, gsplit, gstored, gstacked)
                    sp.wait_ge(stacked, 16 * (1 + 4 * 9))
        with ExitStack() as ctx2:
            r2 = Room(nc, ctx2, tag + "m")
            mx = r2.sb("mx", [P, NH, TB])
            sps, mxd, tr, steps, split, mst = r2.sem("scores_in_psum"), r2.sem("max_done"), r2.sem("max_transposed"), r2.sem("steps"), r2.sem("split"), r2.sem("max_stored")
            mstk = r2.sem("max_stacked")
            with nc.Block() as block:

                @block.tensor
                def _(pe):
                    flag = pe.value_load(over[0:1, 0:1], min_val=0, max_val=1)
                    with pe.If(flag > 0):
                        for h in range(NH):
                            with pe.Fori(0, TB // 2) as j:
                                for k in range(2):
                                    pe.wait_ge(mxd, j * 2 + (h * TB + k + 1))
                                    for q in range(NCH):
                                        mm = pe.matmul(g.ps[:, k * T + q * CH:k * T + (q + 1) * CH], Qs[0:PR, h, bass.ds(j * 2 * P + k * P, P)],
                                                       Ks[0:PR, h, q * CH:(q + 1) * CH], start=True, stop=True)
                                    mm.then_inc(sps, 1)
                        pe.wait_ge(mxd, NH * TB + 2)
                        for b in range(TB):
                            mm = pe.transpose(g.ps[0:NH, b * P:(b + 1) * P], mx[:, :, b], g.ident[:, :])
                        mm.then_inc(tr, 1)

                @block.vector
                def _(dve):
                    flag = dve.value_load(over[0:1, 0:1], min_val=0, max_val=1)
                    with dve.If(flag > 0):
                        dve.sem_inc(mxd, 2)
                        for h in range(NH):
                            with dve.Fori(0, TB // 2) as j:
                                for k in range(2):
                                    dve.wait_ge(sps, j * 2 + (h * TB + k + 1))
                                    dve.tensor_reduce(mx[:, h, bass.ds(j * 2 + k, 1)], g.ps[:, k * T:(k + 1) * T], AX, ALU.max, negate=True).then_inc(mxd, 1)
                        dve.wait_ge(tr, 1)
                        step = Steps(dve, steps)
                        step(dve.tensor_copy(mT[:, :], g.ps[0:NH, 0:T]))
                        split_guard(dve, step, split)

                @block.sync
                def _(sp):
                    flag = sp.value_load(over[0:1, 0:1], min_val=0, max_val=1)
                    with sp.If(flag > 0):
                        stack_guard(sp, split, mst, mstk)
        ctxg.close()
        with ExitStack() as ctx3:
            r3 = Room(nc, ctx3, tag + "e")
            NPT, NST = 8, 3
            pT = r3.sb("pT", [P, NPT, QC])
            oT = r3.sb("oT", [P, QC])
            rc = r3.sb("rc", [P, 4, 4])
            sps, expd, accr = r3.sem("scores_in_psum"), r3.sem("exp_done"), [r3.sem("acc_read0"), r3.sem("acc_read1")]
            pvd = [r3.sem("pv_done0"), r3.sem("pv_done1")]
            otr, xrd, steps, azero = r3.sem("o_transposed"), r3.sem("o_read"), r3.sem("steps"), r3.sem("acc_zeroed")
            ACC = NST * QC
            SEG = TB * 4
            NQ = T // QC
            NSEG = G4 * NQ
            XKT = (4, 6)
            XTURN = [4 * kt + i for i, kt in enumerate(XKT)]
            TURNS = SEG + 2
            assert TURNS % NST == 0 and QC == 2 * CH

            def turn_of(kt, j):
                return 4 * kt + j + sum(kt >= x for x in XKT)

            with nc.Block() as block:

                @block.tensor
                def _(pe):
                    def slot_free(seg, turn):
                        before = seg * TURNS + turn - NST
                        s_, t_ = divmod(before, TURNS)
                        if before < 0 or (t_ in XTURN and s_ == 0):
                            return
                        if t_ in XTURN:
                            pe.wait_ge(xrd, 2 * (s_ - 1) + XTURN.index(t_) + 1)
                        else:
                            pe.wait_ge(expd, s_ * SEG + t_ - sum(t_ > x for x in XTURN) + 1)

                    def scores(n, j):
                        seg, kt = divmod(n, TB)
                        hg, qc = divmod(seg, NQ)
                        turn = turn_of(kt, j)
                        slot = turn % NST
                        slot_free(seg, turn)
                        for c in range(QC // CH):
                            mm = pe.matmul(g.ps[:, slot * QC + c * CH:slot * QC + (c + 1) * CH],
                                           Ks[:, hg * 4 + j, kt * P:(kt + 1) * P],
                                           Qs[:, hg * 4 + j, qc * QC + c * CH:qc * QC + (c + 1) * CH], start=True, stop=True)
                        mm.then_inc(sps, 1)

                    def values(n, c):
                        seg, kt = divmod(n, TB)
                        hg = seg // NQ
                        if c == 0:
                            pe.wait_ge(expd, 4 * n + 4)
                        if kt == 0 and seg:
                            pe.wait_ge(accr[c], seg)
                        for j in range(4):
                            mm = pe.matmul(g.ps[32 * j:32 * j + HS + 1, ACC + c * CH:ACC + (c + 1) * CH],
                                           Va[:, kt, hg * 4 + j, :], pT[:, (4 * n + j) % NPT, c * CH:(c + 1) * CH],
                                           start=(kt == 0), stop=(kt == TB - 1))
                        mm.then_inc(pvd[c], 1)

                    def sums_back(seg, i, slot):
                        pe.wait_ge(accr[i], seg + 1)
                        for b in range(4):
                            mm = pe.transpose(g.ps[:, slot * QC + b * P:slot * QC + (b + 1) * P], oT[:, i * CH + b * P:i * CH + (b + 1) * P],
                                              g.ident[:, :])
                        mm.then_inc(otr, 1)
                    pe.wait_ge(azero, 1)
                    for j in range(4):
                        scores(0, j)
                    for n in range(NSEG * TB):
                        seg, kt = divmod(n + 1, TB)
                        more = n + 1 < NSEG * TB
                        if more and seg and kt in XKT:
                            i = XKT.index(kt)
                            slot_free(seg, XTURN[i])
                            sums_back(seg - 1, i, XTURN[i] % NST)
                        for c in range(2):
                            if more:
                                scores(n + 1, 2 * c)
                                scores(n + 1, 2 * c + 1)
                            values(n, c)
                    pe.wait_ge(expd, NSEG * SEG)
                    for i in range(2):
                        sums_back(NSEG - 1, i, i)

                @block.scalar
                def _(act):
                    with act.Fori(0, NSEG) as seg:
                        for kt in range(TB):
                            for j in range(4):
                                slot = turn_of(kt, j) % NST
                                act.wait_ge(sps, seg * SEG + (4 * kt + j + 1))
                                if j == 0:
                                    act.wait_ge(pvd[1], seg * TB + (kt + 1))
                                act.activation(pT[:, (4 * kt + j) % NPT, :], g.ps[:, slot * QC:(slot + 1) * QC], ACT.Exp).then_inc(expd, 1)

                @block.vector
                def _(dve):
                    step = Steps(dve, steps)
                    dve.memset(g.ps[:, ACC:ACC + QC], 0.0).then_inc(azero, 1)
                    dve.sem_inc(pvd[1], NPT // 4)

                    def finish(seg, i, slot):
                        hg, qc = divmod(seg, NQ)
                        dve.wait_ge(otr, 2 * seg + i + 1)
                        o = g.ps[:, slot * QC:slot * QC + CH].rearrange("p (b j e) -> p b j e", b=4, e=32)
                        b0 = qc * (QC // P) + 4 * i
                        step(dve.reciprocal(rc[:, :, :], o[:, :, :, HS]))
                        for j in range(4):
                            h = hg * 4 + j
                            ins = dve.scalar_tensor_tensor(O[:, b0:b0 + 4, h * HS:(h + 1) * HS], o[:, :, j, 0:HS], out_scale,
                                                           rc[:, :, j].unsqueeze(2).broadcast_to([P, 4, HS]), ALU.mult, ALU.mult)
                        step(ins)
                        dve.sem_inc(xrd, 1)
                    for seg in range(NSEG):
                        if seg:
                            for i in range(2):
                                finish(seg - 1, i, XTURN[i] % NST)
                        for c in range(2):
                            dve.wait_ge(pvd[c], (seg + 1) * TB + (NPT // 4 if c else 0))
                            dve.tensor_copy(oT[:, c * CH:(c + 1) * CH], g.ps[:, ACC + c * CH:ACC + (c + 1) * CH]).then_inc(accr[c], 1)
                    for i in range(2):
                        finish(NSEG - 1, i, i)


def transpose_blocks(pe, g, src, first, sem):
    for b in range(TB):
        mm = pe.transpose(g.ps[:, first + b * P:first + (b + 1) * P], src[:, b, :], g.ident[:, :])
    mm.then_inc(sem, 1)


def find_cut(nc, g, E, kk, Z, var, cut, need, general):
    ITERS, A = 6, TB // 2
    AIM = kk - 4.4
    SPREAD = 90.0
    with ExitStack() as ctx:
        r = Room(nc, ctx, "cut")
        at = r.sb("at", [P, 2, TB])
        lo = r.sb("lo", [P, 2, TB])
        hi = r.sb("hi", [P, 2, TB])
        w = r.sb("width", [P, 2, TB])
        d = r.sb("move", [P, 2, TB])
        sd = r.sb("std", [P, TB])
        nt = r.sb("minus_at", [P, TB])
        u = r.sb("up", [P, TB])
        v = r.sb("down", [P, TB])
        ok = r.sb("ok", [P, TB])
        okr = r.sb("row_ok", [P, 1])
        junk = r.sb("junk", [P, 2, T], BF16)
        junka = r.sb("junk_act", [P, 2, T], BF16)
        steps, sdr, probe, counted, okd, okps = r.sem("steps"), r.sem("std_ready"), r.sem("probe_ready"), r.sem("act_counted"), r.sem("rows_ok"), r.sem("ok_in_psum")
        with nc.Block() as block:

            @block.scalar
            def _(act):
                act.activation(sd[:, :], var, ACT.Sqrt).then_inc(sdr, 1)
                with act.Fori(0, ITERS) as i:
                    for b in range(A, TB):
                        if b == A:
                            act.wait_ge(probe, i + 1)
                        if b >= A + 2:
                            act.wait_ge(counted, i * A + (b - A - 1))
                        act.activation(junka[:, b % 2, :], E[:, b, :], ACT.Sign, bias=nt[:, b:b + 1], accum_out=at[:, 1, b:b + 1]).then_inc(counted, 1)
                    act.wait_ge(counted, i * A + A)

            @block.vector
            def _(dve):
                step = Steps(dve, steps)
                dve.wait_ge(sdr, 1)
                step(dve.tensor_scalar(at[:, 0, :], Z[:, :], 1.0 / T, None, ALU.mult))
                step(dve.scalar_tensor_tensor(at[:, 0, :], sd[:, :], 0.8416, at[:, 0, :], ALU.mult, ALU.add))
                delta = SPREAD / (T * 0.28)
                dve.scalar_tensor_tensor(lo[:, 0, :], sd[:, :], -delta, at[:, 0, :], ALU.mult, ALU.add)
                dve.scalar_tensor_tensor(hi[:, 0, :], sd[:, :], delta, at[:, 0, :], ALU.mult, ALU.add)
                dve.memset(cut[:, :], 0.0)
                dve.memset(need[:, :], 0.0)
                dve.memset(lo[:, 1, :], AIM + SPREAD)
                step(dve.memset(hi[:, 1, :], AIM - SPREAD))
                PER = 7 + A + 1 + 7 + 1 + 3 + 1 + 3
                with dve.Fori(0, ITERS) as i:
                    step.enter(i, PER)
                    step(dve.tensor_tensor(w[:, :, :], hi[:, :, :], lo[:, :, :], ALU.subtract))
                    step(dve.reciprocal(w[:, 1, :], w[:, 1, :]))
                    step(dve.scalar_tensor_tensor(w[:, 1, :], lo[:, 1, :], AIM, w[:, 1, :], ALU.subtract, ALU.mult))
                    step(dve.tensor_scalar(w[:, 1, :], w[:, 1, :], -0.2, -0.8, ALU.min, ALU.max))
                    step(dve.tensor_tensor(w[:, 0, :], w[:, 0, :], w[:, 1, :], ALU.mult))
                    step(dve.tensor_tensor(at[:, 0, :], lo[:, 0, :], w[:, 0, :], ALU.subtract))
                    step(dve.tensor_scalar(nt[:, :], at[:, 0, :], -1.0, None, ALU.mult))
                    dve.sem_inc(probe, 1)
                    for b in range(A):
                        step(dve.tensor_scalar(junk[:, b % 2, :], E[:, b, :], at[:, 0, b:b + 1], 0.0, ALU.is_ge, ALU.add, accum_out=at[:, 1, b:b + 1]))
                    dve.wait_ge(counted, i * A + A)
                    step(dve.tensor_scalar(at[:, 1, A:TB], at[:, 1, A:TB], 0.5, T * 0.5, ALU.mult, ALU.add))
                    step(dve.tensor_scalar(ok[:, :], at[:, 1, :], kk - 8.5, None, ALU.is_ge))
                    step(dve.scalar_tensor_tensor(ok[:, :], at[:, 1, :], kk - 0.5, ok[:, :], ALU.is_le, ALU.mult))
                    step(dve.tensor_scalar(v[:, :], at[:, 1, :], -1.0, float(kk), ALU.mult, ALU.add))
                    step(dve.tensor_tensor(v[:, :], v[:, :], ok[:, :], ALU.mult))
                    step(dve.tensor_tensor(need[:, :], need[:, :], v[:, :], ALU.max))
                    step(dve.tensor_tensor(ok[:, :], ok[:, :], at[:, 0, :], ALU.mult))
                    step(dve.tensor_tensor(cut[:, :], cut[:, :], ok[:, :], ALU.max))
                    step(dve.tensor_scalar(u[:, :], at[:, 1, :], AIM, None, ALU.is_ge))
                    for end, sign in ((lo, 1.0), (hi, -1.0)):
                        if sign < 0:
                            step(dve.tensor_scalar(u[:, :], u[:, :], -1.0, 1.0, ALU.mult, ALU.add))
                        step(dve.tensor_tensor(d[:, :, :], at[:, :, :], end[:, :, :], ALU.subtract))
                        step(dve.tensor_tensor(d[:, :, :], d[:, :, :], u[:, :].unsqueeze(1).broadcast_to([P, 2, TB]), ALU.mult))
                        step(dve.tensor_tensor(end[:, :, :], end[:, :, :], d[:, :, :], ALU.add))
                step.leave(ITERS)
                for b in range(A, TB):
                    step(dve.tensor_scalar(junk[:, b % 2, :], E[:, b, :], cut[:, b:b + 1], 0.0, ALU.is_ge, ALU.add, accum_out=at[:, 1, b:b + 1]))
                step(dve.tensor_scalar(need[:, A:TB], at[:, 1, A:TB], -1.0, float(kk), ALU.mult, ALU.add))
                step(dve.tensor_scalar(ok[:, :], need[:, :], 1.0, None, ALU.is_ge))
                step(dve.scalar_tensor_tensor(ok[:, :], need[:, :], 8.0, ok[:, :], ALU.is_le, ALU.mult))
                dve.tensor_reduce(okr[:, :], ok[:, :], AX, ALU.min).then_inc(okd, 1)
                dve.wait_ge(okps, 1)
                dve.tensor_scalar(general[:, :], g.ps[0:1, 0:1], P - 0.5, None, ALU.is_lt)

            @block.tensor
            def _(pe):
                pe.wait_ge(okd, 1)
                pe.matmul(g.ps[0:1, 0:1], okr[:, :], g.ones[:, 0:1], start=True, stop=True).then_inc(okps, 1)


def find_rest(dve, steps, E, cut, need, room, found, kept):
    rest, top, place, drop = room
    step = Steps(dve, steps)
    for i in range(8):
        dve.memset(place[:, i:i + 1], float(i))
    step(dve.memset(drop[:, :], 0.0))
    for b in range(TB):
        e = E[:, b, :]
        below = rest[:, b % 2, :]
        if b >= 2:
            dve.wait_ge(kept, b - 1)
        step(dve.scalar_tensor_tensor(below, e, cut[:, b:b + 1], e, ALU.is_lt, ALU.mult))
        step(dve.max(top[:, :], below))
        step(dve.scalar_tensor_tensor(drop[:, :], place[:, :], need[:, b:b + 1], top[:, :], ALU.is_lt, ALU.mult))
        step(dve.match_replace(below, drop[:, :], below, 0.0))
        dve.sem_inc(found, 1)


def keep_by_bisection(dve, steps, E, kk, room, kept):
    ITERS = 31
    lo, hi, mid, cnt, need, up, dn, tie, rank = room
    junk = rank
    step = Steps(dve, steps)

    def count(at):
        for b in range(TB):
            step(dve.tensor_scalar(junk[:, :], E[:, b, :], at[:, b:b + 1], 0.0, ALU.is_ge, ALU.add, accum_out=cnt[:, b:b + 1]))
    dve.memset(lo[:, :], 0.0)
    step(dve.memset(hi[:, :], 2.0))
    PER = TB + 7
    with dve.Fori(0, ITERS) as i:
        step.enter(i, PER)
        step(dve.tensor_tensor(mid[:, :], lo[:, :], hi[:, :], ALU.add))
        step(dve.tensor_scalar(mid[:, :], mid[:, :], 0.5, None, ALU.mult))
        count(mid)
        step(dve.tensor_scalar(up[:, :], cnt[:, :], float(kk), None, ALU.is_ge))
        step(dve.tensor_tensor(dn[:, :], up[:, :], mid[:, :], ALU.mult))
        step(dve.tensor_tensor(lo[:, :], lo[:, :], dn[:, :], ALU.max))
        step(dve.scalar_tensor_tensor(dn[:, :], up[:, :], 1.0e30, mid[:, :], ALU.mult, ALU.add))
        step(dve.tensor_tensor(hi[:, :], hi[:, :], dn[:, :], ALU.min))
    step.leave(ITERS)
    count(hi)
    step(dve.tensor_scalar(need[:, :], cnt[:, :], -1.0, float(kk), ALU.mult, ALU.add))
    for b in range(TB):
        e = E[:, b, :]
        step(dve.tensor_scalar(rank[:, :], e, hi[:, b:b + 1], None, ALU.is_ge))
        step(dve.scalar_tensor_tensor(tie[:, :], e, lo[:, b:b + 1], rank[:, :], ALU.is_ge, ALU.subtract))
        step(dve.tensor_tensor_scan(rank[:, :], tie[:, :], tie[:, :], 0.0, ALU.add, ALU.max))
        step(dve.scalar_tensor_tensor(tie[:, :], rank[:, :], need[:, b:b + 1], tie[:, :], ALU.is_le, ALU.mult))
        step(dve.scalar_tensor_tensor(tie[:, :], e, hi[:, b:b + 1], tie[:, :], ALU.is_ge, ALU.add))
        step(dve.tensor_tensor(e, e, tie[:, :], ALU.mult))
    dve.sem_inc(kept, TB)


def dual_attention(nc, g, I):
    R, DFF = 64, 512
    K = DFF // P
    KEEP = max(1, int(T * 0.2))
    with ExitStack() as ctx:
        r = Room(nc, ctx, "l2a")
        dense = r.sb("dense", [P, TB, C])
        bp = r.sb("bp", [R, 2])
        lam = r.sb("lam", [P, 2])
        sc = r.sb("sc", [P, 2])
        with ExitStack() as ctx0:
            r0 = Room(nc, ctx0, "l2h")
            w = r0.sb("wqkv", [C, 3, C])
            bqk = r0.sb("bqk", [P, 2])
            bv = r0.sb("bv", [P, C])

            def load(sp, s):
                sp.dma_start(w[:, :, :].rearrange("c i o -> c (i o)"), I["L2_attn_in_proj_wT"]).then_inc(s, 16)
                sp.dma_start(bqk[:, :], I["L2_attn_in_proj_b"][0:2 * C].rearrange("(i p) -> p i", p=P), allow_slow_non_contiguous=True).then_inc(s, 16)
                sp.dma_start(bv[:, :], I["L2_attn_in_proj_b"][2 * C:3 * C].rearrange("(a c) -> a c", a=1).broadcast_to([P, C])).then_inc(s, 16)
                sp.dma_start(bp[:, 0:1], I["L2_attn_Qp_b"].rearrange("(p a) -> p a", a=1), allow_slow_non_contiguous=True).then_inc(s, 16)
                sp.dma_start(bp[:, 1:2], I["L2_attn_Kp_b"].rearrange("(p a) -> p a", a=1), allow_slow_non_contiguous=True).then_inc(s, 16)
                sp.dma_start(lam[:, 0:1], I["L2_attn_lam"].rearrange("(p a) -> p a", a=1).broadcast_to([P, 1]), allow_slow_non_contiguous=True).then_inc(s, 16)
                return 6
            layernorm_transpose(nc, g, "ln4", load)
            prep = r0.sem("bias_scaled")
            QS = 8 ** -0.5
            with nc.Block() as block:

                @block.vector
                def _(dve):
                    dve.tensor_scalar(bqk[:, 0:1], bqk[:, 0:1], QS, None, ALU.mult).then_inc(prep, 1)
                    dve.tensor_scalar(bp[:, 0:1], bp[:, 0:1], R ** -0.5, None, ALU.mult)
                    dve.tensor_scalar(lam[:, 1:2], lam[:, 0:1], -1.0, None, ALU.mult).then_inc(prep, 1)

                @block.scalar
                def _(act):
                    act.wait_ge(prep, 2)
                    act.activation(sc[:, :], lam[:, :], ACT.Sigmoid)
            head_attention(nc, g, "l2m", w, (bqk[:, 0:1], bqk[:, 1:2], bv[:, :]), QS, 1.0, 1.0, dense)
        wo = r.sb("wo", [C, C])
        wp = r.sb("wp", [C, 2, R])
        wv = r.sb("wv", [C, C])
        rows = r.sb("rows", [P, 7, C])
        f1 = r.sb("f1", [C, DFF])
        f2 = r.sb("f2", [P, K, C])
        b1 = r.sb("b1", [P, K])
        with ExitStack() as ctx0:
            r0 = Room(nc, ctx0, "l2o")
            OT = r0.sb("OT", [C, T])
            tr, cp, yps, dd = r0.sem("o_transposed"), r0.sem("o_copied"), r0.sem("y_in_psum"), r0.sem("dense_done")
            first, rest = r0.sem("projection_loaded"), r0.sem("rest_loaded")
            with nc.Block() as block:

                @block.sync
                def _(sp):
                    rest_loads = 0

                    def ld(dst, src, slow=False):
                        nonlocal rest_loads
                        rest_loads += 1
                        sp.dma_start(dst, src, allow_slow_non_contiguous=slow).then_inc(rest, 16)
                    sp.dma_start(wo[:, :], I["L2_attn_out_proj_wT"]).then_inc(first, 16)
                    for i, nm in enumerate(("out_proj_b", "Vp_b", "ff2_b", "ln1_g", "ln1_b", "ln2_g", "ln2_b")):
                        v = I["L2_attn_" + nm].rearrange("(a c) -> a c", a=1).broadcast_to([P, C])
                        if i == 0:
                            sp.dma_start(rows[:, i, :], v).then_inc(first, 16)
                        else:
                            ld(rows[:, i, :], v)
                    ld(wp[:, 0, :], I["L2_attn_Qp_wT"])
                    ld(wp[:, 1, :], I["L2_attn_Kp_wT"])
                    ld(wv[:, :], I["L2_attn_Vp_wT"])
                    ld(f1[:, :], I["L2_attn_ff1_wT"])
                    ld(f2[:, :, :], I["L2_attn_ff2_wT"].rearrange("(k p) c -> p k c", p=P))
                    ld(b1[:, :], I["L2_attn_ff1_b"].rearrange("(k p) -> p k", p=P), slow=True)
                    sp.wait_ge(rest, 16 * rest_loads)

                @block.tensor
                def _(pe):
                    transpose_blocks(pe, g, dense, 0, tr)
                    pe.wait_ge(first, 32)
                    pe.wait_ge(cp, 1)
                    for b in range(TB):
                        pe.matmul(g.ps[:, T + b * P:T + (b + 1) * P], OT[:, b * P:(b + 1) * P], wo[:, :], start=True, stop=True).then_inc(yps, 1)

                @block.vector
                def _(dve):
                    dve.wait_ge(tr, 1)
                    dve.tensor_copy(OT[:, :], g.ps[:, 0:T]).then_inc(cp, 1)
                    dve.wait_ge(first, 32)
                    for q in range(NCH):
                        dve.wait_ge(yps, 4 * q + 4)
                        dve.tensor_tensor(dense[:, 4 * q:4 * q + 4, :], g.ps[:, T + q * CH:T + (q + 1) * CH].rearrange("p (b c) -> p b c", c=C),
                                          rows[:, 0, :].unsqueeze(1).broadcast_to([P, 4, C]), ALU.add).then_inc(dd, 1)
        with ExitStack() as ctx1:
            r1 = Room(nc, ctx1, "l2s")
            E = r1.sb("E", [P, TB, T])
            V = r1.sb("V", [P, TB, C])
            mx = r1.sb("mx", [P, TB])
            Z = r1.sb("Z", [P, TB])
            ssum = r1.sb("ssum", [P, TB])
            st = r1.sb("bn", [P, TB, 2, 6])
            mv = r1.sb("meanvar", [P, TB, 2])
            cut = r1.sb("cut", [P, TB])
            need = r1.sb("need", [P, TB])
            general = r1.sb("general", [1, 1], I32)
            with ExitStack() as ctx2:
                r2 = Room(nc, ctx2, "l2q")
                qk = r2.sb("qk", [P, 2, T])
                zero, qps, qcp, vps, vcp = r2.sem("zeroed"), r2.sem("qk_in_psum"), r2.sem("qk_copied"), r2.sem("v_in_psum"), r2.sem("v_copied")
                sps, mxd, exd = r2.sem("scores_in_psum"), r2.sem("max_done"), r2.sem("exp_done")
                smp = r2.sem("sampled")
                with nc.Block() as block:

                    @block.gpsimd
                    def _(pool):
                        pool.memset(qk[R:P, :, :], 0.0).then_inc(zero, 1)

                    @block.tensor
                    def _(pe):
                        for i in range(2):
                            for q in range(NCH):
                                mm = pe.matmul(g.ps[0:R, i * T + q * CH:i * T + (q + 1) * CH], wp[:, i, :], g.hT[:, q * CH:(q + 1) * CH],
                                               start=True, stop=True)
                            mm.then_inc(qps, 1)
                        pe.wait_ge(qcp, 1)
                        for b in range(TB):
                            mm = pe.matmul(g.ps[:, b * P:(b + 1) * P], g.hT[:, b * P:(b + 1) * P], wv[:, :], start=True, stop=True)
                        mm.then_inc(vps, 1)
                        pe.wait_ge(zero, 1)
                        pe.wait_ge(qcp, 2)
                        for b in range(TB):
                            if b == 1:
                                pe.wait_ge(vcp, 1)
                            if b >= 2:
                                pe.wait_ge(exd, b - 1)
                            half = (b + 1) % 2
                            for q in range(NCH):
                                mm = pe.matmul(g.ps[:, half * T + q * CH:half * T + (q + 1) * CH], qk[:, 0, b * P:(b + 1) * P],
                                               qk[:, 1, q * CH:(q + 1) * CH], start=True, stop=True)
                            mm.then_inc(sps, 1)

                    @block.scalar
                    def _(act):
                        for i, s in enumerate((R ** -0.5, 1.0)):
                            act.wait_ge(qps, i + 1)
                            act.activation(qk[0:R, i, :], g.ps[0:R, i * T:(i + 1) * T], ACT.Identity, bias=bp[:, i:i + 1], scale=s).then_inc(qcp, 1)
                        for b in range(TB):
                            act.wait_ge(mxd, b + 1)
                            half = (b + 1) % 2
                            act.activation(E[:, b, :], g.ps[:, half * T:(half + 1) * T], ACT.Exp, bias=mx[:, b:b + 1],
                                           accum_out=Z[:, b:b + 1]).then_inc(exd, 1)

                    @block.vector
                    def _(dve):
                        dve.wait_ge(vps, 1)
                        dve.tensor_tensor(V[:, :, :], g.ps[:, 0:T].rearrange("p (b c) -> p b c", c=C),
                                          rows[:, 1, :].unsqueeze(1).broadcast_to([P, TB, C]), ALU.add).then_inc(vcp, 1)

                        def sample(b):
                            dve.wait_ge(exd, b + 1)
                            for k in range(2):
                                ins = dve.bn_stats(st[:, b, k, :], E[:, b, k * (T // 2):(k + 1) * (T // 2):2])
                            ins.then_inc(smp, 1)
                        for b in range(TB):
                            dve.wait_ge(sps, b + 1)
                            half = (b + 1) % 2
                            dve.tensor_reduce(mx[:, b:b + 1], g.ps[:, half * T:(half + 1) * T], AX, ALU.max, negate=True).then_inc(mxd, 1)
                            if b:
                                sample(b - 1)
                        sample(TB - 1)
                        dve.wait_ge(smp, TB)
                        for b in range(TB):
                            dve.bn_aggr(mv[:, b, :], st[:, b, :, :].rearrange("p k s -> p (k s)"))
            find_cut(nc, g, E, KEEP, Z, mv[:, :, 1], cut, need, general)
            with ExitStack() as ctx3:
                r3 = Room(nc, ctx3, "l2v")
                NPT = 3
                pT = r3.sb("pT", [P, NPT, CH])
                sT = r3.sb("sT", [C, NCH, CH])
                rest = r3.sb("rest", [P, 2, T])
                junk = r3.sb("junk", [P, T], BF16)
                small = [r3.sb("small%d" % i, [P, TB]) for i in range(7)]
                top8 = [r3.sb("top%d" % i, [P, 8]) for i in range(3)]
                kept, found, summed, gsteps, fsteps = r3.sem("rows_kept"), r3.sem("rest_found"), r3.sem("rows_summed"), r3.sem("general_steps"), r3.sem("fast_steps")
                tr, pcp, ops, ocp, otr, fin, steps, rsr = r3.sem("p_transposed"), r3.sem("p_copied"), r3.sem("values_done"), r3.sem("values_copied"), r3.sem("values_transposed"), r3.sem("sparse_done"), r3.sem("steps"), r3.sem("str")
                with nc.Block() as block:

                    @block.tensor
                    def _(pe):
                        def back(q):
                            pe.wait_ge(ocp, q + 1)
                            if q >= 2:
                                pe.wait_ge(fin, q - 1)
                            for j in range(4):
                                mm = pe.transpose(g.ps[:, (6 + q % 2) * CH + j * P:(6 + q % 2) * CH + (j + 1) * P], sT[:, q, j * P:(j + 1) * P],
                                                  g.ident[:, :])
                            mm.then_inc(otr, 1)

                        def turn(n):
                            q, kt = divmod(n, TB)
                            if n >= 4:
                                pe.wait_ge(pcp, n - 3)
                            if kt == 0:
                                pe.wait_ge(kept, 4 * q + 4)
                            for j in range(4):
                                mm = pe.transpose(g.ps[:, (n % 4) * CH + j * P:(n % 4) * CH + (j + 1) * P], E[:, 4 * q + j, kt * P:(kt + 1) * P],
                                                  g.ident[:, :])
                            mm.then_inc(tr, 1)

                        def weigh(n):
                            q, kt = divmod(n, TB)
                            pe.wait_ge(pcp, n + 1)
                            if kt == 0 and q >= 2:
                                pe.wait_ge(ocp, q - 1)
                            mm = pe.matmul(g.ps[:, (4 + q % 2) * CH:(5 + q % 2) * CH], V[:, kt, :], pT[:, n % NPT, :], start=(kt == 0), stop=(kt == TB - 1))
                            mm.then_inc(ops, 1)
                        N = NCH * TB
                        for n in range(N + 1):
                            if n < N:
                                turn(n)
                            if n:
                                weigh(n - 1)
                        for q in range(NCH):
                            back(q)

                    @block.gpsimd
                    def _(pool):
                        flag = pool.value_load(general[0:1, 0:1], min_val=0, max_val=1)
                        with pool.If(flag < 1):
                            for b in range(TB):
                                pool.wait_ge(found, b + 1)
                                pool.tensor_tensor(E[:, b, :], E[:, b, :], rest[:, b % 2, :], ALU.subtract).then_inc(kept, 1)

                    @block.scalar
                    def _(act):
                        def sums_copy(q):
                            act.wait_ge(ops, TB * (q + 1))
                            act.copy(sT[:, q, :], g.ps[:, (4 + q % 2) * CH:(5 + q % 2) * CH]).then_inc(ocp, 1)
                        for q in range(NCH):
                            for kt in range(TB):
                                n = q * TB + kt
                                act.wait_ge(tr, n + 1)
                                if n >= NPT:
                                    act.wait_ge(ops, n - NPT + 1)
                                act.copy(pT[:, n % NPT, :], g.ps[:, (n % 4) * CH:(n % 4 + 1) * CH]).then_inc(pcp, 1)
                                if kt == 4 and q:
                                    sums_copy(q - 1)
                                if kt % 4 == 3:
                                    b = 4 * q + kt // 4
                                    act.wait_ge(kept, b + 1)
                                    if b:
                                        act.wait_ge(summed, b)
                                    act.activation(junk[:, :], E[:, b, :], ACT.Identity, accum_out=ssum[:, b:b + 1]).then_inc(summed, 1)
                        sums_copy(NCH - 1)

                    @block.vector
                    def _(dve):
                        step = Steps(dve, steps)
                        flag = dve.value_load(general[0:1, 0:1], min_val=0, max_val=1)
                        with dve.If(flag > 0):
                            keep_by_bisection(dve, gsteps, E, KEEP, (*small, rest[:, 1, :], rest[:, 0, :]), kept)
                        with dve.Else():
                            find_rest(dve, fsteps, E, cut, need, (rest, *top8), found, kept)
                        dve.wait_ge(summed, TB)
                        step(dve.scalar_tensor_tensor(ssum[:, :], Z[:, :], 1.0e-9, ssum[:, :], ALU.mult, ALU.add))
                        step(dve.reciprocal(ssum[:, :], ssum[:, :]))
                        step(dve.tensor_scalar(ssum[:, :], ssum[:, :], sc[:, 1:2], None, ALU.mult))
                        step(dve.tensor_scalar(dense[:, :, :], dense[:, :, :], sc[:, 0:1], None, ALU.mult))
                        for q in range(NCH):
                            dve.wait_ge(otr, q + 1)
                            for j in range(4):
                                b = 4 * q + j
                                ins = dve.scalar_tensor_tensor(dense[:, b, :], g.ps[:, (6 + q % 2) * CH + j * P:(6 + q % 2) * CH + (j + 1) * P],
                                                               ssum[:, b:b + 1], dense[:, b, :], ALU.mult, ALU.add)
                            ins.then_inc(fin, 1)
        with ExitStack() as ctx4:
            r4 = Room(nc, ctx4, "l2p")
            x1 = r4.sb("x1", [P, TB, C])
            hb = r4.sb("hb", [P, K, T])
            tr, add, fps, rel, yps, yd = r4.sem("src_transposed"), r4.sem("src_added"), r4.sem("ff_in_psum"), r4.sem("relu_done"), r4.sem("y_in_psum"), r4.sem("y_done")
            with nc.Block() as block:

                @block.tensor
                def _(pe):
                    for b in range(TB):
                        mm = pe.transpose(g.ps[:, b * P:(b + 1) * P], g.hT[:, b * P:(b + 1) * P], g.ident[:, :])
                    mm.then_inc(tr, 1)

                @block.vector
                def _(dve):
                    dve.wait_ge(tr, 1)
                    dve.tensor_tensor(dense[:, :, :], dense[:, :, :], g.ps[:, 0:T].rearrange("p (b c) -> p b c", c=C), ALU.add).then_inc(add, 1)
            layernorm_transpose(nc, g, "lnp1", None, dense, (rows[:, 3, :], rows[:, 4, :]), x1)
            with nc.Block() as block:

                @block.tensor
                def _(pe):
                    for n in range(K * NCH):
                        m, q = n % K, n // K
                        if n >= 4:
                            pe.wait_ge(rel, n - 3)
                        pe.matmul(g.ps[:, (n % 4) * CH:(n % 4 + 1) * CH], f1[:, m * P:(m + 1) * P], g.hT[:, q * CH:(q + 1) * CH],
                                  start=True, stop=True).then_inc(fps, 1)
                    for b in range(TB):
                        pe.wait_ge(rel, K * (b // 4 + 1))
                        if b >= 4:
                            pe.wait_ge(yd, b - 3)
                        for k in range(K):
                            mm = pe.matmul(g.ps[:, (4 + b % 4) * CH:(4 + b % 4) * CH + C], hb[:, k, b * P:(b + 1) * P], f2[:, k, :],
                                           start=(k == 0), stop=(k == K - 1))
                        mm.then_inc(yps, 1)

                @block.scalar
                def _(act):
                    for n in range(K * NCH):
                        m, q = n % K, n // K
                        act.wait_ge(fps, n + 1)
                        act.activation(hb[:, m, q * CH:(q + 1) * CH], g.ps[:, (n % 4) * CH:(n % 4 + 1) * CH], ACT.Relu, bias=b1[:, m:m + 1]).then_inc(rel, 1)

                @block.gpsimd
                def _(pool):
                    pool.tensor_tensor(x1[:, :, :], x1[:, :, :], rows[:, 2, :].unsqueeze(1).broadcast_to([P, TB, C]), ALU.add).then_inc(add, 1)

                @block.vector
                def _(dve):
                    dve.wait_ge(add, 2)
                    for b in range(TB):
                        dve.wait_ge(yps, b + 1)
                        dve.tensor_tensor(x1[:, b, :], x1[:, b, :], g.ps[:, (4 + b % 4) * CH:(4 + b % 4) * CH + C], ALU.add).then_inc(yd, 1)
            layernorm_transpose(nc, g, "lnp2", None, x1, (rows[:, 5, :], rows[:, 6, :]), dense, transposed=False)
            with nc.Block() as block:

                @block.vector
                def _(dve):
                    dve.tensor_tensor(g.X[:, :, :], g.X[:, :, :], dense[:, :, :], ALU.add)


def ternary_ffn(nc, g, I):
    H = 512
    K = H // P
    with ExitStack() as ctx:
        r = Room(nc, ctx, "l2f")
        w12 = r.sb("w12", [C, 2, H])
        h12 = r.sb("h12", [P, 2, K, H])
        w3 = r.sb("w3", [P, K, C])
        sc = r.sb("scales", [P, 4, K])
        s3 = r.sb("s3", [P, C])
        a = r.sb("a", [P, K, T])
        b_ = r.sb("b", [P, K, T])

        def load(sp, s):
            n = 0
            for i, nm in enumerate(("w1", "w2")):
                sp.dma_start(w12[:, i, :], I[f"L2_ffn_{nm}_wT"]).then_inc(s, 16)
            for i, nm in enumerate(("h1", "h2")):
                sp.dma_start(h12[:, i, :, :], I[f"L2_ffn_{nm}_wT"].rearrange("(k p) o -> p k o", p=P)).then_inc(s, 16)
            for i, nm in enumerate(("w1", "w2", "h1", "h2")):
                sp.dma_start(sc[:, i, :], I[f"L2_ffn_{nm}_s"].rearrange("(k p) -> p k", p=P), allow_slow_non_contiguous=True).then_inc(s, 16)
            sp.dma_start(w3[:, :, :], I["L2_ffn_w3_wT"].rearrange("(k p) o -> p k o", p=P)).then_inc(s, 16)
            sp.dma_start(s3[:, :], I["L2_ffn_w3_s"].rearrange("(a c) -> a c", a=1).broadcast_to([P, C])).then_inc(s, 16)
            return 10
        layernorm_transpose(nc, g, "ln5", load)
        sl = r.sb("silu", [P, 2, CH])
        yb = r.sb("y", [P, 2, C])
        gps, ups, sid, had = r.sem("gate_in_psum"), r.sem("up_in_psum"), r.sem("silu_done"), r.sem("product_done")
        zps, gel = r.sem("hidden_in_psum"), r.sem("gelu_done")
        yps, ysc, xad = r.sem("y_in_psum"), r.sem("y_scaled"), r.sem("x_added")
        N1 = K * NCH
        with nc.Block() as block:

            @block.tensor
            def _(pe):
                for n in range(N1):
                    m, q = n % K, n // K
                    if n >= 2:
                        pe.wait_ge(sid, n - 1)
                    pe.matmul(g.ps[:, (n % 2) * CH:(n % 2 + 1) * CH], w12[:, 0, m * P:(m + 1) * P], g.hT[:, q * CH:(q + 1) * CH],
                              start=True, stop=True).then_inc(gps, 1)
                    if n >= 2:
                        pe.wait_ge(had, n - 1)
                    pe.matmul(g.ps[:, (2 + n % 2) * CH:(3 + n % 2) * CH], w12[:, 1, m * P:(m + 1) * P], g.hT[:, q * CH:(q + 1) * CH],
                              start=True, stop=True).then_inc(ups, 1)
                for layer in range(2):
                    src = a if layer == 0 else b_
                    for n in range(N1):
                        m, q = n % K, n // K
                        i = layer * N1 + n
                        if layer == 0:
                            pe.wait_ge(had, K * (q + 1))
                        else:
                            pe.wait_ge(gel, K * (q + 1))
                        if i >= 4:
                            pe.wait_ge(gel, i - 3)
                        for k in range(K):
                            mm = pe.matmul(g.ps[:, (4 + i % 4) * CH:(5 + i % 4) * CH], h12[:, layer, k, m * P:(m + 1) * P],
                                           src[:, k, q * CH:(q + 1) * CH], start=(k == 0), stop=(k == K - 1))
                        mm.then_inc(zps, 1)
                for t in range(TB):
                    pe.wait_ge(gel, N1 + K * (t // 4 + 1))
                    if t >= 2:
                        pe.wait_ge(ysc, t - 1)
                    for k in range(K):
                        mm = pe.matmul(g.ps[:, (t % 2) * CH:(t % 2) * CH + C], a[:, k, t * P:(t + 1) * P], w3[:, k, :],
                                       start=(k == 0), stop=(k == K - 1))
                    mm.then_inc(yps, 1)

            @block.scalar
            def _(act):
                for n in range(N1):
                    act.wait_ge(gps, n + 1)
                    if n >= 2:
                        act.wait_ge(had, n - 1)
                    act.activation(sl[:, n % 2, :], g.ps[:, (n % 2) * CH:(n % 2 + 1) * CH], ACT.Silu, scale=sc[:, 0, n % K:n % K + 1]).then_inc(sid, 1)
                for i in range(2 * N1):
                    layer, n = divmod(i, N1)
                    m, q = n % K, n // K
                    dst = b_ if layer == 0 else a
                    act.wait_ge(zps, N1 if layer == 1 and n == 0 else i + 1)
                    act.wait_ge(zps, i + 1)
                    act.activation(dst[:, m, q * CH:(q + 1) * CH], g.ps[:, (4 + i % 4) * CH:(5 + i % 4) * CH], ACT.Gelu,
                                   scale=sc[:, 2 + layer, m:m + 1]).then_inc(gel, 1)

            @block.vector
            def _(dve):
                for n in range(N1):
                    dve.wait_ge(ups, n + 1)
                    dve.wait_ge(sid, n + 1)
                    dve.scalar_tensor_tensor(a[:, n % K, (n // K) * CH:(n // K + 1) * CH], g.ps[:, (2 + n % 2) * CH:(3 + n % 2) * CH],
                                             sc[:, 1, n % K:n % K + 1], sl[:, n % 2, :], ALU.mult, ALU.mult).then_inc(had, 1)
                for t in range(TB):
                    dve.wait_ge(yps, t + 1)
                    dve.tensor_tensor(yb[:, t % 2, :], g.ps[:, (t % 2) * CH:(t % 2) * CH + C], s3[:, :], ALU.mult).then_inc(ysc, 1)
                    dve.wait_ge(ysc, t + 1)
                    dve.tensor_tensor(g.X[:, t, :], g.X[:, t, :], yb[:, t % 2, :], ALU.add).then_inc(xad, 1)
                    if t >= 1:
                        dve.wait_ge(xad, t)


def int8_ffn(nc, g, I):
    H = 384
    K = H // P
    import numpy as np
    SCALE = float(np.float32(1.0 / 127.0))
    with ExitStack() as ctx:
        r = Room(nc, ctx, "l3f")
        wi = r.sb("wi", [C, 2, H], I32)
        wdi = r.sb("wdi", [P, K, C], I32)
        w = r.sb("w", [C, 2, H])
        wd = r.sb("wd", [P, K, C])

        def load(sp, s):
            sp.dma_start(wi[:, 0, :], I["L3_ffn_w_gateT"]).then_inc(s, 16)
            sp.dma_start(wi[:, 1, :], I["L3_ffn_w_upT"]).then_inc(s, 16)
            sp.dma_start(wdi[:, :, :], I["L3_ffn_w_downT"].rearrange("(k p) o -> p k o", p=P)).then_inc(s, 16)
            return 3
        layernorm_transpose(nc, g, "ln7", load)
        a = r.sb("a", [P, K, T])
        sl = r.sb("silu", [P, 2, CH])
        deq = r.sem("dequantised")
        gps, ups, sid, had = r.sem("gate_in_psum"), r.sem("up_in_psum"), r.sem("silu_done"), r.sem("product_done")
        yps, xad = r.sem("y_in_psum"), r.sem("x_added")
        N1 = K * NCH
        with nc.Block() as block:

            @block.tensor
            def _(pe):
                def down(t):
                    pe.wait_ge(had, K * (t // 4 + 1))
                    if t >= 2:
                        pe.wait_ge(xad, t - 1)
                    for k in range(K):
                        mm = pe.matmul(g.ps[:, (4 + t % 2) * CH:(4 + t % 2) * CH + C], a[:, k, t * P:(t + 1) * P], wd[:, k, :],
                                       start=(k == 0), stop=(k == K - 1))
                    mm.then_inc(yps, 1)
                pe.wait_ge(deq, 2)
                for n in range(N1):
                    m, q = n % K, n // K
                    if n >= 2:
                        pe.wait_ge(sid, n - 1)
                    pe.matmul(g.ps[:, (n % 2) * CH:(n % 2 + 1) * CH], w[:, 0, m * P:(m + 1) * P], g.hT[:, q * CH:(q + 1) * CH],
                              start=True, stop=True).then_inc(gps, 1)
                    if n >= 2:
                        pe.wait_ge(had, n - 1)
                    pe.matmul(g.ps[:, (2 + n % 2) * CH:(3 + n % 2) * CH], w[:, 1, m * P:(m + 1) * P], g.hT[:, q * CH:(q + 1) * CH],
                              start=True, stop=True).then_inc(ups, 1)
                for t in range(TB):
                    down(t)

            @block.scalar
            def _(act):
                for n in range(N1):
                    act.wait_ge(gps, n + 1)
                    if n >= 2:
                        act.wait_ge(had, n - 1)
                    act.activation(sl[:, n % 2, :], g.ps[:, (n % 2) * CH:(n % 2 + 1) * CH], ACT.Silu).then_inc(sid, 1)

            @block.vector
            def _(dve):
                dve.tensor_scalar(w[:, :, :], wi[:, :, :], SCALE, None, ALU.mult).then_inc(deq, 1)
                dve.tensor_scalar(wd[:, :, :], wdi[:, :, :], SCALE, None, ALU.mult).then_inc(deq, 1)
                for n in range(N1):
                    dve.wait_ge(ups, n + 1)
                    dve.wait_ge(sid, n + 1)
                    dve.tensor_tensor(a[:, n % K, (n // K) * CH:(n // K + 1) * CH], g.ps[:, (2 + n % 2) * CH:(3 + n % 2) * CH],
                                      sl[:, n % 2, :], ALU.mult).then_inc(had, 1)
                for t in range(TB):
                    dve.wait_ge(yps, t + 1)
                    dve.tensor_tensor(g.X[:, t, :], g.X[:, t, :], g.ps[:, (4 + t % 2) * CH:(4 + t % 2) * CH + C], ALU.add).then_inc(xad, 1)


def plain_attention(nc, g, I):
    S = T
    with ExitStack() as ctx:
        r = Room(nc, ctx, "l3a")
        w = r.sb("wqkv", [C, 3, C])
        wo = r.sb("wo", [C, C])

        def load(sp, s):
            sp.dma_start(w[:, :, :].rearrange("c i o -> c (i o)"), I["L3_attn_w_qkvT"]).then_inc(s, 16)
            sp.dma_start(wo[:, :], I["L3_attn_w_oT"]).then_inc(s, 16)
            return 2
        layernorm_transpose(nc, g, "ln6", load)
        O = r.sb("O", [P, TB, C])
        hid = C ** -0.5
        head_attention(nc, g, "l3h", w, None, hid * 8 ** -0.5, hid, hid * (S / (S - 1.0) ** 0.5) * S ** -0.5 * hid, O)
        OT = r.sb("OT", [C, T])
        tr, cp, yps, xad = r.sem("o_transposed"), r.sem("o_copied"), r.sem("y_in_psum"), r.sem("x_added")
        with nc.Block() as block:

            @block.tensor
            def _(pe):
                transpose_blocks(pe, g, O, 0, tr)
                pe.wait_ge(cp, 1)
                for b in range(TB):
                    pe.matmul(g.ps[:, T + b * P:T + (b + 1) * P], OT[:, b * P:(b + 1) * P], wo[:, :], start=True, stop=True).then_inc(yps, 1)

            @block.vector
            def _(dve):
                dve.wait_ge(tr, 1)
                dve.tensor_copy(OT[:, :], g.ps[:, 0:T]).then_inc(cp, 1)
                for q in range(NCH):
                    dve.wait_ge(yps, 4 * q + 4)
                    dve.tensor_tensor(g.X[:, 4 * q:4 * q + 4, :], g.X[:, 4 * q:4 * q + 4, :],
                                      g.ps[:, T + q * CH:T + (q + 1) * CH].rearrange("p (b c) -> p b c", c=C), ALU.add).then_inc(xad, 1)


def store_output(nc, g, out):
    with ExitStack() as ctx:
        r = Room(nc, ctx, "out")
        stored = r.sem("stored")
        with nc.Block() as block:

            @block.sync
            def _(sp):
                sp.dma_start(out.rearrange("a (b p) c -> p (a b) c", p=P), g.X[:, :, :]).then_inc(stored, 16)
                sp.wait_ge(stored, 16)


LAYERS = (bond_attention, masked_ffn, mamba, gated_experts, dual_attention, ternary_ffn, plain_attention, int8_ffn)


def clear_semaphores(nc):
    used = list(nc.released_uncleared_semaphores)
    with nc.Block() as block:

        @block.gpsimd
        def _(pool):
            pool.sem_clear(range(min(used), max(used) + 1))


def build_program(nc, I, out, layers=LAYERS):
    g = Shared()
    with ExitStack() as ctx:
        setup_shared(nc, ctx, g, I["L0_attn_x"])
        for i, layer in enumerate(layers):
            if i:
                clear_semaphores(nc)
            layer(nc, g, I)
        store_output(nc, g, out)


TRANSPOSED = {
    "L0_attn_rel_pos_emb": (1, 0), "L0_ffn_w2": (1, 0, 2),
    "L1_attn_in_proj_w": (1, 0), "L1_attn_out_proj_w": (1, 0),
    "L1_attn_x_proj_w_f": (1, 0), "L1_attn_x_proj_w_r": (1, 0), "L1_attn_dt_proj_w_f": (1, 0), "L1_attn_dt_proj_w_r": (1, 0),
    "L2_attn_in_proj_w": (1, 0), "L2_attn_out_proj_w": (1, 0), "L2_attn_Qp_w": (1, 0), "L2_attn_Kp_w": (1, 0),
    "L2_attn_Vp_w": (1, 0), "L2_attn_ff1_w": (1, 0), "L2_attn_ff2_w": (1, 0),
    "L2_ffn_w1_w": (1, 0), "L2_ffn_w2_w": (1, 0), "L2_ffn_h1_w": (1, 0), "L2_ffn_h2_w": (1, 0), "L2_ffn_w3_w": (1, 0),
    "L3_attn_w_qkv": (1, 0), "L3_attn_w_o": (1, 0), "L3_ffn_w_gate": (1, 0), "L3_ffn_w_up": (1, 0), "L3_ffn_w_down": (1, 0),
}


def lay_out(inputs):
    import numpy as np
    arrays = {}
    for name, a in inputs.items():
        a = np.asarray(a)
        if name in TRANSPOSED:
            name, a = name + "T", a.transpose(TRANSPOSED[name])
        arrays[name] = np.ascontiguousarray(a).reshape(a.shape or (1,))
    return arrays


def kernel(**inputs):
    import numpy as np
    import concourse.bacc as bacc
    from concourse.bass_utils import run_bass_kernel_spmd

    nc = bacc.Bacc("TRN2", target_bir_lowering=False, num_devices=1)
    arrays = {"in_" + k: a for k, a in lay_out(inputs).items()}
    I = {k[3:]: nc.dram_tensor(k, a.shape, mybir.dt.from_np(a.dtype), kind="ExternalInput").ap() for k, a in arrays.items()}
    out = nc.dram_tensor("out_0", (1, T, C), F32, kind="ExternalOutput").ap()
    build_program(nc, I, out)
    r = run_bass_kernel_spmd(nc, [arrays], core_ids=[0])
    return r.results[0]["out_0"]
```
